# Optimizing a Trainium2 kernel written in Bass

```python
import numpy as np
import jax
import jax.numpy as jnp

def _softmax(x, axis=-1):
    return jax.nn.softmax(x, axis=axis)

def _gelu(x):
    return jax.nn.gelu(x, approximate=True)

def _silu(x):
    return jax.nn.silu(x)

def _sigmoid(x):
    return jax.nn.sigmoid(x)

def _layernorm(x, axis=-1, eps=1e-05):
    m = jnp.mean(x, axis=axis, keepdims=True)
    v = jnp.var(x, axis=axis, keepdims=True)
    return (x - m) / jnp.sqrt(v + eps)

def _scatter_add(tgt, idx, src, axis=0):
    return tgt.at[idx].add(src)

def _segment_sum(src, seg, n):
    return jax.ops.segment_sum(src, seg, n)
kernel_name = 'mk_xattn_ffn_d1_seqx_r2_614262'

def setup_inputs(seed: int=0):
    np.random.seed(seed)
    _w = jnp.asarray

    def _rec_inputs():
        import jax
        import jax.numpy as jnp
        _rk = jax.random.key(seed)
        x = -0.000125 + 0.9999 * jax.random.normal(jax.random.fold_in(_rk, 1), (8, 224, 512), jnp.float32)
        _lenS = 224 - jax.random.randint(jax.random.fold_in(_rk, 7), (8,), 0, max(1, 224 // 4) + 1, jnp.int32)
        _lenS2 = 750 - jax.random.randint(jax.random.fold_in(_rk, 8), (8,), 0, max(1, 750 // 4) + 1, jnp.int32)
        _ctx_768P = jax.random.normal(jax.random.fold_in(_rk, 11), (8, 16, 384), jnp.float32)
        _ctx_768c = jax.random.dirichlet(jax.random.fold_in(_rk, 511), 0.3 * jnp.ones((16,), jnp.float32), (8, 750))
        _ctx_768t = jnp.einsum('bsk,bkd->bsd', _ctx_768c, _ctx_768P)
        _ctx_768t = _ctx_768t * jax.lax.rsqrt(jnp.mean(jnp.square(_ctx_768t)) + 1e-12) * 0.953939
        ctx_768 = 0.00243539 + 0.99952 * (_ctx_768t + 0.3 * jax.random.normal(jax.random.fold_in(_rk, 611), (8, 750, 384), jnp.float32))
        return (x, ctx_768)
    x, ctx_768 = _rec_inputs()

    def _L0_xattn_setup():
        import jax, jax.numpy as jnp
        import numpy as np
        HEADS = 16
        DIM_HEAD = 64
        RANK = 32
        LORA_W = 1.0
        IPA_SCALE = 1.0
        IPA_TOKENS = 4
        SCALE = DIM_HEAD ** (-0.5)

        def _split_heads(t):
            b, n, _ = t.shape
            return t.reshape(b, n, HEADS, DIM_HEAD).transpose(0, 2, 1, 3)

        def _merge_heads(t):
            b, h, n, d = t.shape
            return t.transpose(0, 2, 1, 3).reshape(b, n, h * d)

        def _attention(q_in, k_in, v_in):
            q = _split_heads(q_in)
            k = _split_heads(k_in)
            v = _split_heads(v_in)
            s = jnp.einsum('bhid,bhjd->bhij', q, k) * SCALE
            p = jax.nn.softmax(s, axis=-1)
            o = jnp.einsum('bhij,bhjd->bhid', p, v)
            return _merge_heads(o)

        def _lora(t, down, up, alpha):
            return t @ down @ up * (LORA_W * alpha[0] / RANK)
        key = jax.random.key(seed)
        ks = jax.random.split(key, 20)
        B, N, QD, CD, ID = (8, 2048, 512, 384, HEADS * DIM_HEAD)
        CTX = 77 + IPA_TOKENS
        s = 0.02
        return {'x': jax.random.normal(ks[0], (B, N, QD), jnp.float32), 'context': jax.random.normal(ks[1], (B, CTX, CD), jnp.float32), 'Wq': jax.random.normal(ks[2], (QD, ID), jnp.float32) * s, 'Wk': jax.random.normal(ks[3], (CD, ID), jnp.float32) * s, 'Wv': jax.random.normal(ks[4], (CD, ID), jnp.float32) * s, 'Wo': jax.random.normal(ks[5], (ID, QD), jnp.float32) * s, 'bo': jnp.zeros((QD,), jnp.float32), 'q_down': jax.random.normal(ks[6], (QD, RANK), jnp.float32) * s, 'q_up': jax.random.normal(ks[7], (RANK, ID), jnp.float32) * s, 'q_alpha': jnp.ones((1,), jnp.float32) * RANK, 'k_down': jax.random.normal(ks[8], (CD, RANK), jnp.float32) * s, 'k_up': jax.random.normal(ks[9], (RANK, ID), jnp.float32) * s, 'k_alpha': jnp.ones((1,), jnp.float32) * RANK, 'v_down': jax.random.normal(ks[10], (CD, RANK), jnp.float32) * s, 'v_up': jax.random.normal(ks[11], (RANK, ID), jnp.float32) * s, 'v_alpha': jnp.ones((1,), jnp.float32) * RANK, 'o_down': jax.random.normal(ks[12], (ID, RANK), jnp.float32) * s, 'o_up': jax.random.normal(ks[13], (RANK, QD), jnp.float32) * s, 'o_alpha': jnp.ones((1,), jnp.float32) * RANK, 'Wk_ipa': jax.random.normal(ks[14], (CD, ID), jnp.float32) * s, 'Wv_ipa': jax.random.normal(ks[15], (CD, ID), jnp.float32) * s}
    _L0_xattn_all = _L0_xattn_setup()
    _L0_xattn_in = {k: v for k, v in _L0_xattn_all.items() if k in ('Wq', 'Wk', 'Wv', 'Wo', 'bo', 'q_down', 'q_up', 'q_alpha', 'k_down', 'k_up', 'k_alpha', 'v_down', 'v_up', 'v_alpha', 'o_down', 'o_up', 'o_alpha', 'Wk_ipa', 'Wv_ipa')}
    del _L0_xattn_all

    def _L0_ffn_setup():
        import jax, jax.numpy as jnp
        import numpy as np
        N_EMBD = 512
        N_EXP = 8
        TOP_K = 2
        CAPACITY = 2048
        D_FF = 3 * N_EMBD
        key = jax.random.key(seed)
        k1, k2, k3, k4 = jax.random.split(key, 4)
        x = jax.random.normal(k1, (8, 1024, N_EMBD), dtype=jnp.float32)
        w_gate = jax.random.normal(k2, (N_EMBD, N_EXP), dtype=jnp.float32) * 0.02
        c_fc = jax.random.normal(k3, (N_EXP, N_EMBD, D_FF), dtype=jnp.float32) * 0.02
        c_proj = jax.random.normal(k4, (N_EXP, D_FF // 2, N_EMBD), dtype=jnp.float32) * 0.02
        return {'x': x, 'w_gate': w_gate, 'c_fc': c_fc, 'c_proj': c_proj}
    _L0_ffn_all = _L0_ffn_setup()
    _L0_ffn_in = {k: v for k, v in _L0_ffn_all.items() if k in ('w_gate', 'c_fc', 'c_proj')}
    del _L0_ffn_all
    return {'x': x, 'ctx_768': ctx_768, 'L0_xattn_Wq': _L0_xattn_in['Wq'], 'L0_xattn_Wk': _L0_xattn_in['Wk'], 'L0_xattn_Wv': _L0_xattn_in['Wv'], 'L0_xattn_Wo': _L0_xattn_in['Wo'], 'L0_xattn_bo': _L0_xattn_in['bo'], 'L0_xattn_q_down': _L0_xattn_in['q_down'], 'L0_xattn_q_up': _L0_xattn_in['q_up'], 'L0_xattn_q_alpha': _L0_xattn_in['q_alpha'], 'L0_xattn_k_down': _L0_xattn_in['k_down'], 'L0_xattn_k_up': _L0_xattn_in['k_up'], 'L0_xattn_k_alpha': _L0_xattn_in['k_alpha'], 'L0_xattn_v_down': _L0_xattn_in['v_down'], 'L0_xattn_v_up': _L0_xattn_in['v_up'], 'L0_xattn_v_alpha': _L0_xattn_in['v_alpha'], 'L0_xattn_o_down': _L0_xattn_in['o_down'], 'L0_xattn_o_up': _L0_xattn_in['o_up'], 'L0_xattn_o_alpha': _L0_xattn_in['o_alpha'], 'L0_xattn_Wk_ipa': _L0_xattn_in['Wk_ipa'], 'L0_xattn_Wv_ipa': _L0_xattn_in['Wv_ipa'], 'L0_ffn_w_gate': _L0_ffn_in['w_gate'], 'L0_ffn_c_fc': _L0_ffn_in['c_fc'], 'L0_ffn_c_proj': _L0_ffn_in['c_proj']}

def reference(x, ctx_768, L0_xattn_Wq, L0_xattn_Wk, L0_xattn_Wv, L0_xattn_Wo, L0_xattn_bo, L0_xattn_q_down, L0_xattn_q_up, L0_xattn_q_alpha, L0_xattn_k_down, L0_xattn_k_up, L0_xattn_k_alpha, L0_xattn_v_down, L0_xattn_v_up, L0_xattn_v_alpha, L0_xattn_o_down, L0_xattn_o_up, L0_xattn_o_alpha, L0_xattn_Wk_ipa, L0_xattn_Wv_ipa, L0_ffn_w_gate, L0_ffn_c_fc, L0_ffn_c_proj):
    import jax
    import jax.numpy as jnp

    def _L0_xattn_ref(x, context, Wq, Wk, Wv, Wo, bo, q_down, q_up, q_alpha, k_down, k_up, k_alpha, v_down, v_up, v_alpha, o_down, o_up, o_alpha, Wk_ipa, Wv_ipa):
        import jax, jax.numpy as jnp
        import numpy as np
        HEADS = 16
        DIM_HEAD = 64
        RANK = 32
        LORA_W = 1.0
        IPA_SCALE = 1.0
        IPA_TOKENS = 4
        SCALE = DIM_HEAD ** (-0.5)

        def _split_heads(t):
            b, n, _ = t.shape
            return t.reshape(b, n, HEADS, DIM_HEAD).transpose(0, 2, 1, 3)

        def _merge_heads(t):
            b, h, n, d = t.shape
            return t.transpose(0, 2, 1, 3).reshape(b, n, h * d)

        def _attention(q_in, k_in, v_in):
            q = _split_heads(q_in)
            k = _split_heads(k_in)
            v = _split_heads(v_in)
            s = jnp.einsum('bhid,bhjd->bhij', q, k) * SCALE
            p = jax.nn.softmax(s, axis=-1)
            o = jnp.einsum('bhij,bhjd->bhid', p, v)
            return _merge_heads(o)

        def _lora(t, down, up, alpha):
            return t @ down @ up * (LORA_W * alpha[0] / RANK)
        q_in = x @ Wq + _lora(x, q_down, q_up, q_alpha)
        end = context.shape[1] - IPA_TOKENS
        org_ctx = context[:, :end, :]
        ipa_ctx = context[:, end:, :]
        k_in = org_ctx @ Wk + _lora(org_ctx, k_down, k_up, k_alpha)
        v_in = org_ctx @ Wv + _lora(org_ctx, v_down, v_up, v_alpha)
        out = _attention(q_in, k_in, v_in)
        ipa_k = ipa_ctx @ Wk_ipa
        ipa_v = ipa_ctx @ Wv_ipa
        out_ipa = _attention(q_in, ipa_k, ipa_v)
        out = out + IPA_SCALE * out_ipa
        return out @ Wo + bo + _lora(out, o_down, o_up, o_alpha)

    def _L0_ffn_ref(x, w_gate, c_fc, c_proj):
        import jax, jax.numpy as jnp
        import numpy as np
        N_EMBD = 512
        N_EXP = 8
        TOP_K = 2
        CAPACITY = 2048
        D_FF = 3 * N_EMBD
        B, T, d = x.shape
        N = B * T
        xf = x.reshape(N, d)
        scores = jax.nn.softmax(xf @ w_gate, axis=-1)
        weights, idx = jax.lax.top_k(scores, TOP_K)
        flat_e = idx.reshape(-1)
        tok = jnp.repeat(jnp.arange(N), TOP_K)
        oh = jax.nn.one_hot(flat_e, N_EXP, dtype=jnp.int32)
        pos = (jnp.cumsum(oh, axis=0) * oh).sum(-1) - 1
        valid = pos < CAPACITY
        pos_c = jnp.where(valid, pos, 0)
        vmask = valid.astype(x.dtype)[:, None]
        exp_x = jnp.zeros((N_EXP, CAPACITY, d), x.dtype)
        exp_x = exp_x.at[flat_e, pos_c].add(xf[tok] * vmask)
        h = jnp.einsum('ecd,edf->ecf', exp_x, c_fc)
        a, g = jnp.split(h, 2, axis=-1)
        h = jax.nn.silu(a) * g
        exp_out = jnp.einsum('ecf,efd->ecd', h, c_proj)
        gathered = exp_out[flat_e, pos_c]
        w = weights.reshape(-1)[:, None] * vmask
        out = (gathered * w).reshape(N, TOP_K, d).sum(axis=1)
        return out.reshape(B, T, d)
    x = x + _L0_xattn_ref(_layernorm(x, axis=-1), ctx_768, L0_xattn_Wq, L0_xattn_Wk, L0_xattn_Wv, L0_xattn_Wo, L0_xattn_bo, L0_xattn_q_down, L0_xattn_q_up, L0_xattn_q_alpha, L0_xattn_k_down, L0_xattn_k_up, L0_xattn_k_alpha, L0_xattn_v_down, L0_xattn_v_up, L0_xattn_v_alpha, L0_xattn_o_down, L0_xattn_o_up, L0_xattn_o_alpha, L0_xattn_Wk_ipa, L0_xattn_Wv_ipa)
    x = x + _L0_ffn_ref(_layernorm(x, axis=-1), L0_ffn_w_gate, L0_ffn_c_fc, L0_ffn_c_proj)
    return x

_drawn_inputs = setup_inputs


def setup_inputs(seed=0):
    import zlib

    import numpy as np

    out = dict(_drawn_inputs(seed))
    spreads = {'L0_xattn_bo': (0.0, 0.1)}
    factors = {'L0_xattn_Wq': 3.424,
     'L0_xattn_Wk': 7.203,
     'L0_xattn_q_down': 8.0,
     'L0_xattn_q_up': 8.0,
     'L0_xattn_k_down': 8.0,
     'L0_xattn_k_up': 8.0,
     'L0_xattn_v_down': 4.105,
     'L0_xattn_v_up': 4.212,
     'L0_xattn_Wk_ipa': 3.87,
     'L0_ffn_w_gate': 3.897,
     'L0_ffn_c_fc': 3.364,
     'L0_ffn_c_proj': 3.361}
    for name, (base, spread) in spreads.items():
        noise = np.random.default_rng([zlib.crc32(name.encode()), seed]).standard_normal(out[name].shape)
        drawn = base * np.exp(spread * noise) if base else spread * noise
        out[name] = jnp.asarray(drawn.astype(out[name].dtype))
    for name, factor in factors.items():
        out[name] = (out[name] * factor).astype(out[name].dtype)
    return out
```

```python
from contextlib import ExitStack

import numpy as np

import concourse.bass as bass
from concourse import mybir

F32 = mybir.dt.float32
F32R = mybir.dt.float32r
I32 = mybir.dt.int32
U32 = mybir.dt.uint32
ALU = mybir.AluOpType
ACT = mybir.ActivationFunctionType
AX = mybir.AxisListType

B, N, D = 8, 224, 512
CTX, CD = 750, 384
IPA = 4
HEADS, DH = 16, 64
ID = HEADS * DH
RANK = 32
SCALE = DH ** -0.5
EPS = 1e-5
P = 128
QT, TQ = 2, 112
NT = B * QT
PAIRS = HEADS // 2
XC, CC = D // P, CD // P
KH, KHP = CTX // 2, CTX // 2 + 1
ORG = KH - 2
KC, KCN = 125, 6
VG, VH = 4, 4
E, F = 8, 768
FC = F // P
GROUPS = 8 + 3 * PAIRS + KCN * VG
SUB = 128
STEP = 2 * SUB
TOKENS = B * N
MAXSTEPS = (2 * TOKENS + E * (STEP - 1)) // STEP
KMAX = -(-TOKENS // STEP)
ROOM = MAXSTEPS + KMAX + 1


def prepare(nc, dram, const):
    wq_h, wq_l, wk_h, wk_l, wv_h, wv_l, ident, kipa, rstd, mean = (
        const[k] for k in ("wq_h", "wq_l", "wk_h", "wk_l", "wv_h", "wv_l", "ident", "kipa", "rstd", "mean"))
    with ExitStack() as ctx:
        def sb(name, shape, dt=F32):
            return ctx.enter_context(nc.sbuf_tensor(name, shape, dt))

        def sem(name):
            return ctx.enter_context(nc.semaphore(name))

        raw = {"q": sb("wq_raw", [P, XC, ID]), "k": sb("wk_raw", [P, CC, ID]), "v": sb("wv_raw", [P, CC, ID])}
        split = {"q": (wq_h, wq_l), "k": (wk_h, wk_l), "v": (wv_h, wv_l)}
        down = sb("down", [P, XC + 2 * CC, RANK])
        up = sb("up", [RANK, 3, ID])
        alpha = sb("alpha", [P, 3])
        alpha_r = sb("alpha_r", [P, 3])
        downT = sb("downT", [RANK, XC + 2 * CC, P])
        wki = sb("wk_ipa", [P, CC, ID])
        wvi = sb("wv_ipa", [P, CC, ID])
        ictx = sb("ipa_ctx", [B * IPA, CD])
        ictxT = sb("ipa_ctxT", [P, CC, B * IPA])
        vipa_h = sb("vipa_h", [B * IPA, HEADS, DH], F32R)
        vipa = sb("vipa", [B * IPA, HEADS, 2 * DH])
        xb = sb("x_stat", [TQ, 2, QT, D])
        bn = sb("bn", [TQ, NT, 6])
        mv = sb("mv", [TQ, NT, 2])
        eps = sb("eps", [TQ, 1])
        std = sb("std", [TQ, NT])
        ones = sb("ones_sq", [P, P])
        ps_down = ctx.enter_context(nc.psum_tensor("ps_down", [RANK, 12, P], F32))
        ps_w = ctx.enter_context(nc.psum_tensor("ps_w", [P, 2, 512], F32))
        ps_i = ctx.enter_context(nc.psum_tensor("ps_i", [P, 512], F32))
        ps_v = ctx.enter_context(nc.psum_tensor("ps_v", [B * IPA, 2, 512], F32))

        small_loaded = sem("small_loaded")
        w_loaded = {k: sem(f"w{k}_loaded") for k in "qkv"}
        ipa_loaded = sem("ipa_loaded")
        x_loaded = [sem(f"xstat{i}_loaded") for i in range(2)]
        stats_done = sem("stats_done")
        ident_done = sem("ident_done")
        down_turned = sem("down_turned")
        down_copied = sem("down_copied")
        lora_done = sem("lora_done")
        eff_done = sem("eff_done")
        high_done = sem("high_done")
        low_done = sem("low_done")
        ictx_turned = sem("ictx_turned")
        ictx_copied = sem("ictx_copied")
        kipa_done = sem("kipa_done")
        vipa_done = sem("vipa_done")
        kipa_h = sem("kipa_h_done")
        vipa_hd = sem("vipa_h_done")
        vipa_stored = sem("vipa_stored")
        aggr_done = sem("aggr_done")
        std_done = sem("std_done")
        prep_done = sem("prep_done")
        bn_done = sem("bn_done")
        pieces = [("k", c, n, XC + c, 1.0, 1) for c in range(CC) for n in range(2)]
        pieces += [("q", c, n, c, SCALE, 0) for c in range(XC) for n in range(2)]
        pieces += [("v", c, n, XC + CC + c, 1.0, 2) for c in range(CC) for n in range(2)]
        block = ctx.enter_context(nc.Block())

        @block.sync
        def _(sp):
            for i, (k, c0, n) in enumerate((("q", 0, XC), ("k", XC, CC), ("v", XC + CC, CC))):
                sp.dma_start(down[:, c0:c0 + n, :], dram[f"{k}_down"].rearrange("(c p) r -> p c r", p=P)).then_inc(small_loaded, 16)
                sp.dma_start(up[:, i, :], dram[f"{k}_up"]).then_inc(small_loaded, 16)
                sp.dma_start(alpha[:, i:i + 1], dram[f"{k}_alpha"].rearrange("(a o) -> a o", o=1).to_broadcast((P, 1))).then_inc(small_loaded, 16)
            for k in "kqv":
                sp.dma_start(raw[k][:], dram[f"W{k}"].rearrange("(c p) n -> p c n", p=P)).then_inc(w_loaded[k], 16)
            for b in range(B):
                sp.dma_start(ictx[b * IPA:(b + 1) * IPA, :], dram["ctx"][b, CTX - IPA:CTX, :]).then_inc(ipa_loaded, 16)
            sp.dma_start(wki[:], dram["Wk_ipa"].rearrange("(c p) n -> p c n", p=P)).then_inc(ipa_loaded, 16)
            sp.dma_start(wvi[:], dram["Wv_ipa"].rearrange("(c p) n -> p c n", p=P)).then_inc(ipa_loaded, 16)
            sp.wait_ge(prep_done, 3)
            sp.dma_start(dram["vipa"], vipa[:].rearrange("p h d -> p (h d)")).then_inc(vipa_stored, 16)
            sp.wait_ge(vipa_stored, 16)

        @block.gpsimd
        def _(pool):
            nc.gpsimd.memset(ones[:], 1.0).then_inc(ident_done, 1)
            pool.wait_ge(ident_done, 1)
            nc.gpsimd.affine_select(out=ident[:], in_=ones[:], compare_op=ALU.is_equal, fill=0.0, base=0,
                                    pattern=[[-1, P]], channel_multiplier=1).then_inc(ident_done, 1)

        @block.scalar
        def _(act):
            for i in range(2):
                act.dma_start(xb[:, i], dram["x_pq"][i]).then_inc(x_loaded[i], 16)
            with act.Fori(0, B // 2 - 1) as two:
                for i in range(2):
                    act.wait_ge(bn_done, two * (2 * QT) + QT * (i + 1))
                    act.dma_start(xb[:, i], dram["x_pq"][bass.ds(two * 2 + (2 + i), 1)].rearrange("o p t d -> (o p) t d")).then_inc(x_loaded[i], 16)
            act.wait_ge(down_turned, 1)
            nc.scalar.copy(downT[:], ps_down[:, 0:XC + 2 * CC, :]).then_inc(down_copied, 1)
            for i, (k, c, n, _, s, _) in enumerate(pieces):
                act.wait_ge(eff_done, i + 1)
                nc.scalar.activation(split[k][0][:, c, n * 512:n * 512 + 512], raw[k][:, c, n * 512:n * 512 + 512],
                                     ACT.Copy, scale=s).then_inc(high_done, 1)
            act.wait_ge(kipa_done, 1)
            nc.scalar.copy(kipa[:, :, 0, :], ps_i[:, 0:PAIRS * B * IPA].rearrange("p (s j) -> p s j", s=PAIRS)).then_inc(kipa_h, 1)
            act.wait_ge(vipa_done, 1)
            nc.scalar.copy(vipa_h[:], ps_v[:].rearrange("p n (h d) -> p (n h) d", d=DH)).then_inc(vipa_hd, 1)
            act.wait_ge(aggr_done, NT + 1)
            nc.scalar.activation(std[:], mv[:, :, 1], ACT.Sqrt, bias=eps[:, 0:1]).then_inc(std_done, 1)

        @block.vector
        def _(dve):
            nc.vector.memset(eps[:], EPS).then_inc(aggr_done, 1)
            with dve.Fori(0, B // 2) as two:
                b = two * 2
                for i in range(2):
                    dve.wait_ge(x_loaded[i], b * 8 + 16)
                    for q in range(QT):
                        nc.vector.bn_stats(bn[:, bass.ds(b * QT + (i * QT + q), 1), :].rearrange("p o s -> p (o s)"), xb[:, i, q, :]).then_inc(bn_done, 1)
            dve.wait_ge(bn_done, NT)
            for n in range(NT):
                nc.vector.bn_aggr(mv[:, n, :], bn[:, n, :]).then_inc(aggr_done, 1)
            dve.wait_ge(small_loaded, 9 * 16)
            nc.vector.tensor_scalar(alpha_r[:], alpha[:], 1.0 / RANK, None, ALU.mult).then_inc(stats_done, 1)
            dve.wait_ge(stats_done, 1)
            for i, (k, c, n, _, s, j) in enumerate(pieces):
                w = raw[k][:, c, n * 512:n * 512 + 512]
                if i in (0, 6, 14):
                    dve.wait_ge(w_loaded[k], 16)
                dve.wait_ge(lora_done, i + 1)
                nc.vector.scalar_tensor_tensor(out=w, in0=ps_w[:, i % 2, :], scalar=alpha_r[:, j:j + 1], in1=w,
                                               op0=ALU.mult, op1=ALU.add).then_inc(eff_done, 1)
                dve.wait_ge(high_done, i + 1)
                nc.vector.scalar_tensor_tensor(out=split[k][1][:, c, n * 512:n * 512 + 512], in0=w, scalar=s,
                                               in1=split[k][0][:, c, n * 512:n * 512 + 512].bitcast(F32),
                                               op0=ALU.mult, op1=ALU.subtract).then_inc(low_done, 1)
            dve.wait_ge(ictx_turned, 1)
            nc.vector.tensor_copy(ictxT[:], ps_i[:, 0:CC * B * IPA].rearrange("p (c j) -> p c j", c=CC)).then_inc(ictx_copied, 1)
            dve.wait_ge(kipa_h, 1)
            nc.vector.tensor_tensor(kipa[:, :, 1, :], ps_i[:, 0:PAIRS * B * IPA].rearrange("p (s j) -> p s j", s=PAIRS),
                                    kipa[:, :, 0, :].bitcast(F32), ALU.subtract).then_inc(prep_done, 1)
            dve.wait_ge(vipa_hd, 1)
            nc.vector.tensor_copy(vipa[:, :, 0:DH], vipa_h[:].bitcast(F32)).then_inc(prep_done, 1)
            nc.vector.tensor_tensor(vipa[:, :, DH:2 * DH], ps_v[:].rearrange("p n (h d) -> p (n h) d", d=DH),
                                    vipa_h[:].bitcast(F32), ALU.subtract).then_inc(prep_done, 1)
            dve.wait_ge(aggr_done, NT + 1)
            nc.vector.tensor_copy(mean[:], mv[:, :, 0]).then_inc(prep_done, 1)
            dve.wait_ge(std_done, 1)
            nc.vector.reciprocal(rstd[:], std[:]).then_inc(prep_done, 1)

        @block.tensor
        def _(pe):
            pe.wait_ge(ident_done, 2)
            pe.wait_ge(small_loaded, 9 * 16)
            for c in range(XC + 2 * CC):
                mm = nc.tensor.transpose(ps_down[:, c, :], down[:, c, :], ident[:])
            mm.then_inc(down_turned, 1)
            pe.wait_ge(down_copied, 1)
            for i, (k, c, n, dc, _, j) in enumerate(pieces):
                if i >= 2:
                    pe.wait_ge(eff_done, i - 1)
                nc.tensor.matmul(ps_w[:, i % 2, :], downT[:, dc, :], up[:, j, n * 512:n * 512 + 512],
                                 start=True, stop=True).then_inc(lora_done, 1)
            pe.wait_ge(ipa_loaded, (B + 2) * 16)
            for c in range(CC):
                mm = nc.tensor.transpose(ps_i[:, c * B * IPA:(c + 1) * B * IPA], ictx[:, c * P:(c + 1) * P], ident[0:B * IPA, 0:B * IPA])
            mm.then_inc(ictx_turned, 1)
            pe.wait_ge(ictx_copied, 1)
            for s in range(PAIRS):
                for c in range(CC):
                    mm = nc.tensor.matmul(ps_i[:, s * B * IPA:(s + 1) * B * IPA], wki[:, c, s * P:(s + 1) * P], ictxT[:, c, :],
                                          start=(c == 0), stop=(c == CC - 1))
            mm.then_inc(kipa_done, 1)
            for n in range(2):
                for c in range(CC):
                    mm = nc.tensor.matmul(ps_v[:, n, :], ictxT[:, c, :], wvi[:, c, n * 512:n * 512 + 512],
                                          start=(c == 0), stop=(c == CC - 1))
            mm.then_inc(vipa_done, 1)


def batch_schedule():
    prep = [("ctx", c) for c in range(KCN)] + [("x", q) for q in range(QT)]
    pair = lambda s: [("k", s, 0), ("k", s, 1), ("q", s)]
    values = lambda g: [("v", g, c) for c in range(KCN)]
    own = prep + pair(0) + values(0)
    prologue = list(enumerate(own))
    per_head = [[] for _ in range(HEADS)]
    n = len(own)
    for k in range(13):
        if k % 2 == 0:
            new = pair(k // 2 + 1)
        elif k < 12:
            g = (k + 3) // 4
            new = values(g)[:3] if (k + 3) % 4 == 0 else values((k + 1) // 4)[3:]
        per_head[k] = [(n + i, w) for i, w in enumerate(new)]
        n += len(new)
    assert n == GROUPS
    after = {13: prologue[:8], 14: prologue[8:11], 15: prologue[11:]}
    return prologue, per_head, after


def attend(nc, dram, const):
    wq_h, wq_l, wk_h, wk_l, wv_h, wv_l, ident, kipa, rstd, mean = (
        const[k] for k in ("wq_h", "wq_l", "wk_h", "wk_l", "wv_h", "wv_l", "ident", "kipa", "rstd", "mean"))
    with ExitStack() as ctx:
        def sb(name, shape, dt=F32):
            return ctx.enter_context(nc.sbuf_tensor(name, shape, dt))

        def psum(name, shape):
            return ctx.enter_context(nc.psum_tensor(name, shape, F32))

        def sem(name):
            return ctx.enter_context(nc.semaphore(name))

        x_raw = sb("x_raw", [TQ, QT, D])
        xn = sb("xn", [TQ, QT, D])
        xT = [sb(f"xT_{p}", [P, XC, N], F32R) for p in "hl"]
        ctx_raw = sb("ctx_raw", [KC, KCN, CD])
        ctxT = [sb(f"ctxT_{p}", [P, CC, 2, KHP], F32R) for p in "hl"]
        K = sb("K", [P, 2, 2, 2, KHP], F32R)
        Q = sb("Q", [P, 2, 2, 2, N], F32R)
        V = sb("V", [KC, 2, KCN, VH, 2 * DH], F32R)
        vipa = sb("vipa_rows", [2, 2, VH * 2 * DH])
        prob = sb("prob", [TQ, 2, QT, 2, KHP])
        pT = [sb(f"pT_{p}", [KC, KCN, N], F32R) for p in "hl"]
        nmax = sb("nmax", [TQ, 2, QT, 2])
        sums = sb("sums", [TQ, 2, QT, 2])
        rsum = sb("rsum", [TQ, 2, QT, 2])
        one = sb("one", [2, 1])
        zero = sb("zero", [P, D // 2])
        low_o = sb("low_o", [DH, 2, N])
        oT = sb("oT", [P, 2, N])
        ps_s = psum("ps_s", [TQ, QT, 2, 512])
        ps_t = psum("ps_t", [P, 512])
        ps_o = psum("ps_o", [P, 512])
        banks = psum("ps_g", [P, 2, 512])

        x_loaded = sem("x_loaded")
        ctx_loaded = sem("ctx_loaded")
        x_normed = sem("x_normed")
        vipa_loaded = sem("vipa_loaded")
        vipa_used = sem("vipa_used")
        zeroed = sem("zeroed")
        cleared = sem("cleared")
        group_ready = sem("group_ready")
        group_high = sem("group_high")
        group_done = sem("group_done")
        kipa_ready = sem("kipa_ready")
        scores_ready = sem("scores_ready")
        max_ready = sem("max_ready")
        exp_done = sem("exp_done")
        rsum_ready = sem("rsum_ready")
        prob_ready = sem("prob_ready")
        turned = sem("turned")
        turned_high = sem("turned_high")
        turned_done = sem("turned_done")
        out_ready = sem("out_ready")
        out_low = sem("out_low")
        out_done = sem("out_done")
        out_stored = [sem(f"out_stored{i}") for i in range(2)]

        prologue, per_head, after = batch_schedule()
        block = ctx.enter_context(nc.Block())

        def group_no(b, n, ahead):
            return b * GROUPS + (n + GROUPS * ahead)

        def scores_unit(b, k, q):
            return b * HEADS * QT + (k * QT + q)

        def iteration(b, k, last):
            todo, ahead = (per_head[k], 0) if per_head[k] else (after[k], 1)
            return ([] if last and ahead else todo), ahead, (k + 1 < HEADS or not last), ((b, k + 1) if k + 1 < HEADS else (b + 1, 0))

        def thirds(todo):
            m = -(-len(todo) // 3)
            return todo[:m], todo[m:2 * m], todo[2 * m:]

        def each_batch(engine, first, body):
            first()
            with engine.Fori(0, B - 1) as b:
                body(b, False)
            body(B - 1, True)

        @block.sync
        def _(sp):
            def load_ctx(b):
                src = dram["ctx"][b] if isinstance(b, int) else dram["ctx"][bass.ds(b, 1)].rearrange("o k d -> (o k) d")
                for h in range(2):
                    t0 = h * ORG
                    c0 = 3 * h
                    sp.dma_start(ctx_raw[0:2, c0, :], src[CTX - IPA + 2 * h:CTX - IPA + 2 * h + 2, :]).then_inc(ctx_loaded, 16)
                    sp.dma_start(ctx_raw[2:KC, c0, :], src[t0:t0 + KC - 2, :]).then_inc(ctx_loaded, 16)
                    sp.dma_start(ctx_raw[:, c0 + 1:c0 + 3, :],
                                 src[t0 + KC - 2:t0 + ORG, :].rearrange("(c p) d -> p c d", p=KC)).then_inc(ctx_loaded, 16)

            def load_x(b):
                src = dram["x_pq"][b] if isinstance(b, int) else dram["x_pq"][bass.ds(b, 1)].rearrange("o p t d -> (o p) t d")
                sp.dma_start(x_raw[:], src).then_inc(x_loaded, 16)

            def load_vipa(b, g):
                src = dram["vipa"].rearrange("(b h j) n -> b j h n", h=2, j=2)
                src = src[b] if isinstance(b, int) else src[bass.ds(b, 1)].rearrange("o j h n -> (o j) h n")
                sp.dma_start(vipa[:], src[:, :, g * VH * 2 * DH:(g + 1) * VH * 2 * DH]).then_inc(vipa_loaded, 16)

            def store(b, s):
                sp.wait_ge(out_done, b * HEADS + (2 * s + 3))
                dst = dram["oT"][s * P:(s + 1) * P]
                dst = dst[:, b, :] if isinstance(b, int) else dst[:, bass.ds(b, 1), :].rearrange("p o n -> p (o n)")
                sp.dma_start(dst, oT[:, s % 2, :]).then_inc(out_stored[s % 2], 16)

            def first():
                for i in range(2):
                    sp.sem_inc(out_stored[i], 16)
                load_ctx(0)
                load_x(0)
                load_vipa(0, 0)
                sp.wait_ge(cleared, 5)
                slots = dram["slots"].rearrange("(p s) (h d) -> p (s h) d", p=P, h=2)
                sp.dma_start(slots, zero[:].rearrange("p (o d) -> p o d", o=1).to_broadcast((P, ROOM * STEP // P * 2, D // 2))).then_inc(zeroed, 16)

            def body(b, last):
                for s in range(PAIRS):
                    if s in (0, 2, 4):
                        g = s // 2 + 1
                        sp.wait_ge(vipa_used, b * VG + g)
                        load_vipa(b, g)
                    if s == 1 and not last:
                        sp.wait_ge(group_ready, group_no(b, 6, 0))
                        load_ctx(b + 1)
                        sp.wait_ge(x_normed, b + 1)
                        load_x(b + 1)
                    if s == 6 and not last:
                        sp.wait_ge(vipa_used, b * VG + VG)
                        load_vipa(b + 1, 0)
                    store(b, s)

            each_batch(sp, first, body)
            for i in range(2):
                sp.wait_ge(out_stored[i], 16 * B * PAIRS // 2 + 16)
            sp.wait_ge(zeroed, 16)

        @block.gpsimd
        def _(pool):
            nc.gpsimd.memset(Q[:].bitcast(F32), 0.0).then_inc(cleared, 1)
            nc.gpsimd.memset(one[:], 1.0).then_inc(cleared, 1)
            nc.gpsimd.memset(zero[:], 0.0).then_inc(cleared, 1)
            for p in range(2):
                nc.gpsimd.memset(ctxT[p][:, :, :, KH:KHP].bitcast(F32), 0.0).then_inc(cleared, 1)

            def kipa_columns(b, n, s, ahead):
                pool.wait_ge(group_ready, group_no(b, n + 1, ahead))
                j0 = b * IPA + ahead * IPA
                src = kipa[:, s, :, bass.ds(j0, IPA)] if not isinstance(j0, int) else kipa[:, s, :, j0:j0 + IPA]
                nc.gpsimd.tensor_copy(K[:, s % 2, :, :, 0:2],
                                      src.bitcast(F32).rearrange("p l (h j) -> p l h j", h=2)).then_inc(kipa_ready, 1)

            def vipa_rows(b, n, g, ahead):
                pool.wait_ge(group_done, group_no(b, n + 1, ahead))
                pool.wait_ge(vipa_loaded, 16 * (b * VG + (g + ahead * VG + 1)))
                nc.gpsimd.tensor_tensor(V[0:2, g % 2, 0:4:3].rearrange("p c h d -> p c (h d)"), vipa[:],
                                        one[:].rearrange("p (o u) -> p o u", o=1).to_broadcast((2, 2, VH * 2 * DH)), ALU.mult).then_inc(vipa_used, 1)

            def normalise(b, k, q):
                pool.wait_ge(rsum_ready, scores_unit(b, k, q) + 1)
                p = prob[:, k % 2, q]
                nc.gpsimd.tensor_tensor(p[:, :, 0:2], p[:, :, 0:2], rsum[:, k % 2, q, 1:2].rearrange("p (o u) -> p o u", o=1).to_broadcast((TQ, 2, 2)), ALU.mult)
                nc.gpsimd.tensor_scalar(p[:, :, 2:KH], p[:, :, 2:KH], rsum[:, k % 2, q, 0:1], 1.0, ALU.mult, ALU.mult).then_inc(prob_ready, 1)

            def keys(b, todo, ahead):
                for n, what in todo:
                    if what[0] == "k" and what[2] == 0:
                        kipa_columns(b, n, what[1], ahead)

            def value_rows(b, todo, ahead):
                for n, what in todo:
                    if what[0] == "v" and what[2] == KCN - 1:
                        vipa_rows(b, n, what[1], ahead)

            def first():
                pool.wait_ge(cleared, 5)
                keys(0, prologue, 0)
                value_rows(0, prologue, 0)
                for q in range(QT):
                    normalise(0, 0, q)

            def body(b, last):
                for k in range(HEADS):
                    todo, ahead, more, nxt = iteration(b, k, last)
                    keys(b, todo, ahead)
                    if more:
                        for q in range(QT):
                            normalise(*nxt, q)
                    value_rows(b, todo, ahead)

            each_batch(pool, first, body)

        @block.scalar
        def _(act):
            def high(b, todo, ahead):
                for n, what in todo:
                    ps_g = banks[:, n % 2]
                    act.wait_ge(group_ready, group_no(b, n + 1, ahead))
                    if what[0] == "ctx":
                        c = what[1]
                        last = nc.scalar.copy(ctxT[0][:, :, c // 3, c % 3 * KC:(c % 3 + 1) * KC], ps_g[:, 0:CC * KC].rearrange("p (c k) -> p c k", c=CC))
                    elif what[0] == "x":
                        q = what[1]
                        last = nc.scalar.copy(xT[0][:, :, q * TQ:(q + 1) * TQ], ps_g[:, 0:XC * TQ].rearrange("p (c k) -> p c k", c=XC))
                    elif what[0] == "k":
                        s, h = what[1:]
                        last = nc.scalar.copy(K[:, s % 2, 0, h, 2:KHP], ps_g[:, 2:KHP])
                    elif what[0] == "q":
                        s = what[1]
                        nc.scalar.copy(Q[0:DH, s % 2, 0, 0, :], ps_g[0:DH, 0:N])
                        last = nc.scalar.copy(Q[DH:P, s % 2, 0, 1, :], ps_g[DH:P, 0:N])
                    else:
                        g, c = what[1:]
                        last = nc.scalar.copy(V[:, g % 2, c, :, 0:DH], ps_g[0:KC, 0:VH * DH].rearrange("p (h d) -> p h d", d=DH))
                    last.then_inc(group_high, 1)

            def exponentials(b, k, q):
                act.wait_ge(max_ready, scores_unit(b, k, q) + 1)
                for i, (a, e) in enumerate(((2, KH), (0, 2))):
                    last = nc.scalar.activation(prob[:, k % 2, q, :, a:e], ps_s[:, q, :, a:e], ACT.Exp,
                                                bias=nmax[:, k % 2, q, i:i + 1], accum_out=sums[:, k % 2, q, i:i + 1])
                last.then_inc(exp_done, 1)

            def out_part(b, k):
                act.wait_ge(out_ready, b * HEADS + (k + 1))
                nc.scalar.copy(low_o[:, k % 2, :], ps_o[DH:P, 0:N]).then_inc(out_low, 1)

            def turned_part(b, k, j):
                act.wait_ge(turned, b * HEADS * 3 + (k * 3 + j + 1))
                nc.scalar.copy(pT[0][:, 2 * j:2 * j + 2, :].rearrange("p c n -> p (c n)"), ps_t[0:KC, 0:2 * N]).then_inc(turned_high, 1)

            def first():
                act.wait_ge(cleared, 5)
                high(0, prologue, 0)
                exponentials(0, 0, 0)
                exponentials(0, 0, 1)

            def body(b, last):
                for k in range(HEADS):
                    todo, ahead, more, nxt = iteration(b, k, last)
                    g1, g2, g3 = thirds(todo)
                    if k > 0:
                        out_part(b, k - 1)
                    turned_part(b, k, 0)
                    if more:
                        exponentials(*nxt, 0)
                    high(b, g1, ahead)
                    turned_part(b, k, 1)
                    if more:
                        exponentials(*nxt, 1)
                    high(b, g2, ahead)
                    turned_part(b, k, 2)
                    high(b, g3, ahead)
                out_part(b, HEADS - 1)

            each_batch(act, first, body)

        @block.vector
        def _(dve):
            def norm_x(b):
                dve.wait_ge(x_loaded, 16 * b + 16)
                for q in range(QT):
                    i = b * QT + q
                    m = mean[:, i:i + 1] if isinstance(i, int) else mean[:, bass.ds(i, 1)]
                    r = rstd[:, i:i + 1] if isinstance(i, int) else rstd[:, bass.ds(i, 1)]
                    last = nc.vector.tensor_scalar(xn[:, q, :], x_raw[:, q, :], m, r, ALU.subtract, ALU.mult)
                last.then_inc(x_normed, 1)

            def low(b, todo, ahead):
                for n, what in todo:
                    ps_g = banks[:, n % 2]
                    dve.wait_ge(group_high, group_no(b, n + 1, ahead))
                    if what[0] == "ctx":
                        c = what[1]
                        at = (slice(None), slice(None), c // 3, slice(c % 3 * KC, (c % 3 + 1) * KC))
                        last = nc.vector.tensor_tensor(ctxT[1][at], ps_g[:, 0:CC * KC].rearrange("p (c k) -> p c k", c=CC), ctxT[0][at].bitcast(F32), ALU.subtract)
                    elif what[0] == "x":
                        q = what[1]
                        last = nc.vector.tensor_tensor(xT[1][:, :, q * TQ:(q + 1) * TQ], ps_g[:, 0:XC * TQ].rearrange("p (c k) -> p c k", c=XC),
                                                       xT[0][:, :, q * TQ:(q + 1) * TQ].bitcast(F32), ALU.subtract)
                    elif what[0] == "k":
                        s, h = what[1:]
                        last = nc.vector.tensor_tensor(K[:, s % 2, 1, h, 2:KHP], ps_g[:, 2:KHP], K[:, s % 2, 0, h, 2:KHP].bitcast(F32), ALU.subtract)
                    elif what[0] == "q":
                        s = what[1]
                        for i, r in enumerate((slice(0, DH), slice(DH, P))):
                            last = nc.vector.tensor_tensor(Q[r, s % 2, 1, i, :], ps_g[r, 0:N], Q[r, s % 2, 0, i, :].bitcast(F32), ALU.subtract)
                    else:
                        g, c = what[1:]
                        last = nc.vector.tensor_tensor(V[:, g % 2, c, :, DH:2 * DH], ps_g[0:KC, 0:VH * DH].rearrange("p (h d) -> p h d", d=DH),
                                                       V[:, g % 2, c, :, 0:DH].bitcast(F32), ALU.subtract)
                    last.then_inc(group_done, 1)

            def maxima(b, k, q):
                dve.wait_ge(scores_ready, scores_unit(b, k, q) + 1)
                for i, (a, e) in enumerate(((2, KH), (0, 2))):
                    last = nc.vector.tensor_reduce(nmax[:, k % 2, q, i:i + 1], ps_s[:, q, :, a:e], AX.XY, ALU.max, negate=True)
                last.then_inc(max_ready, 1)

            def reciprocals(b, k, q):
                dve.wait_ge(exp_done, scores_unit(b, k, q) + 1)
                nc.vector.reciprocal(rsum[:, k % 2, q], sums[:, k % 2, q]).then_inc(rsum_ready, 1)

            def out_part(b, k):
                s = k // 2
                if k % 2 == 0:
                    dve.wait_ge(out_stored[s % 2], b * (16 * PAIRS // 2) + 16 * (s // 2 + 1))
                dve.wait_ge(out_low, b * HEADS + (k + 1))
                nc.vector.tensor_tensor(oT[k % 2 * DH:(k % 2 + 1) * DH, s % 2, :], ps_o[0:DH, 0:N], low_o[:, k % 2, :], ALU.add).then_inc(out_done, 1)

            def turned_part(b, k, j):
                dve.wait_ge(turned_high, b * HEADS * 3 + (k * 3 + j + 1))
                nc.vector.tensor_tensor(pT[1][:, 2 * j:2 * j + 2, :].rearrange("p c n -> p (c n)"), ps_t[0:KC, 0:2 * N],
                                        pT[0][:, 2 * j:2 * j + 2, :].rearrange("p c n -> p (c n)").bitcast(F32), ALU.subtract).then_inc(turned_done, 1)

            def first():
                dve.sem_inc(out_done, 1)
                norm_x(0)
                dve.wait_ge(cleared, 5)
                low(0, prologue, 0)
                for q in range(QT):
                    maxima(0, 0, q)
                for q in range(QT):
                    reciprocals(0, 0, q)

            def body(b, last):
                for k in range(HEADS):
                    todo, ahead, more, nxt = iteration(b, k, last)
                    g1, g2, g3 = thirds(todo)
                    if k > 0:
                        out_part(b, k - 1)
                    if more:
                        maxima(*nxt, 0)
                    turned_part(b, k, 0)
                    low(b, g1, ahead)
                    if more:
                        reciprocals(*nxt, 0)
                        maxima(*nxt, 1)
                    turned_part(b, k, 1)
                    low(b, g2, ahead)
                    if more:
                        reciprocals(*nxt, 1)
                    turned_part(b, k, 2)
                    low(b, g3, ahead)
                    if k == 11 and not last:
                        norm_x(b + 1)
                out_part(b, HEADS - 1)

            each_batch(dve, first, body)

        @block.tensor
        def _(pe):
            passes = ((0, 0), (1, 0), (0, 1))

            def project(b, todo, ahead):
                for n, what in todo:
                    ps_g = banks[:, n % 2]
                    if not (isinstance(b, int) and b == 0 and n < 2):
                        pe.wait_ge(group_done, group_no(b, n - 1, ahead))
                    if what[0] == "ctx":
                        c = what[1]
                        if c == 0:
                            pe.wait_ge(ctx_loaded, 96 * b + 96 * (1 + ahead))
                        for j in range(CC):
                            mm = nc.tensor.transpose(ps_g[:, j * KC:(j + 1) * KC], ctx_raw[:, c, j * P:(j + 1) * P], ident[0:KC, 0:KC])
                    elif what[0] == "x":
                        q = what[1]
                        if q == 0:
                            pe.wait_ge(x_normed, b + (1 + ahead))
                        for j in range(XC):
                            mm = nc.tensor.transpose(ps_g[:, j * TQ:(j + 1) * TQ], xn[:, q, j * P:(j + 1) * P], ident[0:TQ, 0:TQ])
                    elif what[0] == "k":
                        s, h = what[1:]
                        w = (wk_h, wk_l)
                        for i, (c, (a, m)) in enumerate((c, p) for c in range(CC) for p in passes):
                            mm = nc.tensor.matmul(ps_g[:, 0:KHP], w[a][:, c, s * P:(s + 1) * P], ctxT[m][:, c, h, :], start=(i == 0), stop=(i == 3 * CC - 1))
                    elif what[0] == "q":
                        s = what[1]
                        w = (wq_h, wq_l)
                        for i, (c, (a, m)) in enumerate((c, p) for c in range(XC) for p in passes):
                            mm = nc.tensor.matmul(ps_g[:, 0:N], w[a][:, c, s * P:(s + 1) * P], xT[m][:, c, :], start=(i == 0), stop=(i == 3 * XC - 1))
                    else:
                        g, kc = what[1:]
                        w = (wv_h, wv_l)
                        for i, (c, (a, m)) in enumerate((c, p) for c in range(CC) for p in passes):
                            mm = nc.tensor.matmul(ps_g[0:KC, 0:VH * DH], ctxT[a][:, c, kc // 3, kc % 3 * KC:(kc % 3 + 1) * KC],
                                                  w[m][:, c, g * VH * DH:(g + 1) * VH * DH], start=(i == 0), stop=(i == 3 * CC - 1))
                    mm.then_inc(group_ready, 1)

            def score(b, k, q, first=False):
                s = k // 2
                if k % 2 == 0 and q == 0:
                    n = 11 if s == 0 else next(n for n, w in per_head[2 * s - 2] if w[0] == "q") + 1
                    pe.wait_ge(group_done, group_no(b, n, 0))
                    pe.wait_ge(kipa_ready, b * PAIRS + (s + 1))
                if not first:
                    pe.wait_ge(exp_done, scores_unit(b, k, q) - 1)
                for h in range(2):
                    for i, (a, m) in enumerate(passes):
                        mm = nc.tensor.matmul(ps_s[:, q, h, 0:KHP], Q[:, s % 2, a, k % 2, q * TQ:(q + 1) * TQ], K[:, s % 2, m, h, :],
                                              start=(i == 0), stop=(i == 2))
                mm.then_inc(scores_ready, 1)

            def turn(b, k, j):
                if j == 0:
                    pe.wait_ge(prob_ready, scores_unit(b, k, 1) + 1)
                if k > 0 or j > 0:
                    pe.wait_ge(turned_done, b * HEADS * 3 + (k * 3 + j))
                for c in range(2 * j, 2 * j + 2):
                    for q in range(QT):
                        o = (c - 2 * j) * N + q * TQ
                        mm = nc.tensor.transpose(ps_t[0:KC, o:o + TQ],
                                                 prob[:, k % 2, q, c // 3, c % 3 * KC:(c % 3 + 1) * KC], ident[0:TQ, 0:TQ])
                mm.then_inc(turned, 1)

            def values(b, k):
                pe.wait_ge(turned_done, b * HEADS * 3 + 3 * (k + 1))
                if k % VH == 0:
                    pe.wait_ge(vipa_used, b * VG + (k // VH + 1))
                pe.wait_ge(out_done, b * HEADS + (k + 1))
                for i, (c, m) in enumerate((c, m) for c in range(KCN) for m in range(2)):
                    mm = nc.tensor.matmul(ps_o[:, 0:N], V[:, k // VH % 2, c, k % VH, :], pT[m][:, c, :], start=(i == 0), stop=(i == 2 * KCN - 1))
                mm.then_inc(out_ready, 1)

            def first():
                pe.wait_ge(cleared, 5)
                project(0, prologue, 0)
                score(0, 0, 0, True)
                score(0, 0, 1, True)

            def body(b, last):
                for k in range(HEADS):
                    todo, ahead, more, nxt = iteration(b, k, last)
                    g1, g2, g3 = thirds(todo)
                    if k > 0:
                        values(b, k - 1)
                    if more:
                        score(*nxt, 0)
                    turn(b, k, 0)
                    project(b, g1, ahead)
                    if more:
                        score(*nxt, 1)
                    turn(b, k, 1)
                    project(b, g2, ahead)
                    turn(b, k, 2)
                    project(b, g3, ahead)
                values(b, HEADS - 1)

            each_batch(pe, first, body)


def project(nc, dram, const):
    ident, logits = const["ident"], const["logits"]
    OC = ID // P
    with ExitStack() as ctx:
        def sb(name, shape, dt=F32):
            return ctx.enter_context(nc.sbuf_tensor(name, shape, dt))

        def psum(name, shape):
            return ctx.enter_context(nc.psum_tensor(name, shape, F32))

        def sem(name):
            return ctx.enter_context(nc.semaphore(name))

        wo = sb("wo_raw", [P, OC, D])
        wo_h = sb("wo_h", [P, OC, D], F32R)
        wo_l = sb("wo_l", [P, OC, D], F32R)
        down = sb("o_down_sb", [P, OC, RANK])
        downT = sb("o_downT", [RANK, OC, P])
        up = sb("o_up_sb", [RANK, D])
        alpha = sb("o_alpha_sb", [P, 2])
        bo = sb("bo_sb", [TQ, D])
        wg = sb("w_gate_sb", [P, XC, E])
        eps = sb("eps2", [TQ, 1])
        o_raw = sb("o_raw", [P, 2, OC, N])
        o_h = sb("o_h", [P, QT, OC, TQ], F32R)
        o_l = sb("o_l", [P, QT, OC, TQ], F32R)
        x_in = sb("x_in", [TQ, 2, QT, D])
        x2 = sb("x2_sb", [TQ, 2, QT, D])
        xn = sb("xn2_sb", [TQ, 2, QT, D])
        xnT = sb("xn2T", [P, QT, XC, TQ])
        bn = sb("bn2", [TQ, QT, 6])
        mv = sb("mv2", [TQ, QT, 2])
        std = sb("std2", [TQ, QT])
        rstd = sb("rstd2", [TQ, QT])
        ps_o = psum("ps_proj", [TQ, QT, 512])
        ps_t = psum("ps_xn2T", [P, QT, 512])
        ps_l = psum("ps_logits", [TQ, QT, 512])
        ps_w = psum("ps_wo", [P, 2, 512])

        small_loaded = sem("o_small_loaded")
        wo_loaded = sem("wo_loaded")
        in_loaded = [sem(f"in_loaded{i}") for i in range(2)]
        eps_set = sem("eps_set")
        down_turned = sem("o_down_turned")
        down_copied = sem("o_down_copied")
        lora_done = sem("o_lora_done")
        eff_done = sem("o_eff_done")
        high_done = sem("wo_high")
        low_done = sem("wo_low")
        o_high = sem("o_high")
        o_split = sem("o_split")
        projected = sem("projected")
        x2_partial = sem("x2_partial")
        x2_done = sem("x2_done")
        stats = sem("stats2")
        passed = sem("passed2")
        var_done = sem("var_done")
        std_done = sem("std2_done")
        rstd_done = sem("rstd2_done")
        xn_done = sem("xn2_done")
        xn_stored = [sem(f"xn2_stored{i}") for i in range(2)]
        xn_turned = sem("xn2_turned")
        xn_copied = sem("xn2_copied")
        gated = sem("gated")
        logits_done = sem("logits_done")
        x2_stored = [sem(f"x2_stored{i}") for i in range(2)]
        block = ctx.enter_context(nc.Block())

        @block.sync
        def _(sp):
            sp.dma_start(down[:], dram["o_down"].rearrange("(c p) r -> p c r", p=P)).then_inc(small_loaded, 16)
            sp.dma_start(up[:], dram["o_up"]).then_inc(small_loaded, 16)
            sp.dma_start(alpha[:, 0:1], dram["o_alpha"].rearrange("(a o) -> a o", o=1).to_broadcast((P, 1))).then_inc(small_loaded, 16)
            sp.dma_start(wo[:], dram["Wo"].rearrange("(c p) n -> p c n", p=P)).then_inc(wo_loaded, 16)
            sp.dma_start(bo[:], dram["bo"].rearrange("(o d) -> o d", o=1).to_broadcast((TQ, D))).then_inc(small_loaded, 16)
            sp.dma_start(wg[:], dram["w_gate"].rearrange("(c p) e -> p c e", p=P)).then_inc(small_loaded, 16)

            def load(b, i):
                sp.dma_start(o_raw[:, i], dram["oT"].rearrange("(c p) b n -> p c b n", p=P)[:, :, bass.ds(b, 1), :].rearrange("p c o n -> p c (o n)")).then_inc(in_loaded[i], 16)
                sp.dma_start(x_in[:, i], dram["x_pq"][bass.ds(b, 1)].rearrange("o p t d -> (o p) t d")).then_inc(in_loaded[i], 16)

            load(0, 0)
            load(1, 1)
            with sp.Fori(0, B // 2 - 1) as two:
                for i in range(2):
                    sp.wait_ge(x2_done, two * 4 + QT * (i + 1))
                    load(two * 2 + (2 + i), i)

        @block.gpsimd
        def _(pool):
            pool.wait_ge(small_loaded, 5 * 16)
            with pool.Fori(0, B // 2) as two:
                for i in range(2):
                    pool.wait_ge(in_loaded[i], two * 32 + 32)
                    for q in range(QT):
                        nc.gpsimd.tensor_tensor(x_in[:, i, q], x_in[:, i, q], bo[:], ALU.add).then_inc(x2_partial, 1)

        @block.scalar
        def _(act):
            for i in range(2):
                act.sem_inc(x2_stored[i], 16)
                act.sem_inc(xn_stored[i], 16)
            act.wait_ge(down_turned, 1)
            nc.scalar.copy(downT[:, 0:4], ps_w[0:RANK, 0].rearrange("r (c p) -> r c p", p=P))
            nc.scalar.copy(downT[:, 4:8], ps_w[0:RANK, 1].rearrange("r (c p) -> r c p", p=P)).then_inc(down_copied, 1)
            for c in range(OC):
                act.wait_ge(eff_done, c + 1)
                nc.scalar.copy(wo_h[:, c], wo[:, c]).then_inc(high_done, 1)

            def turned_copy(two, i):
                for q in range(QT):
                    T = two * 4 + (2 * i + q)
                    act.wait_ge(xn_turned, T + 1)
                    nc.scalar.copy(xnT[:, q], ps_t[:, q, 0:XC * TQ].rearrange("p (c t) -> p c t", c=XC)).then_inc(xn_copied, 1)

            def batch(two, i):
                act.wait_ge(in_loaded[i], two * 32 + 32)
                for q in range(QT):
                    nc.scalar.copy(o_h[:, q], o_raw[:, i, :, q * TQ:(q + 1) * TQ]).then_inc(o_high, 1)
                for q in range(QT):
                    T = two * 4 + (2 * i + q)
                    act.wait_ge(var_done, T + 1)
                    nc.scalar.activation(std[:, q:q + 1], mv[:, q, 1:2], ACT.Sqrt, bias=eps[:, 0:1]).then_inc(std_done, 1)
                turned_copy(two, i)
                act.wait_ge(x2_done, two * 4 + QT * (i + 1))
                act.dma_start(dram["x2"][bass.ds(two * 2 + i, 1)].rearrange("o p t d -> (o p) t d"), x2[:, i]).then_inc(x2_stored[i], 16)
                act.wait_ge(xn_done, two * 4 + QT * (i + 1))
                act.dma_start(dram["xn2"][bass.ds(two * 2 + i, 1)].rearrange("o p t d -> (o p) t d"), xn[:, i]).then_inc(xn_stored[i], 16)

            with act.Fori(0, B // 2) as two:
                for i in range(2):
                    batch(two, i)
            for i in range(2):
                act.wait_ge(x2_stored[i], 16 * B // 2 + 16)
                act.wait_ge(xn_stored[i], 16 * B // 2 + 16)

        @block.vector
        def _(dve):
            nc.vector.memset(eps[:], EPS).then_inc(eps_set, 1)
            dve.wait_ge(small_loaded, 5 * 16)
            nc.vector.tensor_scalar(alpha[:, 1:2], alpha[:, 0:1], 1.0 / RANK, None, ALU.mult).then_inc(eps_set, 1)
            dve.wait_ge(eps_set, 2)
            dve.wait_ge(wo_loaded, 16)
            for c in range(OC):
                dve.wait_ge(lora_done, c + 1)
                nc.vector.scalar_tensor_tensor(out=wo[:, c], in0=ps_w[:, c % 2, :], scalar=alpha[:, 1:2], in1=wo[:, c],
                                               op0=ALU.mult, op1=ALU.add).then_inc(eff_done, 1)
                dve.wait_ge(high_done, c + 1)
                nc.vector.tensor_tensor(wo_l[:, c], wo[:, c], wo_h[:, c].bitcast(F32), ALU.subtract).then_inc(low_done, 1)
            with dve.Fori(0, B // 2) as two:
                for i in range(2):
                    for q in range(QT):
                        T = two * 4 + (2 * i + q)
                        dve.wait_ge(o_high, T + 1)
                        nc.vector.tensor_tensor(o_l[:, q], o_raw[:, i, :, q * TQ:(q + 1) * TQ], o_h[:, q].bitcast(F32), ALU.subtract).then_inc(o_split, 1)
                    dve.wait_ge(x2_stored[i], two * 16 + 16)
                    for q in range(QT):
                        T = two * 4 + (2 * i + q)
                        dve.wait_ge(projected, T + 1)
                        dve.wait_ge(x2_partial, T + 1)
                        nc.vector.tensor_tensor(x2[:, i, q], ps_o[:, q, :], x_in[:, i, q], ALU.add).then_inc(x2_done, 1)
                        dve.wait_ge(x2_done, T + 1)
                        nc.vector.bn_stats(bn[:, q], x2[:, i, q]).then_inc(stats, 1)
                        dve.wait_ge(stats, T + 1)
                        dve.sem_inc(passed, 1)
                        nc.vector.bn_aggr(mv[:, q], bn[:, q]).then_inc(var_done, 1)
                        dve.wait_ge(std_done, T + 1)
                        nc.vector.reciprocal(rstd[:, q:q + 1], std[:, q:q + 1]).then_inc(rstd_done, 1)
                        dve.wait_ge(rstd_done, T + 1)
                        dve.wait_ge(xn_stored[i], two * 16 + 16)
                        nc.vector.tensor_scalar(xn[:, i, q], x2[:, i, q], mv[:, q, 0:1], rstd[:, q:q + 1], ALU.subtract, ALU.mult).then_inc(xn_done, 1)
                    for q in range(QT):
                        T = two * 4 + (2 * i + q)
                        dve.wait_ge(gated, T + 1)
                        nc.vector.tensor_copy(logits[:, bass.ds(T, 1), :].rearrange("p o e -> p (o e)"), ps_l[:, q, 0:E]).then_inc(logits_done, 1)

        @block.tensor
        def _(pe):
            pe.wait_ge(small_loaded, 5 * 16)
            for c in range(OC):
                mm = nc.tensor.transpose(ps_w[0:RANK, c // 4, c % 4 * P:(c % 4 + 1) * P], down[:, c], ident[:])
            mm.then_inc(down_turned, 1)
            pe.wait_ge(down_copied, 1)
            for c in range(OC):
                if c >= 2:
                    pe.wait_ge(eff_done, c - 1)
                nc.tensor.matmul(ps_w[:, c % 2, :], downT[:, c], up[:], start=True, stop=True).then_inc(lora_done, 1)
            pe.wait_ge(low_done, OC)
            with pe.Fori(0, B // 2) as two:
                for i in range(2):
                    for q in range(QT):
                        T = two * 4 + (2 * i + q)
                        pe.wait_ge(o_split, T + 1)
                        for n, (c, (a, m)) in enumerate((c, p) for c in range(OC) for p in ((0, 0), (1, 0), (0, 1))):
                            mm = nc.tensor.matmul(ps_o[:, q, :], (o_h, o_l)[a][:, q, c], (wo_h, wo_l)[m][:, c], start=(n == 0), stop=(n == 3 * OC - 1))
                        mm.then_inc(projected, 1)
                    for q in range(QT):
                        T = two * 4 + (2 * i + q)
                        pe.wait_ge(xn_done, T + 1)
                        for c in range(XC):
                            mm = nc.tensor.transpose(ps_t[:, q, c * TQ:(c + 1) * TQ], xn[:, i, q, c * P:(c + 1) * P], ident[0:TQ, 0:TQ])
                        mm.then_inc(xn_turned, 1)
                    for q in range(QT):
                        T = two * 4 + (2 * i + q)
                        pe.wait_ge(xn_copied, T + 1)
                        for c in range(XC):
                            mm = nc.tensor.matmul(ps_l[:, q, 0:E], xnT[:, q, c], wg[:, c], start=(c == 0), stop=(c == XC - 1))
                        mm.then_inc(gated, 1)


def experts(nc, dram, const):
    ident, logits, pos, weight = (const[k] for k in ("ident", "logits", "pos", "weight"))
    with ExitStack() as ctx:
        def sb(name, shape, dt=F32):
            return ctx.enter_context(nc.sbuf_tensor(name, shape, dt))

        def psum(name, shape):
            return ctx.enter_context(nc.psum_tensor(name, shape, F32))

        def sem(name):
            return ctx.enter_context(nc.semaphore(name))

        W1 = sb("w1", [P, 2, 2, XC, 2 * F], F32R)
        W2 = sb("w2", [P, 2, 2, FC, D], F32R)
        raw = sb("w_stage", [P, 2, 2 * F])
        xg = sb("x_slots", [P, 2, D])
        xT = sb("x_slotsT", [P, 2, 2, XC, SUB], F32R)
        act_sb = sb("act", [P, 2, F])
        hT = sb("hT", [P, 2, 2, FC, SUB], F32R)
        y = sb("y", [P, 2, D])
        rows = hT[0:TQ].rearrange("p s l c t -> p (s l c t)").rearrange("p (n d) -> p n d", d=D).bitcast(F32)
        RING = 2 * 2 * FC * SUB // D
        ones = sb("ones_r", [TQ, TQ])
        tri = sb("tri", [TQ, TQ])
        iota = sb("iota_e", [TQ, E])
        thr = sb("thresholds", [TQ, KMAX])
        top = sb("top", [TQ, NT, 8])
        idx = sb("idx", [TQ, NT, 8], U32)
        idxf = sb("idxf", [TQ, NT, 2])
        hot = sb("hot", [TQ, 2, NT, E])
        both = sb("both", [TQ, NT, E])
        shifted = sb("shifted", [TQ, NT, E])
        expo = sb("expo", [TQ, NT, E])
        second = sb("second", [TQ, NT])
        second_e = sb("second_e", [TQ, NT])
        total = sb("total", [TQ, E])
        over = sb("over", [TQ, E, KMAX])
        nsteps = sb("nsteps", [TQ, E])
        before = sb("before", [TQ, E])
        count = sb("count", [TQ, NT, E])
        start = sb("start", [TQ, NT, E])
        slot = sb("slot", [TQ, NT, E])
        picked = sb("picked", [TQ, 2, NT, E])
        posf = sb("posf", [TQ, 2, NT])
        table = sb("table", [1, 2 * E], I32)
        ps_h = [psum(f"ps_h{i}", [P, 3, 512]) for i in range(2)]
        ps_t = psum("ps_turn", [P, 512])
        ps_y = psum("ps_y", [P, 512])

        raw_loaded = [sem(f"stage{i}_loaded") for i in range(2)]
        stage_loaded = [sem(f"stage{i}_loaded_pool") for i in range(2)]
        w0_high = sem("w0_high")
        w0_ready = sem("w0_ready")
        const_set = sem("const_set")
        tri_set = sem("tri_set")
        routed = sem("routed")
        shifted_ready = sem("shifted_ready")
        expo_ready = sem("expo_ready")
        both_ready = sem("both_ready")
        ranked = sem("ranked")
        table_ready = sem("table_ready")
        rows_loaded = [sem(f"rows{i}_loaded") for i in range(RING)]
        scattered = [sem(f"scattered{i}") for i in range(RING)]
        passed = sem("passed")
        ended = sem("ended")
        w_high = sem("w_high")
        w_ready = sem("w_ready")
        x_loaded = sem("slots_loaded")
        turned = sem("slots_turned")
        turned_high = sem("slots_turned_high")
        turned_done = sem("slots_turned_done")
        hidden = sem("hidden")
        silu_done = sem("silu_done")
        glu_done = sem("glu_done")
        y_ready = sem("y_ready")
        y_done = sem("y_done")
        y_stored = [sem(f"y{i}_stored") for i in range(2)]
        block = ctx.enter_context(nc.Block())

        PIECES = XC + FC * D // (2 * F)

        def piece_src(e, c):
            w1 = dram["c_fc"].rearrange("e (c p) f -> e c p f", p=P)
            w2 = dram["c_proj"].rearrange("e (h c p) d -> e h p c d", p=P, h=2)
            if c < XC:
                return w1[e, c] if isinstance(e, int) else w1[bass.ds(e, 1), c].rearrange("o p f -> (o p) f")
            return w2[e, c - XC] if isinstance(e, int) else w2[bass.ds(e, 1), c - XC].rearrange("o p c d -> (o p) c d")

        def stage(i, c):
            return raw[:, i] if c < XC else raw[:, i].rearrange("p (c d) -> p c d", d=D)

        def piece_dst(buf, part, c):
            if c < XC:
                return W1[:, buf, part, c]
            h = (c - XC) * (FC // 2)
            return W2[:, buf, part, h:h + FC // 2].rearrange("p c d -> p (c d)")

        def each_step(engine, body):
            engine.wait_ge(table_ready, 1)
            with engine.Fori(0, E // 2) as pair:
                for buf in range(2):
                    e = pair * 2 + buf
                    n = engine.value_load(table[0:1, bass.ds(e, 1)], min_val=1, max_val=KMAX)
                    first = engine.value_load(table[0:1, bass.ds(e + E, 1)], min_val=0, max_val=MAXSTEPS - 1)
                    with engine.Fori(0, n) as j:
                        body(buf, first + j, e)

        @block.sync
        def _(sp):
            for c in range(PIECES):
                if c >= 2:
                    sp.wait_ge(w0_ready, c - 1)
                sp.dma_start(stage(c % 2, c), piece_src(0, c)).then_inc(raw_loaded[c % 2], 16)
            for n in range(NT):
                if n >= RING:
                    sp.wait_ge(scattered[n % RING], 32 * (n // RING))
                sp.dma_start(rows[:, n % RING], dram["xn2"][n // QT, :, n % QT]).then_inc(rows_loaded[n % RING], 16)
            for i in range(RING):
                sp.wait_ge(scattered[i], 32 * len(range(i, NT, RING)))
            slots = dram["slots"].rearrange("(g s p) d -> g p s d", s=2, p=P)
            ys = dram["slots"].rearrange("(g s p) d -> g s p d", s=2, p=P)

            def load(g):
                sp.dma_start(xg[:], slots[bass.ds(g, 1)].rearrange("o p s d -> (o p) s d")).then_inc(x_loaded, 16)

            for i in range(2):
                sp.sem_inc(y_stored[i], 16)
            load(0)
            sp.wait_ge(turned, 2)
            load(1)

            def body(buf, g, e):
                sp.wait_ge(y_done, g * 2 + 2)
                sp.dma_start(ys[bass.ds(g, 1), 0].rearrange("o p d -> (o p) d"), y[:, 0]).then_inc(y_stored[0], 16)
                sp.wait_ge(turned, g * 6 + 6)
                load(g + 2)
                sp.wait_ge(y_done, g * 2 + 3)
                sp.dma_start(ys[bass.ds(g, 1), 1].rearrange("o p d -> (o p) d"), y[:, 1]).then_inc(y_stored[1], 16)

            each_step(sp, body)
            steps = sp.value_load(table[0:1, 2 * E - 1:2 * E], min_val=E - 1, max_val=MAXSTEPS - 1) \
                + sp.value_load(table[0:1, E - 1:E], min_val=1, max_val=KMAX)
            sp.wait_ge(x_loaded, steps * 16 + 32)
            sp.sem_inc(ended, 1)
            for i in range(2):
                sp.wait_ge(y_stored[i], steps * 16 + 16)
                sp.sem_inc(ended, 1)

        @block.gpsimd
        def _(pool):
            nc.gpsimd.memset(ones[:], 1.0).then_inc(const_set, 1)
            pool.wait_ge(const_set, 1)
            nc.gpsimd.affine_select(out=tri[:], in_=ones[:], compare_op=ALU.is_gt, fill=0.0, base=0,
                                    pattern=[[1, TQ]], channel_multiplier=-1).then_inc(tri_set, 1)
            pool.wait_ge(table_ready, 1)
            for n in range(NT):
                pool.wait_ge(rows_loaded[n % RING], 16 * (n // RING + 1))
                for j in range(2):
                    nc.gpsimd.indirect_dma_start(out=dram["slots"], out_offset=bass.IndirectOffsetOnAxis(ap=pos[:, j, n:n + 1], axis=0),
                                                 in_=rows[:, n % RING], in_offset=None).then_inc(scattered[n % RING], 16)

            def weights(e, buf):
                for c in range(PIECES):
                    if c < 2:
                        pool.dma_start(stage(c, c), piece_src(e, c)).then_inc(stage_loaded[c], 16)
                for c in range(PIECES):
                    pool.wait_ge(stage_loaded[c % 2], (e - 1) * (8 * PIECES) + 16 * (c // 2 + 1))
                    pool.sem_inc(passed, 1)
                    nc.gpsimd.tensor_scalar(piece_dst(buf, 0, c), raw[:, c % 2], 1.0, 1.0, ALU.mult, ALU.mult).then_inc(w_high, 1)
                    pool.wait_ge(w_high, (e - 1) * PIECES + (c + 1))
                    nc.gpsimd.tensor_tensor(piece_dst(buf, 1, c), raw[:, c % 2], piece_dst(buf, 0, c).bitcast(F32), ALU.subtract).then_inc(w_ready, 1)
                    if c + 2 < PIECES:
                        pool.wait_ge(w_ready, (e - 1) * PIECES + (c + 2))
                        pool.sem_inc(passed, 1)
                        pool.dma_start(stage(c % 2, c + 2), piece_src(e, c + 2)).then_inc(stage_loaded[c % 2], 16)

            pool.wait_ge(w0_ready, PIECES)
            pool.sem_inc(w_ready, 1)
            weights(1, 1)
            with pool.Fori(0, E // 2 - 1) as pair:
                for buf in range(2):
                    e = pair * 2 + (buf + 2)
                    steps = pool.value_load(table[0:1, bass.ds(e + (E - 1), 1)], min_val=1, max_val=MAXSTEPS - 1)
                    pool.wait_ge(y_ready, steps * 2)
                    pool.sem_inc(passed, 1)
                    pool.wait_ge(w_ready, (e - 1) * PIECES + 1)
                    pool.sem_inc(passed, 1)
                    weights(e, buf)

        @block.scalar
        def _(act):
            act.wait_ge(shifted_ready, 1)
            nc.scalar.activation(expo[:], shifted[:], ACT.Exp)
            nc.scalar.activation(second_e[:], second[:], ACT.Exp).then_inc(expo_ready, 1)
            for c in range(PIECES):
                act.wait_ge(raw_loaded[c % 2], 16 * (c // 2 + 1))
                nc.scalar.copy(piece_dst(0, 0, c), raw[:, c % 2]).then_inc(w0_high, 1)

            def high(no, dst, src):
                act.wait_ge(turned, no + 1)
                nc.scalar.copy(dst, src.rearrange("p (c t) -> p c t", t=SUB)).then_inc(turned_high, 1)

            def silu(g, s):
                act.wait_ge(hidden, g * 2 + (s + 1))
                nc.scalar.activation(act_sb[:, s], ps_h[s][:].rearrange("p j n -> p (j n)")[:, 0:F], ACT.Silu).then_inc(silu_done, 1)

            def out(g, s):
                act.wait_ge(y_ready, g * 2 + (s + 1))
                act.wait_ge(y_stored[s], g * 16 + 16)
                nc.scalar.copy(y[:, s], ps_y[:]).then_inc(y_done, 1)

            act.sem_inc(y_done, 1)
            for s in range(2):
                high(s, xT[:, s, 0], ps_t[:])

            def body(buf, g, e):
                no = g * 6 + 2
                silu(g, 0)
                high(no, hT[:, 0, 0, 0:3], ps_t[:, 0:3 * SUB])
                high(no + 1, hT[:, 0, 0, 3:6], ps_t[:, 0:3 * SUB])
                silu(g, 1)
                high(no + 2, xT[:, 0, 0], ps_t[:])
                high(no + 3, xT[:, 1, 0], ps_t[:])
                high(no + 4, hT[:, 1, 0, 0:3], ps_h[0][:, 0, 0:3 * SUB])
                high(no + 5, hT[:, 1, 0, 3:6], ps_h[0][:, 1, 0:3 * SUB])
                out(g, 0)
                out(g, 1)

            each_step(act, body)

        @block.vector
        def _(dve):
            done = [0]

            def step(ins):
                done[0] += 1
                ins.then_inc(routed, 1)
                dve.wait_ge(routed, done[0])

            def over_e(ap):
                return ap.rearrange("p (n o) -> p n o", o=1).to_broadcast((TQ, NT, E))

            for e in range(E):
                last = nc.vector.memset(iota[:, e:e + 1], float(e))
            for k in range(KMAX):
                last = nc.vector.memset(thr[:, k:k + 1], float(STEP * k))
            step(last)
            for n in range(NT):
                last = nc.vector.max(top[:, n], logits[:, n])
            step(last)
            for n in range(NT):
                last = nc.vector.max_index(idx[:, n], top[:, n], logits[:, n])
            step(last)
            step(nc.vector.tensor_tensor(second[:], top[:, :, 1], top[:, :, 0], ALU.subtract))
            nc.vector.tensor_tensor(shifted[:], logits[:], over_e(top[:, :, 0].rearrange("p n -> p n")), ALU.subtract).then_inc(shifted_ready, 1)
            step(nc.vector.tensor_copy(idxf[:], idx[:, :, 0:2]))
            for j in range(2):
                last = nc.vector.tensor_tensor(hot[:, j], iota[:].rearrange("p (o e) -> p o e", o=1).to_broadcast((TQ, NT, E)),
                                               over_e(idxf[:, :, j]), ALU.is_equal)
            step(last)
            nc.vector.tensor_tensor(both[:], hot[:, 0], hot[:, 1], ALU.add).then_inc(both_ready, 1)
            dve.wait_ge(expo_ready, 1)
            step(nc.vector.tensor_reduce(weight[:, 1], expo[:], AX.X, ALU.add))
            step(nc.vector.reciprocal(weight[:, 0], weight[:, 1]))
            step(nc.vector.tensor_tensor(weight[:, 1], weight[:, 0], second_e[:], ALU.mult))
            dve.wait_ge(ranked, 1)
            step(nc.vector.tensor_copy(count[:], ps_y[0:TQ, 0:NT * E].rearrange("p (n e) -> p n e", e=E)))
            step(nc.vector.tensor_reduce(total[:], count[:].rearrange("p n e -> p e n"), AX.X, ALU.add))
            step(nc.vector.tensor_tensor(over[:], total[:].rearrange("p (e o) -> p e o", o=1).to_broadcast((TQ, E, KMAX)),
                                         thr[:].rearrange("p (o k) -> p o k", o=1).to_broadcast((TQ, E, KMAX)), ALU.is_gt))
            step(nc.vector.tensor_reduce(nsteps[:], over[:], AX.X, ALU.add))
            step(nc.vector.tensor_scalar(nsteps[:], nsteps[:], 1.0, None, ALU.max))
            step(nc.vector.memset(before[:, 0:1], 0.0))
            for e in range(1, E):
                step(nc.vector.tensor_tensor(before[:, e:e + 1], before[:, e - 1:e], nsteps[:, e - 1:e], ALU.add))
            nc.vector.tensor_copy(table[0:1, 0:E], nsteps[0:1, :])
            nc.vector.tensor_copy(table[0:1, E:2 * E], before[0:1, :])
            step(nc.vector.tensor_scalar(start[:, 0], before[:], float(STEP), None, ALU.mult))
            for n in range(1, NT):
                step(nc.vector.tensor_tensor(start[:, n], start[:, n - 1], count[:, n - 1], ALU.add))
            step(nc.vector.tensor_tensor(slot[:], ps_t[0:TQ, 0:NT * E].rearrange("p (n e) -> p n e", e=E), start[:], ALU.add))
            for j in range(2):
                last = nc.vector.tensor_tensor(picked[:, j], hot[:, j], slot[:], ALU.mult)
            step(last)
            step(nc.vector.tensor_reduce(posf[:].rearrange("p j n -> p (j n)"), picked[:].rearrange("p j n e -> p (j n) e"), AX.X, ALU.add))
            nc.vector.tensor_copy(pos[:], posf[:]).then_inc(table_ready, 1)
            for c in range(PIECES):
                dve.wait_ge(w0_high, c + 1)
                nc.vector.tensor_tensor(piece_dst(0, 1, c), raw[:, c % 2], piece_dst(0, 0, c).bitcast(F32), ALU.subtract).then_inc(w0_ready, 1)

            def low(no, dst, high, src):
                dve.wait_ge(turned_high, no + 1)
                nc.vector.tensor_tensor(dst, src.rearrange("p (c t) -> p c t", t=SUB), high.bitcast(F32), ALU.subtract).then_inc(turned_done, 1)

            def glu(g, s):
                dve.wait_ge(silu_done, g * 2 + (s + 1))
                nc.vector.tensor_tensor(act_sb[:, s], ps_h[s][:].rearrange("p j n -> p (j n)")[:, F:2 * F], act_sb[:, s], ALU.mult).then_inc(glu_done, 1)

            for s in range(2):
                low(s, xT[:, s, 1], xT[:, s, 0], ps_t[:])

            def body(buf, g, e):
                no = g * 6 + 2
                glu(g, 0)
                low(no, hT[:, 0, 1, 0:3], hT[:, 0, 0, 0:3], ps_t[:, 0:3 * SUB])
                low(no + 1, hT[:, 0, 1, 3:6], hT[:, 0, 0, 3:6], ps_t[:, 0:3 * SUB])
                glu(g, 1)
                low(no + 2, xT[:, 0, 1], xT[:, 0, 0], ps_t[:])
                low(no + 3, xT[:, 1, 1], xT[:, 1, 0], ps_t[:])
                low(no + 4, hT[:, 1, 1, 0:3], hT[:, 1, 0, 0:3], ps_h[0][:, 0, 0:3 * SUB])
                low(no + 5, hT[:, 1, 1, 3:6], hT[:, 1, 0, 3:6], ps_h[0][:, 1, 0:3 * SUB])

            each_step(dve, body)

        @block.tensor
        def _(pe):
            passes = ((0, 0), (1, 0), (0, 1))
            pe.wait_ge(tri_set, 1)
            pe.wait_ge(both_ready, 1)
            flat = both[:].rearrange("p n e -> p (n e)")
            nc.tensor.matmul(ps_t[0:TQ, 0:NT * E], tri[:], flat, start=True, stop=True)
            nc.tensor.matmul(ps_y[0:TQ, 0:NT * E], ones[:], flat, start=True, stop=True).then_inc(ranked, 1)

            def turn(dst, src):
                n = src.shape[-1] // SUB
                for c in range(n):
                    mm = nc.tensor.transpose(dst[:, c * SUB:(c + 1) * SUB], src[:, c * SUB:(c + 1) * SUB], ident[:])
                mm.then_inc(turned, 1)

            def hidden_bank(buf, s, j):
                for n, (c, (a, m)) in enumerate((c, p) for c in range(XC) for p in passes):
                    mm = nc.tensor.matmul(ps_h[s][:, j], xT[:, s, a, c], W1[:, buf, m, c, j * 512:(j + 1) * 512], start=(n == 0), stop=(n == 3 * XC - 1))
                return mm

            def result(buf, s, half):
                for n, (c, (a, m)) in enumerate((c, p) for c in range(FC) for p in passes):
                    if n // (3 * FC // 2) == half:
                        mm = nc.tensor.matmul(ps_y[:], hT[:, s, a, c], W2[:, buf, m, c], start=(n == 0), stop=(n == 3 * FC - 1))
                if half == 1:
                    mm.then_inc(y_ready, 1)

            pe.wait_ge(table_ready, 1)
            pe.wait_ge(x_loaded, 16)
            turn(ps_t[:], xg[:, 0])
            pe.wait_ge(turned_done, 1)
            turn(ps_t[:], xg[:, 1])
            pe.wait_ge(turned_done, 2)

            def body(buf, g, e):
                no = g * 6 + 2
                pe.wait_ge(w_ready, e * PIECES + 1)
                for j in range(3):
                    mm = hidden_bank(buf, 0, j)
                mm.then_inc(hidden, 1)
                hidden_bank(buf, 1, 0)
                pe.wait_ge(glu_done, g * 2 + 1)
                turn(ps_t[:], act_sb[:, 0, 0:F // 2])
                hidden_bank(buf, 1, 1)
                pe.wait_ge(turned_done, no + 1)
                turn(ps_t[:], act_sb[:, 0, F // 2:F])
                hidden_bank(buf, 1, 2).then_inc(hidden, 1)
                pe.wait_ge(x_loaded, g * 16 + 32)
                pe.wait_ge(turned_done, no + 2)
                turn(ps_t[:], xg[:, 0])
                pe.wait_ge(y_done, g * 2 + 1)
                result(buf, 0, 0)
                pe.wait_ge(turned_done, no + 3)
                turn(ps_t[:], xg[:, 1])
                pe.wait_ge(glu_done, g * 2 + 2)
                turn(ps_h[0][:, 0], act_sb[:, 1, 0:F // 2])
                turn(ps_h[0][:, 1], act_sb[:, 1, F // 2:F])
                result(buf, 0, 1)
                pe.wait_ge(turned_done, no + 6)
                pe.wait_ge(y_done, g * 2 + 2)
                result(buf, 1, 0)
                result(buf, 1, 1)

            each_step(pe, body)


def combine(nc, dram, const):
    pos, weight = const["pos"], const["weight"]
    RING = 4
    with ExitStack() as ctx:
        def sb(name, shape, dt=F32):
            return ctx.enter_context(nc.sbuf_tensor(name, shape, dt))

        def sem(name):
            return ctx.enter_context(nc.semaphore(name))

        x2 = sb("x2_in", [TQ, NT, D])
        got = sb("got", [TQ, RING, 2, D])
        part = sb("part", [TQ, RING, D])
        x2_loaded = sem("x2_loaded")
        gathered = [sem(f"gathered{i}") for i in range(RING)]
        first_added = sem("first_added")
        added = sem("added")
        stored = sem("stored")
        block = ctx.enter_context(nc.Block())

        @block.sync
        def _(sp):
            sp.dma_start(x2[:].rearrange("p (b t) d -> p b t d", t=QT), dram["x2"].rearrange("b p t d -> p b t d")).then_inc(x2_loaded, 16)
            for n in range(NT):
                sp.wait_ge(added, n + 1)
                sp.dma_start(dram["out_pq"][n // QT, :, n % QT], x2[:, n]).then_inc(stored, 16)
            sp.wait_ge(stored, 16 * NT)

        @block.gpsimd
        def _(pool):
            for n in range(NT):
                if n >= RING:
                    pool.wait_ge(added, n - RING + 1)
                for j in range(2):
                    nc.gpsimd.indirect_dma_start(out=got[:, n % RING, j], out_offset=None, in_=dram["slots"],
                                                 in_offset=bass.IndirectOffsetOnAxis(ap=pos[:, j, n:n + 1], axis=0)).then_inc(gathered[n % RING], 16)

        @block.vector
        def _(dve):
            dve.wait_ge(x2_loaded, 16)
            for n in range(NT):
                dve.wait_ge(gathered[n % RING], 32 * (n // RING + 1))
                nc.vector.scalar_tensor_tensor(out=part[:, n % RING], in0=got[:, n % RING, 0], scalar=weight[:, 0, n:n + 1], in1=x2[:, n],
                                               op0=ALU.mult, op1=ALU.add).then_inc(first_added, 1)
                dve.wait_ge(first_added, n + 1)
                nc.vector.scalar_tensor_tensor(out=x2[:, n], in0=got[:, n % RING, 1], scalar=weight[:, 1, n:n + 1], in1=part[:, n % RING],
                                               op0=ALU.mult, op1=ALU.add).then_inc(added, 1)


def block_kernel(nc, x, ctx_768, Wq, Wk, Wv, Wo, bo, q_down, q_up, q_alpha, k_down, k_up, k_alpha, v_down, v_up,
                 v_alpha, o_down, o_up, o_alpha, Wk_ipa, Wv_ipa, w_gate, c_fc, c_proj, out):
    dram = dict(x=x, ctx=ctx_768, Wq=Wq, Wk=Wk, Wv=Wv, Wo=Wo, bo=bo, q_down=q_down, q_up=q_up, q_alpha=q_alpha,
                k_down=k_down, k_up=k_up, k_alpha=k_alpha, v_down=v_down, v_up=v_up, v_alpha=v_alpha,
                o_down=o_down, o_up=o_up, o_alpha=o_alpha, Wk_ipa=Wk_ipa, Wv_ipa=Wv_ipa,
                w_gate=w_gate, c_fc=c_fc, c_proj=c_proj,
                x_pq=x.rearrange("b (t p) d -> b p t d", p=TQ), out_pq=out.rearrange("b (t p) d -> b p t d", p=TQ))
    for name, shape in (("vipa", [B * IPA, HEADS * 2 * DH]), ("oT", [ID, B, N]), ("x2", [B, TQ, QT, D]), ("xn2", [B, TQ, QT, D]),
                        ("slots", [ROOM * STEP, D])):
        dram[name] = nc.dram_tensor(f"{name}_scratch", shape, F32).ap()
    with ExitStack() as ctx:
        const = {}

        def sb(stack, name, shape, dt=F32):
            const[name] = stack.enter_context(nc.sbuf_tensor(name, shape, dt))

        sb(ctx, "ident", [P, P])
        sb(ctx, "logits", [TQ, NT, E])
        sb(ctx, "pos", [TQ, 2, NT], U32)
        sb(ctx, "weight", [TQ, 2, NT])
        with ExitStack() as inner:
            sb(inner, "kipa", [P, PAIRS, 2, B * IPA], F32R)
            sb(inner, "rstd", [TQ, NT])
            sb(inner, "mean", [TQ, NT])
            for k, n in (("q", XC), ("k", CC), ("v", CC)):
                for part in "hl":
                    sb(inner, f"w{k}_{part}", [P, n, ID], F32R)
            prepare(nc, dram, const)
            attend(nc, dram, const)
        project(nc, dram, const)
        experts(nc, dram, const)
        combine(nc, dram, const)


_INS = ["x", "ctx_768"] + [f"L0_xattn_{n}" for n in (
    "Wq", "Wk", "Wv", "Wo", "bo", "q_down", "q_up", "q_alpha", "k_down", "k_up", "k_alpha", "v_down", "v_up", "v_alpha",
    "o_down", "o_up", "o_alpha", "Wk_ipa", "Wv_ipa")] + [f"L0_ffn_{n}" for n in ("w_gate", "c_fc", "c_proj")]


def kernel(**inputs):
    import concourse.bacc as bacc
    from concourse.bass_utils import run_bass_kernel_spmd

    nc = bacc.Bacc("TRN2", target_bir_lowering=False, num_devices=1)
    arrays, args = {}, []
    for name in _INS:
        a = np.ascontiguousarray(inputs[name])
        arrays[f"in_{name}"] = a
        args.append(nc.dram_tensor(f"in_{name}", a.shape, mybir.dt.from_np(a.dtype), kind="ExternalInput").ap())
    args.append(nc.dram_tensor("out_0", (B, N, D), F32, kind="ExternalOutput").ap())
    block_kernel(nc, *args)
    r = run_bass_kernel_spmd(nc, [arrays], core_ids=[0])
    return r.results[0]["out_0"]
```

```python
from contextlib import ExitStack

import numpy as np

import concourse.bass as bass
from concourse import mybir

F32 = mybir.dt.float32
F32R = mybir.dt.float32r
I32 = mybir.dt.int32
U32 = mybir.dt.uint32
ALU = mybir.AluOpType
ACT = mybir.ActivationFunctionType
AX = mybir.AxisListType

B, N, D = 8, 224, 512
CTX, CD = 750, 384
IPA = 4
HEADS, DH = 16, 64
ID = HEADS * DH
RANK = 32
SCALE = DH ** -0.5
EPS = 1e-5
P = 128
QT, TQ = 2, 112
NT = B * QT
PAIRS = HEADS // 2
XC, CC = D // P, CD // P
KH, KHP = CTX // 2, CTX // 2 + 1
ORG = KH - 2
KC, KCN = 125, 6
VG, VH = 4, 4
E, F = 8, 768
FC = F // P
GROUPS = 8 + 3 * PAIRS + KCN * VG
SUB = 128
STEP = 2 * SUB
TOKENS = B * N
MAXSTEPS = (2 * TOKENS + E * (STEP - 1)) // STEP
KMAX = -(-TOKENS // STEP)
ROOM = MAXSTEPS + KMAX + 1


def prepare(nc, dram, const):
    wq_h, wq_l, wk_h, wk_l, wv_h, wv_l, ident, kipa, rstd, mean = (
        const[k] for k in ("wq_h", "wq_l", "wk_h", "wk_l", "wv_h", "wv_l", "ident", "kipa", "rstd", "mean"))
    with ExitStack() as ctx:
        def sb(name, shape, dt=F32):
            return ctx.enter_context(nc.sbuf_tensor(name, shape, dt))

        def sem(name):
            return ctx.enter_context(nc.semaphore(name))

        raw = {"q": sb("wq_raw", [P, XC, ID]), "k": sb("wk_raw", [P, CC, ID]), "v": sb("wv_raw", [P, CC, ID])}
        split = {"q": (wq_h, wq_l), "k": (wk_h, wk_l), "v": (wv_h, wv_l)}
        down = sb("down", [P, XC + 2 * CC, RANK])
        up = sb("up", [RANK, 3, ID])
        alpha = sb("alpha", [P, 3])
        alpha_r = sb("alpha_r", [P, 3])
        downT = sb("downT", [RANK, XC + 2 * CC, P])
        wki = sb("wk_ipa", [P, CC, ID])
        wvi = sb("wv_ipa", [P, CC, ID])
        ictx = sb("ipa_ctx", [B * IPA, CD])
        ictxT = sb("ipa_ctxT", [P, CC, B * IPA])
        vipa_h = sb("vipa_h", [B * IPA, HEADS, DH], F32R)
        vipa = sb("vipa", [B * IPA, HEADS, 2 * DH])
        xb = sb("x_stat", [TQ, 2, QT, D])
        bn = sb("bn", [TQ, NT, 6])
        mv = sb("mv", [TQ, NT, 2])
        eps = sb("eps", [TQ, 1])
        std = sb("std", [TQ, NT])
        ones = sb("ones_sq", [P, P])
        ps_down = ctx.enter_context(nc.psum_tensor("ps_down", [RANK, 12, P], F32))
        ps_w = ctx.enter_context(nc.psum_tensor("ps_w", [P, 2, 512], F32))
        ps_i = ctx.enter_context(nc.psum_tensor("ps_i", [P, 512], F32))
        ps_v = ctx.enter_context(nc.psum_tensor("ps_v", [B * IPA, 2, 512], F32))

        small_loaded = sem("small_loaded")
        w_loaded = {k: sem(f"w{k}_loaded") for k in "qkv"}
        ipa_loaded = sem("ipa_loaded")
        x_loaded = [sem(f"xstat{i}_loaded") for i in range(2)]
        stats_done = sem("stats_done")
        ident_done = sem("ident_done")
        down_turned = sem("down_turned")
        down_copied = sem("down_copied")
        lora_done = sem("lora_done")
        eff_done = sem("eff_done")
        high_done = sem("high_done")
        low_done = sem("low_done")
        ictx_turned = sem("ictx_turned")
        ictx_copied = sem("ictx_copied")
        kipa_done = sem("kipa_done")
        vipa_done = sem("vipa_done")
        kipa_h = sem("kipa_h_done")
        vipa_hd = sem("vipa_h_done")
        vipa_stored = sem("vipa_stored")
        aggr_done = sem("aggr_done")
        std_done = sem("std_done")
        prep_done = sem("prep_done")
        bn_done = sem("bn_done")
        pieces = [("k", c, n, XC + c, 1.0, 1) for c in range(CC) for n in range(2)]
        pieces += [("q", c, n, c, SCALE, 0) for c in range(XC) for n in range(2)]
        pieces += [("v", c, n, XC + CC + c, 1.0, 2) for c in range(CC) for n in range(2)]
        block = ctx.enter_context(nc.Block())

        @block.sync
        def _(sp):
            for i, (k, c0, n) in enumerate((("q", 0, XC), ("k", XC, CC), ("v", XC + CC, CC))):
                sp.dma_start(down[:, c0:c0 + n, :], dram[f"{k}_down"].rearrange("(c p) r -> p c r", p=P)).then_inc(small_loaded, 16)
                sp.dma_start(up[:, i, :], dram[f"{k}_up"]).then_inc(small_loaded, 16)
                sp.dma_start(alpha[:, i:i + 1], dram[f"{k}_alpha"].rearrange("(a o) -> a o", o=1).to_broadcast((P, 1))).then_inc(small_loaded, 16)
            for k in "kqv":
                sp.dma_start(raw[k][:], dram[f"W{k}"].rearrange("(c p) n -> p c n", p=P)).then_inc(w_loaded[k], 16)
            for b in range(B):
                sp.dma_start(ictx[b * IPA:(b + 1) * IPA, :], dram["ctx"][b, CTX - IPA:CTX, :]).then_inc(ipa_loaded, 16)
            sp.dma_start(wki[:], dram["Wk_ipa"].rearrange("(c p) n -> p c n", p=P)).then_inc(ipa_loaded, 16)
            sp.dma_start(wvi[:], dram["Wv_ipa"].rearrange("(c p) n -> p c n", p=P)).then_inc(ipa_loaded, 16)
            sp.wait_ge(prep_done, 3)
            sp.dma_start(dram["vipa"], vipa[:].rearrange("p h d -> p (h d)")).then_inc(vipa_stored, 16)
            sp.wait_ge(vipa_stored, 16)

        @block.gpsimd
        def _(pool):
            nc.gpsimd.memset(ones[:], 1.0).then_inc(ident_done, 1)
            pool.wait_ge(ident_done, 1)
            nc.gpsimd.affine_select(out=ident[:], in_=ones[:], compare_op=ALU.is_equal, fill=0.0, base=0,
                                    pattern=[[-1, P]], channel_multiplier=1).then_inc(ident_done, 1)

        @block.scalar
        def _(act):
            for i in range(2):
                act.dma_start(xb[:, i], dram["x_pq"][i]).then_inc(x_loaded[i], 16)
            with act.Fori(0, B // 2 - 1) as two:
                for i in range(2):
                    act.wait_ge(bn_done, two * (2 * QT) + QT * (i + 1))
                    act.dma_start(xb[:, i], dram["x_pq"][bass.ds(two * 2 + (2 + i), 1)].rearrange("o p t d -> (o p) t d")).then_inc(x_loaded[i], 16)
            act.wait_ge(down_turned, 1)
            nc.scalar.copy(downT[:], ps_down[:, 0:XC + 2 * CC, :]).then_inc(down_copied, 1)
            for i, (k, c, n, _, s, _) in enumerate(pieces):
                act.wait_ge(eff_done, i + 1)
                nc.scalar.activation(split[k][0][:, c, n * 512:n * 512 + 512], raw[k][:, c, n * 512:n * 512 + 512],
                                     ACT.Copy, scale=s).then_inc(high_done, 1)
            act.wait_ge(kipa_done, 1)
            nc.scalar.copy(kipa[:, :, 0, :], ps_i[:, 0:PAIRS * B * IPA].rearrange("p (s j) -> p s j", s=PAIRS)).then_inc(kipa_h, 1)
            act.wait_ge(vipa_done, 1)
            nc.scalar.copy(vipa_h[:], ps_v[:].rearrange("p n (h d) -> p (n h) d", d=DH)).then_inc(vipa_hd, 1)
            act.wait_ge(aggr_done, NT + 1)
            nc.scalar.activation(std[:], mv[:, :, 1], ACT.Sqrt, bias=eps[:, 0:1]).then_inc(std_done, 1)

        @block.vector
        def _(dve):
            nc.vector.memset(eps[:], EPS).then_inc(aggr_done, 1)
            with dve.Fori(0, B // 2) as two:
                b = two * 2
                for i in range(2):
                    dve.wait_ge(x_loaded[i], b * 8 + 16)
                    for q in range(QT):
                        nc.vector.bn_stats(bn[:, bass.ds(b * QT + (i * QT + q), 1), :].rearrange("p o s -> p (o s)"), xb[:, i, q, :]).then_inc(bn_done, 1)
            dve.wait_ge(bn_done, NT)
            for n in range(NT):
                nc.vector.bn_aggr(mv[:, n, :], bn[:, n, :]).then_inc(aggr_done, 1)
            dve.wait_ge(small_loaded, 9 * 16)
            nc.vector.tensor_scalar(alpha_r[:], alpha[:], 1.0 / RANK, None, ALU.mult).then_inc(stats_done, 1)
            dve.wait_ge(stats_done, 1)
            for i, (k, c, n, _, s, j) in enumerate(pieces):
                w = raw[k][:, c, n * 512:n * 512 + 512]
                if i in (0, 6, 14):
                    dve.wait_ge(w_loaded[k], 16)
                dve.wait_ge(lora_done, i + 1)
                nc.vector.scalar_tensor_tensor(out=w, in0=ps_w[:, i % 2, :], scalar=alpha_r[:, j:j + 1], in1=w,
                                               op0=ALU.mult, op1=ALU.add).then_inc(eff_done, 1)
                dve.wait_ge(high_done, i + 1)
                nc.vector.scalar_tensor_tensor(out=split[k][1][:, c, n * 512:n * 512 + 512], in0=w, scalar=s,
                                               in1=split[k][0][:, c, n * 512:n * 512 + 512].bitcast(F32),
                                               op0=ALU.mult, op1=ALU.subtract).then_inc(low_done, 1)
            dve.wait_ge(ictx_turned, 1)
            nc.vector.tensor_copy(ictxT[:], ps_i[:, 0:CC * B * IPA].rearrange("p (c j) -> p c j", c=CC)).then_inc(ictx_copied, 1)
            dve.wait_ge(kipa_h, 1)
            nc.vector.tensor_tensor(kipa[:, :, 1, :], ps_i[:, 0:PAIRS * B * IPA].rearrange("p (s j) -> p s j", s=PAIRS),
                                    kipa[:, :, 0, :].bitcast(F32), ALU.subtract).then_inc(prep_done, 1)
            dve.wait_ge(vipa_hd, 1)
            nc.vector.tensor_copy(vipa[:, :, 0:DH], vipa_h[:].bitcast(F32)).then_inc(prep_done, 1)
            nc.vector.tensor_tensor(vipa[:, :, DH:2 * DH], ps_v[:].rearrange("p n (h d) -> p (n h) d", d=DH),
                                    vipa_h[:].bitcast(F32), ALU.subtract).then_inc(prep_done, 1)
            dve.wait_ge(aggr_done, NT + 1)
            nc.vector.tensor_copy(mean[:], mv[:, :, 0]).then_inc(prep_done, 1)
            dve.wait_ge(std_done, 1)
            nc.vector.reciprocal(rstd[:], std[:]).then_inc(prep_done, 1)

        @block.tensor
        def _(pe):
            pe.wait_ge(ident_done, 2)
            pe.wait_ge(small_loaded, 9 * 16)
            for c in range(XC + 2 * CC):
                mm = nc.tensor.transpose(ps_down[:, c, :], down[:, c, :], ident[:])
            mm.then_inc(down_turned, 1)
            pe.wait_ge(down_copied, 1)
            for i, (k, c, n, dc, _, j) in enumerate(pieces):
                if i >= 2:
                    pe.wait_ge(eff_done, i - 1)
                nc.tensor.matmul(ps_w[:, i % 2, :], downT[:, dc, :], up[:, j, n * 512:n * 512 + 512],
                                 start=True, stop=True).then_inc(lora_done, 1)
            pe.wait_ge(ipa_loaded, (B + 2) * 16)
            for c in range(CC):
                mm = nc.tensor.transpose(ps_i[:, c * B * IPA:(c + 1) * B * IPA], ictx[:, c * P:(c + 1) * P], ident[0:B * IPA, 0:B * IPA])
            mm.then_inc(ictx_turned, 1)
            pe.wait_ge(ictx_copied, 1)
            for s in range(PAIRS):
                for c in range(CC):
                    mm = nc.tensor.matmul(ps_i[:, s * B * IPA:(s + 1) * B * IPA], wki[:, c, s * P:(s + 1) * P], ictxT[:, c, :],
                                          start=(c == 0), stop=(c == CC - 1))
            mm.then_inc(kipa_done, 1)
            for n in range(2):
                for c in range(CC):
                    mm = nc.tensor.matmul(ps_v[:, n, :], ictxT[:, c, :], wvi[:, c, n * 512:n * 512 + 512],
                                          start=(c == 0), stop=(c == CC - 1))
            mm.then_inc(vipa_done, 1)


def batch_schedule():
    prep = [("ctx", c) for c in range(KCN)] + [("x", q) for q in range(QT)]
    pair = lambda s: [("k", s, 0), ("k", s, 1), ("q", s)]
    values = lambda g: [("v", g, c) for c in range(KCN)]
    own = prep + pair(0) + values(0) + pair(1)[:1]
    prologue = list(enumerate(own))
    rest = pair(1)[1:]
    for s in range(2, PAIRS):
        rest += values(s // 2)[(s % 2) * 3:(s % 2) * 3 + 3] + pair(s)
    rest = list(enumerate(rest, len(own)))
    assert len(own) + len(rest) == GROUPS
    per_head = [rest[3 * k:3 * k + 3] for k in range(HEADS)]
    after = {13: prologue[:8], 14: prologue[8:13], 15: prologue[13:]}
    return prologue, per_head, after


def attend(nc, dram, const):
    wq_h, wq_l, wk_h, wk_l, wv_h, wv_l, ident, kipa, rstd, mean = (
        const[k] for k in ("wq_h", "wq_l", "wk_h", "wk_l", "wv_h", "wv_l", "ident", "kipa", "rstd", "mean"))
    with ExitStack() as ctx:
        def sb(name, shape, dt=F32):
            return ctx.enter_context(nc.sbuf_tensor(name, shape, dt))

        def psum(name, shape):
            return ctx.enter_context(nc.psum_tensor(name, shape, F32))

        def sem(name):
            return ctx.enter_context(nc.semaphore(name))

        x_raw = sb("x_raw", [TQ, QT, D])
        xT = [sb(f"xT_{p}", [P, XC, N], F32R) for p in "hl"]
        ctx_raw = sb("ctx_raw", [KC, KCN, CD])
        ctxT = [sb(f"ctxT_{p}", [P, CC, 2, KHP], F32R) for p in "hl"]
        K = sb("K", [P, 2, 2, 2, KHP], F32R)
        Q = sb("Q", [P, 2, 2, 2, N], F32R)
        V = sb("V", [KC, 2, KCN, VH, 2 * DH], F32R)
        vipa = sb("vipa_rows", [2, 2, VH * 2 * DH])
        prob = sb("prob", [TQ, 2, QT, 2, KHP])
        pT = [sb(f"pT_{p}", [KC, 2, KCN, N], F32R) for p in "hl"]
        nmax = sb("nmax", [TQ, 2, QT, 2])
        sums = sb("sums", [TQ, 2, QT, 2])
        rsum = sb("rsum", [TQ, 2, QT, 2])
        one = sb("one", [2, 1])
        zero = sb("zero", [P, D // 2])
        low_o = sb("low_o", [DH, 2, N])
        oT = sb("oT", [P, 2, N])
        ps_s = psum("ps_s", [TQ, QT, 2, 512])
        ps_t = psum("ps_t", [P, 512])
        ps_o = psum("ps_o", [P, 512])
        banks = psum("ps_g", [P, 2, 512])

        x_loaded = sem("x_loaded")
        ctx_loaded = sem("ctx_loaded")
        x_normed = sem("x_normed")
        vipa_loaded = sem("vipa_loaded")
        vipa_used = sem("vipa_used")
        zeroed = sem("zeroed")
        cleared = sem("cleared")
        group_ready = sem("group_ready")
        group_high = sem("group_high")
        group_done = sem("group_done")
        kipa_ready = sem("kipa_ready")
        scores_ready = sem("scores_ready")
        max_ready = sem("max_ready")
        exp_done = sem("exp_done")
        rsum_ready = sem("rsum_ready")
        prob_ready = sem("prob_ready")
        turned = sem("turned")
        turned_high = sem("turned_high")
        turned_done = sem("turned_done")
        out_ready = sem("out_ready")
        out_low = sem("out_low")
        out_done = sem("out_done")
        out_stored = [sem(f"out_stored{i}") for i in range(2)]

        prologue, per_head, after = batch_schedule()
        block = ctx.enter_context(nc.Block())

        def group_no(b, n, ahead):
            return b * GROUPS + (n + GROUPS * ahead)

        def scores_unit(b, k, q):
            return b * HEADS * QT + (k * QT + q)

        def iteration(b, k, last):
            todo, ahead = (per_head[k], 0) if per_head[k] else (after[k], 1)
            return ([] if last and ahead else todo), ahead, (k + 1 < HEADS or not last), ((b, k + 1) if k + 1 < HEADS else (b + 1, 0))

        def places(todo):
            sizes = {0: (0, 0, 0, 0, 0, 0), 2: (0, 0, 1, 0, 1, 0), 3: (0, 0, 1, 0, 1, 1), 5: (0, 0, 2, 0, 1, 2), 8: (1, 1, 1, 1, 2, 2)}[len(todo)]
            return [todo[sum(sizes[:i]):sum(sizes[:i + 1])] for i in range(6)]

        def each_batch(engine, first, body):
            first()
            with engine.Fori(0, B - 1) as b:
                body(b, False)
            body(B - 1, True)

        @block.sync
        def _(sp):
            def load_ctx(b):
                src = dram["ctx"][b] if isinstance(b, int) else dram["ctx"][bass.ds(b, 1)].rearrange("o k d -> (o k) d")
                for h in range(2):
                    t0 = h * ORG
                    c0 = 3 * h
                    sp.dma_start(ctx_raw[0:2, c0, :], src[CTX - IPA + 2 * h:CTX - IPA + 2 * h + 2, :]).then_inc(ctx_loaded, 16)
                    sp.dma_start(ctx_raw[2:KC, c0, :], src[t0:t0 + KC - 2, :]).then_inc(ctx_loaded, 16)
                    sp.dma_start(ctx_raw[:, c0 + 1:c0 + 3, :],
                                 src[t0 + KC - 2:t0 + ORG, :].rearrange("(c p) d -> p c d", p=KC)).then_inc(ctx_loaded, 16)

            def load_x(b):
                src = dram["x_pq"][b] if isinstance(b, int) else dram["x_pq"][bass.ds(b, 1)].rearrange("o p t d -> (o p) t d")
                sp.dma_start(x_raw[:], src).then_inc(x_loaded, 16)

            def load_vipa(b, g):
                src = dram["vipa"].rearrange("(b h j) n -> b j h n", h=2, j=2)
                src = src[b] if isinstance(b, int) else src[bass.ds(b, 1)].rearrange("o j h n -> (o j) h n")
                sp.dma_start(vipa[:], src[:, :, g * VH * 2 * DH:(g + 1) * VH * 2 * DH]).then_inc(vipa_loaded, 16)

            def store(b, s):
                sp.wait_ge(out_done, b * HEADS + (2 * s + 3))
                dst = dram["oT"][s * P:(s + 1) * P]
                dst = dst[:, b, :] if isinstance(b, int) else dst[:, bass.ds(b, 1), :].rearrange("p o n -> p (o n)")
                sp.dma_start(dst, oT[:, s % 2, :]).then_inc(out_stored[s % 2], 16)

            def first():
                for i in range(2):
                    sp.sem_inc(out_stored[i], 16)
                load_ctx(0)
                load_x(0)
                load_vipa(0, 0)
                sp.wait_ge(cleared, 5)
                slots = dram["slots"].rearrange("(p s) (h d) -> p (s h) d", p=P, h=2)
                sp.dma_start(slots, zero[:].rearrange("p (o d) -> p o d", o=1).to_broadcast((P, ROOM * STEP // P * 2, D // 2))).then_inc(zeroed, 16)

            def body(b, last):
                for s in range(PAIRS):
                    if s in (0, 2, 4):
                        g = s // 2 + 1
                        sp.wait_ge(vipa_used, b * VG + g)
                        load_vipa(b, g)
                    if s == 1 and not last:
                        sp.wait_ge(group_ready, group_no(b, KCN + QT, 0))
                        load_ctx(b + 1)
                        load_x(b + 1)
                    if s == 6 and not last:
                        sp.wait_ge(vipa_used, b * VG + VG)
                        load_vipa(b + 1, 0)
                    store(b, s)

            each_batch(sp, first, body)
            for i in range(2):
                sp.wait_ge(out_stored[i], 16 * B * PAIRS // 2 + 16)
            sp.wait_ge(zeroed, 16)

        @block.gpsimd
        def _(pool):
            nc.gpsimd.memset(Q[:].bitcast(F32), 0.0).then_inc(cleared, 1)
            nc.gpsimd.memset(one[:], 1.0).then_inc(cleared, 1)
            nc.gpsimd.memset(zero[:], 0.0).then_inc(cleared, 1)
            for p in range(2):
                nc.gpsimd.memset(ctxT[p][:, :, :, KH:KHP].bitcast(F32), 0.0).then_inc(cleared, 1)

            def kipa_columns(b, n, s, ahead):
                pool.wait_ge(group_ready, group_no(b, n + 1, ahead))
                j0 = b * IPA + ahead * IPA
                src = kipa[:, s, :, bass.ds(j0, IPA)] if not isinstance(j0, int) else kipa[:, s, :, j0:j0 + IPA]
                nc.gpsimd.tensor_copy(K[:, s % 2, :, :, 0:2],
                                      src.bitcast(F32).rearrange("p l (h j) -> p l h j", h=2)).then_inc(kipa_ready, 1)

            def vipa_rows(b, n, g, ahead):
                pool.wait_ge(group_done, group_no(b, n + 1, ahead))
                pool.wait_ge(vipa_loaded, 16 * (b * VG + (g + ahead * VG + 1)))
                nc.gpsimd.tensor_tensor(V[0:2, g % 2, 0:4:3].rearrange("p c h d -> p c (h d)"), vipa[:],
                                        one[:].rearrange("p (o u) -> p o u", o=1).to_broadcast((2, 2, VH * 2 * DH)), ALU.mult).then_inc(vipa_used, 1)

            def normalise(b, k, q):
                pool.wait_ge(rsum_ready, scores_unit(b, k, q) + 1)
                p = prob[:, k % 2, q]
                nc.gpsimd.tensor_tensor(p[:, :, 0:2], p[:, :, 0:2], rsum[:, k % 2, q, 1:2].rearrange("p (o u) -> p o u", o=1).to_broadcast((TQ, 2, 2)), ALU.mult)
                nc.gpsimd.tensor_scalar(p[:, :, 2:KH], p[:, :, 2:KH], rsum[:, k % 2, q, 0:1], 1.0, ALU.mult, ALU.mult).then_inc(prob_ready, 1)

            def keys(b, todo, ahead):
                for n, what in todo:
                    if what[0] == "k" and what[2] == 0:
                        kipa_columns(b, n, what[1], ahead)

            def value_rows(b, todo, ahead):
                for n, what in todo:
                    if what[0] == "v" and what[2] == KCN - 1:
                        vipa_rows(b, n, what[1], ahead)

            def first():
                pool.wait_ge(cleared, 5)
                keys(0, prologue, 0)
                value_rows(0, prologue, 0)
                for q in range(QT):
                    normalise(0, 0, q)

            def body(b, last):
                for k in range(HEADS):
                    todo, ahead, more, nxt = iteration(b, k, last)
                    if more:
                        for q in range(QT):
                            normalise(*nxt, q)
                    value_rows(b, todo, ahead)
                    keys(b, todo, ahead)

            each_batch(pool, first, body)

        @block.scalar
        def _(act):
            def high(b, todo, ahead):
                for n, what in todo:
                    ps_g = banks[:, n % 2]
                    act.wait_ge(group_ready, group_no(b, n + 1, ahead))
                    if what[0] == "ctx":
                        c = what[1]
                        last = nc.scalar.copy(ctxT[0][:, :, c // 3, c % 3 * KC:(c % 3 + 1) * KC], ps_g[:, 0:CC * KC].rearrange("p (c k) -> p c k", c=CC))
                    elif what[0] == "x":
                        q = what[1]
                        last = nc.scalar.copy(xT[0][:, :, q * TQ:(q + 1) * TQ], ps_g[:, 0:XC * TQ].rearrange("p (c k) -> p c k", c=XC))
                    elif what[0] == "k":
                        s, h = what[1:]
                        last = nc.scalar.copy(K[:, s % 2, 0, h, 2:KHP], ps_g[:, 2:KHP])
                    elif what[0] == "q":
                        s = what[1]
                        nc.scalar.copy(Q[0:DH, s % 2, 0, 0, :], ps_g[0:DH, 0:N])
                        last = nc.scalar.copy(Q[DH:P, s % 2, 0, 1, :], ps_g[DH:P, 0:N])
                    else:
                        g, c = what[1:]
                        last = nc.scalar.copy(V[:, g % 2, c, :, 0:DH], ps_g[0:KC, 0:VH * DH].rearrange("p (h d) -> p h d", d=DH))
                    last.then_inc(group_high, 1)

            def exponentials(b, k, q):
                act.wait_ge(max_ready, scores_unit(b, k, q) + 1)
                for i, (a, e) in enumerate(((2, KH), (0, 2))):
                    last = nc.scalar.activation(prob[:, k % 2, q, :, a:e], ps_s[:, q, :, a:e], ACT.Exp,
                                                bias=nmax[:, k % 2, q, i:i + 1], accum_out=sums[:, k % 2, q, i:i + 1])
                last.then_inc(exp_done, 1)

            def out_part(b, k):
                act.wait_ge(out_ready, b * HEADS + (k + 1))
                nc.scalar.copy(low_o[:, k % 2, :], ps_o[DH:P, 0:N]).then_inc(out_low, 1)

            def turned_part(b, k, j):
                act.wait_ge(turned, b * HEADS * 3 + (k * 3 + j + 1))
                nc.scalar.copy(pT[0][:, k % 2, 2 * j:2 * j + 2, :].rearrange("p c n -> p (c n)"), ps_t[0:KC, 0:2 * N]).then_inc(turned_high, 1)

            def first():
                act.wait_ge(cleared, 5)
                high(0, prologue, 0)
                exponentials(0, 0, 0)
                exponentials(0, 0, 1)

            def body(b, last):
                for k in range(HEADS):
                    todo, ahead, more, nxt = iteration(b, k, last)
                    at = places(todo)
                    turned_part(b, k, 0)
                    high(b, at[0] + at[1], ahead)
                    if more:
                        exponentials(*nxt, 0)
                    turned_part(b, k, 1)
                    if more:
                        exponentials(*nxt, 1)
                    high(b, at[2], ahead)
                    if k > 0:
                        out_part(b, k - 1)
                    high(b, at[3], ahead)
                    turned_part(b, k, 2)
                    high(b, at[4] + at[5], ahead)
                out_part(b, HEADS - 1)

            each_batch(act, first, body)

        @block.vector
        def _(dve):
            def norm_x(b):
                dve.wait_ge(x_loaded, 16 * b + 16)
                for q in range(QT):
                    i = b * QT + q
                    m = mean[:, i:i + 1] if isinstance(i, int) else mean[:, bass.ds(i, 1)]
                    r = rstd[:, i:i + 1] if isinstance(i, int) else rstd[:, bass.ds(i, 1)]
                    last = nc.vector.tensor_scalar(x_raw[:, q, :], x_raw[:, q, :], m, r, ALU.subtract, ALU.mult)
                last.then_inc(x_normed, 1)

            def low(b, todo, ahead):
                for n, what in todo:
                    ps_g = banks[:, n % 2]
                    dve.wait_ge(group_high, group_no(b, n + 1, ahead))
                    if what[0] == "ctx":
                        c = what[1]
                        at = (slice(None), slice(None), c // 3, slice(c % 3 * KC, (c % 3 + 1) * KC))
                        last = nc.vector.tensor_tensor(ctxT[1][at], ps_g[:, 0:CC * KC].rearrange("p (c k) -> p c k", c=CC), ctxT[0][at].bitcast(F32), ALU.subtract)
                    elif what[0] == "x":
                        q = what[1]
                        last = nc.vector.tensor_tensor(xT[1][:, :, q * TQ:(q + 1) * TQ], ps_g[:, 0:XC * TQ].rearrange("p (c k) -> p c k", c=XC),
                                                       xT[0][:, :, q * TQ:(q + 1) * TQ].bitcast(F32), ALU.subtract)
                    elif what[0] == "k":
                        s, h = what[1:]
                        last = nc.vector.tensor_tensor(K[:, s % 2, 1, h, 2:KHP], ps_g[:, 2:KHP], K[:, s % 2, 0, h, 2:KHP].bitcast(F32), ALU.subtract)
                    elif what[0] == "q":
                        s = what[1]
                        for i, r in enumerate((slice(0, DH), slice(DH, P))):
                            last = nc.vector.tensor_tensor(Q[r, s % 2, 1, i, :], ps_g[r, 0:N], Q[r, s % 2, 0, i, :].bitcast(F32), ALU.subtract)
                    else:
                        g, c = what[1:]
                        last = nc.vector.tensor_tensor(V[:, g % 2, c, :, DH:2 * DH], ps_g[0:KC, 0:VH * DH].rearrange("p (h d) -> p h d", d=DH),
                                                       V[:, g % 2, c, :, 0:DH].bitcast(F32), ALU.subtract)
                    last.then_inc(group_done, 1)

            def maxima(b, k, q):
                dve.wait_ge(scores_ready, scores_unit(b, k, q) + 1)
                for i, (a, e) in enumerate(((2, KH), (0, 2))):
                    last = nc.vector.tensor_reduce(nmax[:, k % 2, q, i:i + 1], ps_s[:, q, :, a:e], AX.XY, ALU.max, negate=True)
                last.then_inc(max_ready, 1)

            def reciprocals(b, k, q):
                dve.wait_ge(exp_done, scores_unit(b, k, q) + 1)
                nc.vector.reciprocal(rsum[:, k % 2, q], sums[:, k % 2, q]).then_inc(rsum_ready, 1)

            def out_part(b, k):
                s = k // 2
                if k % 2 == 0:
                    dve.wait_ge(out_stored[s % 2], b * (16 * PAIRS // 2) + 16 * (s // 2 + 1))
                dve.wait_ge(out_low, b * HEADS + (k + 1))
                nc.vector.tensor_tensor(oT[k % 2 * DH:(k % 2 + 1) * DH, s % 2, :], ps_o[0:DH, 0:N], low_o[:, k % 2, :], ALU.add).then_inc(out_done, 1)

            def turned_part(b, k, j):
                dve.wait_ge(turned_high, b * HEADS * 3 + (k * 3 + j + 1))
                nc.vector.tensor_tensor(pT[1][:, k % 2, 2 * j:2 * j + 2, :].rearrange("p c n -> p (c n)"), ps_t[0:KC, 0:2 * N],
                                        pT[0][:, k % 2, 2 * j:2 * j + 2, :].rearrange("p c n -> p (c n)").bitcast(F32), ALU.subtract).then_inc(turned_done, 1)

            def first():
                dve.sem_inc(out_done, 1)
                norm_x(0)
                dve.wait_ge(cleared, 5)
                low(0, prologue, 0)
                for q in range(QT):
                    maxima(0, 0, q)
                for q in range(QT):
                    reciprocals(0, 0, q)

            def body(b, last):
                for k in range(HEADS):
                    todo, ahead, more, nxt = iteration(b, k, last)
                    at = places(todo)
                    turned_part(b, k, 0)
                    low(b, at[0], ahead)
                    if more:
                        maxima(*nxt, 0)
                    low(b, at[1], ahead)
                    if more:
                        maxima(*nxt, 1)
                        reciprocals(*nxt, 0)
                    turned_part(b, k, 1)
                    if more:
                        reciprocals(*nxt, 1)
                    low(b, at[2], ahead)
                    if k > 0:
                        out_part(b, k - 1)
                    low(b, at[3], ahead)
                    turned_part(b, k, 2)
                    low(b, at[4] + at[5], ahead)
                    if k == 11 and not last:
                        norm_x(b + 1)
                out_part(b, HEADS - 1)

            each_batch(dve, first, body)

        @block.tensor
        def _(pe):
            passes = ((0, 0), (1, 0), (0, 1))

            def project(b, todo, ahead):
                for n, what in todo:
                    ps_g = banks[:, n % 2]
                    if not (isinstance(b, int) and b == 0 and n < 2):
                        pe.wait_ge(group_done, group_no(b, n - 1, ahead))
                    if what[0] == "ctx":
                        c = what[1]
                        if c == 0:
                            pe.wait_ge(ctx_loaded, 96 * b + 96 * (1 + ahead))
                        for j in range(CC):
                            mm = nc.tensor.transpose(ps_g[:, j * KC:(j + 1) * KC], ctx_raw[:, c, j * P:(j + 1) * P], ident[0:KC, 0:KC])
                    elif what[0] == "x":
                        q = what[1]
                        if q == 0:
                            pe.wait_ge(x_normed, b + (1 + ahead))
                        for j in range(XC):
                            mm = nc.tensor.transpose(ps_g[:, j * TQ:(j + 1) * TQ], x_raw[:, q, j * P:(j + 1) * P], ident[0:TQ, 0:TQ])
                    elif what[0] == "k":
                        s, h = what[1:]
                        w = (wk_h, wk_l)
                        for i, (c, (a, m)) in enumerate((c, p) for c in range(CC) for p in passes):
                            mm = nc.tensor.matmul(ps_g[:, 0:KHP], w[a][:, c, s * P:(s + 1) * P], ctxT[m][:, c, h, :], start=(i == 0), stop=(i == 3 * CC - 1))
                    elif what[0] == "q":
                        s = what[1]
                        w = (wq_h, wq_l)
                        for i, (c, (a, m)) in enumerate((c, p) for c in range(XC) for p in passes):
                            mm = nc.tensor.matmul(ps_g[:, 0:N], w[a][:, c, s * P:(s + 1) * P], xT[m][:, c, :], start=(i == 0), stop=(i == 3 * XC - 1))
                    else:
                        g, kc = what[1:]
                        w = (wv_h, wv_l)
                        for i, (c, (a, m)) in enumerate((c, p) for c in range(CC) for p in passes):
                            mm = nc.tensor.matmul(ps_g[0:KC, 0:VH * DH], ctxT[a][:, c, kc // 3, kc % 3 * KC:(kc % 3 + 1) * KC],
                                                  w[m][:, c, g * VH * DH:(g + 1) * VH * DH], start=(i == 0), stop=(i == 3 * CC - 1))
                    mm.then_inc(group_ready, 1)

            def score(b, k, q, first=False):
                s = k // 2
                if k % 2 == 0 and q == 0:
                    n = 11 if s == 0 else next(n for n, w in per_head[2 * s - 2] if w[0] == "q") + 1
                    pe.wait_ge(group_done, group_no(b, n, 0))
                    pe.wait_ge(kipa_ready, b * PAIRS + (s + 1))
                if not first:
                    pe.wait_ge(exp_done, scores_unit(b, k, q) - 1)
                for h in range(2):
                    for i, (a, m) in enumerate(passes):
                        mm = nc.tensor.matmul(ps_s[:, q, h, 0:KHP], Q[:, s % 2, a, k % 2, q * TQ:(q + 1) * TQ], K[:, s % 2, m, h, :],
                                              start=(i == 0), stop=(i == 2))
                mm.then_inc(scores_ready, 1)

            def turn(b, k, j):
                if j == 0:
                    pe.wait_ge(prob_ready, scores_unit(b, k, 1) + 1)
                if k > 0 or j > 0:
                    pe.wait_ge(turned_done, b * HEADS * 3 + (k * 3 + j))
                for c in range(2 * j, 2 * j + 2):
                    for q in range(QT):
                        o = (c - 2 * j) * N + q * TQ
                        mm = nc.tensor.transpose(ps_t[0:KC, o:o + TQ],
                                                 prob[:, k % 2, q, c // 3, c % 3 * KC:(c % 3 + 1) * KC], ident[0:TQ, 0:TQ])
                mm.then_inc(turned, 1)

            def values(b, k):
                pe.wait_ge(turned_done, b * HEADS * 3 + 3 * (k + 1))
                if k % VH == 0:
                    pe.wait_ge(vipa_used, b * VG + (k // VH + 1))
                pe.wait_ge(out_done, b * HEADS + (k + 1))
                for i, (c, m) in enumerate((c, m) for c in range(KCN) for m in range(2)):
                    mm = nc.tensor.matmul(ps_o[:, 0:N], V[:, k // VH % 2, c, k % VH, :], pT[m][:, k % 2, c, :], start=(i == 0), stop=(i == 2 * KCN - 1))
                mm.then_inc(out_ready, 1)

            def first():
                pe.wait_ge(cleared, 5)
                project(0, prologue, 0)
                score(0, 0, 0, True)
                score(0, 0, 1, True)

            def body(b, last):
                for k in range(HEADS):
                    todo, ahead, more, nxt = iteration(b, k, last)
                    at = places(todo)
                    turn(b, k, 0)
                    project(b, at[0], ahead)
                    if more:
                        score(*nxt, 0)
                    project(b, at[1], ahead)
                    if more:
                        score(*nxt, 1)
                    turn(b, k, 1)
                    project(b, at[2], ahead)
                    if k > 0:
                        values(b, k - 1)
                    project(b, at[3], ahead)
                    turn(b, k, 2)
                    project(b, at[4] + at[5], ahead)
                values(b, HEADS - 1)

            each_batch(pe, first, body)


def project(nc, dram, const):
    ident, logits = const["ident"], const["logits"]
    OC = ID // P
    with ExitStack() as ctx:
        def sb(name, shape, dt=F32):
            return ctx.enter_context(nc.sbuf_tensor(name, shape, dt))

        def psum(name, shape):
            return ctx.enter_context(nc.psum_tensor(name, shape, F32))

        def sem(name):
            return ctx.enter_context(nc.semaphore(name))

        wo = sb("wo_raw", [P, OC, D])
        wo_h = sb("wo_h", [P, OC, D], F32R)
        wo_l = sb("wo_l", [P, OC, D], F32R)
        down = sb("o_down_sb", [P, OC, RANK])
        downT = sb("o_downT", [RANK, OC, P])
        up = sb("o_up_sb", [RANK, D])
        alpha = sb("o_alpha_sb", [P, 2])
        bo = sb("bo_sb", [TQ, D])
        wg = sb("w_gate_sb", [P, XC, E])
        eps = sb("eps2", [TQ, 1])
        o_raw = sb("o_raw", [P, 2, OC, N])
        o_h = sb("o_h", [P, 2, QT, OC, TQ], F32R)
        o_l = sb("o_l", [P, 2, QT, OC, TQ], F32R)
        x_in = sb("x_in", [TQ, 2, QT, D])
        x2 = sb("x2_sb", [TQ, 2, QT, D])
        xn = sb("xn2_sb", [TQ, 2, QT, D])
        xnT = sb("xn2T", [P, QT, XC, TQ])
        bn = sb("bn2", [TQ, QT, 6])
        mv = sb("mv2", [TQ, QT, 2])
        std = sb("std2", [TQ, QT])
        rstd = sb("rstd2", [TQ, QT])
        ps_o = psum("ps_proj", [TQ, QT, 512])
        ps_t = psum("ps_xn2T", [P, QT, 512])
        ps_l = psum("ps_logits", [TQ, QT, 512])
        ps_w = psum("ps_wo", [P, 2, 512])

        small_loaded = sem("o_small_loaded")
        late_loaded = sem("o_late_loaded")
        wo_loaded = [sem(f"wo_loaded{i}") for i in range(2)]
        o_loaded = [sem(f"o_loaded{i}") for i in range(2)]
        x_loaded = [sem(f"x_in_loaded{i}") for i in range(2)]
        eps_set = sem("eps_set")
        down_turned = sem("o_down_turned")
        down_copied = sem("o_down_copied")
        lora_done = sem("o_lora_done")
        eff_done = sem("o_eff_done")
        high_done = sem("wo_high")
        low_done = sem("wo_low")
        o_high = sem("o_high")
        o_split = sem("o_split")
        projected = sem("projected")
        x2_partial = sem("x2_partial")
        x2_done = sem("x2_done")
        stats = sem("stats2")
        passed = sem("passed2")
        var_done = sem("var_done")
        std_done = sem("std2_done")
        rstd_done = sem("rstd2_done")
        xn_done = sem("xn2_done")
        xn_stored = [sem(f"xn2_stored{i}") for i in range(2)]
        xn_turned = sem("xn2_turned")
        xn_copied = sem("xn2_copied")
        gated = sem("gated")
        logits_done = sem("logits_done")
        x2_stored = [sem(f"x2_stored{i}") for i in range(2)]
        block = ctx.enter_context(nc.Block())

        def pairs(engine, n, body):
            with engine.Fori(0, n) as two:
                body(two * 2 + 1, two, 1)
                body(two * 2 + 2, two + 1, 0)

        def rows(name, b):
            return dram[name][bass.ds(b, 1)].rearrange("o p t d -> (o p) t d")

        @block.sync
        def _(sp):
            sp.dma_start(down[:], dram["o_down"].rearrange("(c p) r -> p c r", p=P)).then_inc(small_loaded, 16)
            sp.dma_start(up[:], dram["o_up"]).then_inc(small_loaded, 16)
            sp.dma_start(alpha[:, 0:1], dram["o_alpha"].rearrange("(a o) -> a o", o=1).to_broadcast((P, 1))).then_inc(small_loaded, 16)
            for i in range(2):
                h = slice(i * OC // 2, (i + 1) * OC // 2)
                sp.dma_start(wo[:, h], dram["Wo"].rearrange("(c p) n -> p c n", p=P)[:, h]).then_inc(wo_loaded[i], 16)

            def load_o(b, i):
                sp.dma_start(o_raw[:, i], dram["oT"].rearrange("(c p) b n -> p c b n", p=P)[:, :, bass.ds(b, 1), :].rearrange("p c o n -> p c (o n)")).then_inc(o_loaded[i], 16)

            def load_x(b, i):
                sp.dma_start(x_in[:, i], rows("x_pq", b)).then_inc(x_loaded[i], 16)

            load_o(0, 0)
            load_x(0, 0)
            sp.dma_start(bo[:], dram["bo"].rearrange("(o d) -> o d", o=1).to_broadcast((TQ, D))).then_inc(late_loaded, 16)
            load_o(1, 1)
            load_x(1, 1)
            sp.dma_start(wg[:], dram["w_gate"].rearrange("(c p) e -> p c e", p=P)).then_inc(late_loaded, 16)
            sp.wait_ge(o_split, QT)
            load_o(2, 0)

            def batch(b, i, more_o=True, more_x=True):
                if more_o:
                    sp.wait_ge(o_split, b * QT + 2 * QT)
                    load_o(b + 3, 1 - i)
                sp.wait_ge(x2_done, b * QT + QT)
                sp.dma_start(rows("x2", b), x2[:, i]).then_inc(x2_stored[i], 16)
                if more_x:
                    load_x(b + 2, i)
                sp.wait_ge(xn_done, b * QT + QT)
                sp.dma_start(rows("xn2", b), xn[:, i]).then_inc(xn_stored[i], 16)

            batch(0, 0)
            pairs(sp, 2, lambda b, h, i: batch(b, i))
            batch(B - 3, 1, more_o=False)
            batch(B - 2, 0, more_o=False, more_x=False)
            batch(B - 1, 1, more_o=False, more_x=False)
            for i in range(2):
                sp.wait_ge(x2_stored[i], 16 * B // 2)
                sp.wait_ge(xn_stored[i], 16 * B // 2)

        @block.gpsimd
        def _(pool):
            pool.wait_ge(late_loaded, 2 * 16)
            with pool.Fori(0, B // 2) as two:
                for i in range(2):
                    pool.wait_ge(x_loaded[i], two * 16 + 16)
                    for q in range(QT):
                        nc.gpsimd.tensor_tensor(x_in[:, i, q], x_in[:, i, q], bo[:], ALU.add).then_inc(x2_partial, 1)

        @block.scalar
        def _(act):
            act.wait_ge(down_turned, 1)
            nc.scalar.copy(downT[:, 0:4], ps_w[0:RANK, 0].rearrange("r (c p) -> r c p", p=P))
            nc.scalar.copy(downT[:, 4:8], ps_w[0:RANK, 1].rearrange("r (c p) -> r c p", p=P)).then_inc(down_copied, 1)
            for c in range(OC):
                act.wait_ge(eff_done, c + 1)
                nc.scalar.copy(wo_h[:, c], wo[:, c]).then_inc(high_done, 1)

            def split(b, h, i):
                act.wait_ge(o_loaded[i], h * 16 + 16)
                for q in range(QT):
                    if not (isinstance(b, int) and b < 2):
                        act.wait_ge(projected, b * QT + (q - 2 * QT + 1))
                    nc.scalar.copy(o_h[:, i, q], o_raw[:, i, :, q * TQ:(q + 1) * TQ]).then_inc(o_high, 1)

            def turned_copy(b):
                for q in range(QT):
                    act.wait_ge(xn_turned, b * QT + (q + 1))
                    nc.scalar.copy(xnT[:, q], ps_t[:, q, 0:XC * TQ].rearrange("p (c t) -> p c t", c=XC)).then_inc(xn_copied, 1)

            def deviations(b):
                for q in range(QT):
                    act.wait_ge(var_done, b * QT + (q + 1))
                    nc.scalar.activation(std[:, q:q + 1], mv[:, q, 1:2], ACT.Sqrt, bias=eps[:, 0:1]).then_inc(std_done, 1)

            split(0, 0, 0)
            split(1, 0, 1)
            deviations(0)

            def batch(b, h, i):
                split(b + 1, h + i, 1 - i)
                turned_copy(b - 1)
                deviations(b)

            pairs(act, B // 2 - 1, batch)
            turned_copy(B - 2)
            deviations(B - 1)
            turned_copy(B - 1)

        @block.vector
        def _(dve):
            nc.vector.memset(eps[:], EPS).then_inc(eps_set, 1)
            dve.wait_ge(small_loaded, 3 * 16)
            nc.vector.tensor_scalar(alpha[:, 1:2], alpha[:, 0:1], 1.0 / RANK, None, ALU.mult).then_inc(eps_set, 1)
            dve.wait_ge(eps_set, 2)

            def low(c):
                dve.wait_ge(high_done, c + 1)
                nc.vector.tensor_tensor(wo_l[:, c], wo[:, c], wo_h[:, c].bitcast(F32), ALU.subtract).then_inc(low_done, 1)

            for c in range(OC):
                if c % (OC // 2) == 0:
                    dve.wait_ge(wo_loaded[c // (OC // 2)], 16)
                dve.wait_ge(lora_done, c + 1)
                nc.vector.scalar_tensor_tensor(out=wo[:, c], in0=ps_w[:, c % 2, :], scalar=alpha[:, 1:2], in1=wo[:, c],
                                               op0=ALU.mult, op1=ALU.add).then_inc(eff_done, 1)
                if c > 0:
                    low(c - 1)
            low(OC - 1)

            def split(b, i):
                for q in range(QT):
                    dve.wait_ge(o_high, b * QT + (q + 1))
                    nc.vector.tensor_tensor(o_l[:, i, q], o_raw[:, i, :, q * TQ:(q + 1) * TQ], o_h[:, i, q].bitcast(F32), ALU.subtract).then_inc(o_split, 1)

            def norm(b, h, i):
                for q in range(QT):
                    T = b * QT + q
                    dve.wait_ge(projected, T + 1)
                    dve.wait_ge(x2_partial, T + 1)
                    if q == 0 and not (isinstance(b, int) and b < 2):
                        dve.wait_ge(x2_stored[i], h * 16)
                        dve.wait_ge(xn_stored[i], h * 16)
                    nc.vector.tensor_tensor(x2[:, i, q], ps_o[:, q, :], x_in[:, i, q], ALU.add).then_inc(x2_done, 1)
                    dve.wait_ge(x2_done, T + 1)
                    nc.vector.bn_stats(bn[:, q], x2[:, i, q]).then_inc(stats, 1)
                    dve.wait_ge(stats, T + 1)
                    dve.sem_inc(passed, 1)
                    nc.vector.bn_aggr(mv[:, q], bn[:, q]).then_inc(var_done, 1)
                    dve.wait_ge(std_done, T + 1)
                    nc.vector.reciprocal(rstd[:, q:q + 1], std[:, q:q + 1]).then_inc(rstd_done, 1)
                    dve.wait_ge(rstd_done, T + 1)
                    nc.vector.tensor_scalar(xn[:, i, q], x2[:, i, q], mv[:, q, 0:1], rstd[:, q:q + 1], ALU.subtract, ALU.mult).then_inc(xn_done, 1)

            def keep_logits(b):
                for q in range(QT):
                    T = b * QT + q
                    dve.wait_ge(gated, T + 1)
                    nc.vector.tensor_copy(logits[:, bass.ds(T, 1), :].rearrange("p o e -> p (o e)"), ps_l[:, q, 0:E]).then_inc(logits_done, 1)

            split(0, 0)
            split(1, 1)
            norm(0, 0, 0)

            def batch(b, h, i):
                split(b + 1, 1 - i)
                norm(b, h, i)
                keep_logits(b - 1)

            split(2, 0)
            norm(1, 0, 1)
            keep_logits(0)
            with dve.Fori(1, B // 2 - 1) as two:
                batch(two * 2, two, 0)
                batch(two * 2 + 1, two, 1)
            batch(B - 2, B // 2 - 1, 0)
            norm(B - 1, B // 2 - 1, 1)
            keep_logits(B - 2)
            keep_logits(B - 1)

        @block.tensor
        def _(pe):
            pe.wait_ge(small_loaded, 3 * 16)
            for c in range(OC):
                mm = nc.tensor.transpose(ps_w[0:RANK, c // 4, c % 4 * P:(c % 4 + 1) * P], down[:, c], ident[:])
            mm.then_inc(down_turned, 1)
            pe.wait_ge(down_copied, 1)
            for c in range(OC):
                if c >= 2:
                    pe.wait_ge(eff_done, c - 1)
                nc.tensor.matmul(ps_w[:, c % 2, :], downT[:, c], up[:], start=True, stop=True).then_inc(lora_done, 1)
            pe.wait_ge(low_done, OC)

            def multiply(b, i, q):
                T = b * QT + q
                pe.wait_ge(o_split, T + 1)
                if not (isinstance(b, int) and b == 0):
                    pe.wait_ge(x2_done, T - 1)
                for n, (c, (a, m)) in enumerate((c, p) for c in range(OC) for p in ((0, 0), (1, 0), (0, 1))):
                    mm = nc.tensor.matmul(ps_o[:, q, :], (o_h, o_l)[a][:, i, q, c], (wo_h, wo_l)[m][:, c], start=(n == 0), stop=(n == 3 * OC - 1))
                mm.then_inc(projected, 1)

            def turn(b, i):
                for q in range(QT):
                    pe.wait_ge(xn_done, b * QT + (q + 1))
                    for c in range(XC):
                        mm = nc.tensor.transpose(ps_t[:, q, c * TQ:(c + 1) * TQ], xn[:, i, q, c * P:(c + 1) * P], ident[0:TQ, 0:TQ])
                    mm.then_inc(xn_turned, 1)

            def gate(b):
                for q in range(QT):
                    T = b * QT + q
                    pe.wait_ge(xn_copied, T + 1)
                    if not (isinstance(b, int) and b == 0):
                        pe.wait_ge(logits_done, T - 1)
                    for c in range(XC):
                        mm = nc.tensor.matmul(ps_l[:, q, 0:E], xnT[:, q, c], wg[:, c], start=(c == 0), stop=(c == XC - 1))
                    mm.then_inc(gated, 1)

            def batch(b, i):
                multiply(b, i, 0)
                turn(b - 1, 1 - i)
                multiply(b, i, 1)
                gate(b - 1)

            for q in range(QT):
                multiply(0, 0, q)
            pe.wait_ge(late_loaded, 2 * 16)
            batch(1, 1)
            with pe.Fori(1, B // 2) as two:
                batch(two * 2, 0)
                batch(two * 2 + 1, 1)
            turn(B - 1, 1)
            gate(B - 1)


def experts(nc, dram, const):
    ident, logits, pos, weight = (const[k] for k in ("ident", "logits", "pos", "weight"))
    with ExitStack() as ctx:
        def sb(name, shape, dt=F32):
            return ctx.enter_context(nc.sbuf_tensor(name, shape, dt))

        def psum(name, shape):
            return ctx.enter_context(nc.psum_tensor(name, shape, F32))

        def sem(name):
            return ctx.enter_context(nc.semaphore(name))

        W1 = sb("w1", [P, 2, 2, XC, 2 * F], F32R)
        W2 = sb("w2", [P, 2, 2, FC, D], F32R)
        raw = sb("w_stage", [P, 2, 2 * F])
        xg = sb("x_slots", [P, 2, D])
        xT = sb("x_slotsT", [P, 2, 2, XC, SUB], F32R)
        act_sb = sb("act", [P, 2, F])
        hT = sb("hT", [P, 2, 2, FC, SUB], F32R)
        y = sb("y", [P, 2, D])
        rows = hT[0:TQ].rearrange("p s l c t -> p (s l c t)").rearrange("p (n d) -> p n d", d=D).bitcast(F32)
        RING = 2 * 2 * FC * SUB // D
        ones = sb("ones_r", [TQ, TQ])
        tri = sb("tri", [TQ, TQ])
        iota = sb("iota_e", [TQ, E])
        thr = sb("thresholds", [TQ, KMAX])
        top = sb("top", [TQ, NT, 8])
        idx = sb("idx", [TQ, NT, 8], U32)
        idxf = sb("idxf", [TQ, NT, 2])
        hot = sb("hot", [TQ, 2, NT, E])
        both = sb("both", [TQ, NT, E])
        shifted = sb("shifted", [TQ, NT, E])
        expo = sb("expo", [TQ, NT, E])
        second = sb("second", [TQ, NT])
        second_e = sb("second_e", [TQ, NT])
        total = sb("total", [TQ, E])
        over = sb("over", [TQ, E, KMAX])
        nsteps = sb("nsteps", [TQ, E])
        before = sb("before", [TQ, E])
        count = sb("count", [TQ, NT, E])
        start = sb("start", [TQ, NT, E])
        slot = sb("slot", [TQ, NT, E])
        picked = sb("picked", [TQ, 2, NT, E])
        posf = sb("posf", [TQ, 2, NT])
        table = sb("table", [1, 2 * E], I32)
        ps_h = [psum(f"ps_h{i}", [P, 3, 512]) for i in range(2)]
        ps_t = psum("ps_turn", [P, 512])
        ps_y = psum("ps_y", [P, 512])

        raw_loaded = [sem(f"stage{i}_loaded") for i in range(2)]
        stage_loaded = [sem(f"stage{i}_loaded_pool") for i in range(2)]
        w0_high = sem("w0_high")
        w0_ready = sem("w0_ready")
        const_set = sem("const_set")
        tri_set = sem("tri_set")
        routed = sem("routed")
        shifted_ready = sem("shifted_ready")
        expo_ready = sem("expo_ready")
        both_ready = sem("both_ready")
        ranked = sem("ranked")
        table_ready = sem("table_ready")
        rows_loaded = [sem(f"rows{i}_loaded") for i in range(RING)]
        scattered = [sem(f"scattered{i}") for i in range(RING)]
        passed = sem("passed")
        ended = sem("ended")
        w_high = sem("w_high")
        w_ready = sem("w_ready")
        x_loaded = sem("slots_loaded")
        turned = sem("slots_turned")
        turned_high = sem("slots_turned_high")
        turned_done = sem("slots_turned_done")
        hidden = sem("hidden")
        silu_done = sem("silu_done")
        glu_done = sem("glu_done")
        y_ready = sem("y_ready")
        y_done = sem("y_done")
        y_stored = [sem(f"y{i}_stored") for i in range(2)]
        block = ctx.enter_context(nc.Block())

        PIECES = XC + FC * D // (2 * F)

        def piece_src(e, c):
            w1 = dram["c_fc"].rearrange("e (c p) f -> e c p f", p=P)
            w2 = dram["c_proj"].rearrange("e (h c p) d -> e h p c d", p=P, h=2)
            if c < XC:
                return w1[e, c] if isinstance(e, int) else w1[bass.ds(e, 1), c].rearrange("o p f -> (o p) f")
            return w2[e, c - XC] if isinstance(e, int) else w2[bass.ds(e, 1), c - XC].rearrange("o p c d -> (o p) c d")

        def stage(i, c):
            return raw[:, i] if c < XC else raw[:, i].rearrange("p (c d) -> p c d", d=D)

        def piece_dst(buf, part, c):
            if c < XC:
                return W1[:, buf, part, c]
            h = (c - XC) * (FC // 2)
            return W2[:, buf, part, h:h + FC // 2].rearrange("p c d -> p (c d)")

        def each_step(engine, body):
            engine.wait_ge(table_ready, 1)
            with engine.Fori(0, E // 2) as pair:
                for buf in range(2):
                    e = pair * 2 + buf
                    n = engine.value_load(table[0:1, bass.ds(e, 1)], min_val=1, max_val=KMAX)
                    first = engine.value_load(table[0:1, bass.ds(e + E, 1)], min_val=0, max_val=MAXSTEPS - 1)
                    with engine.Fori(0, n) as j:
                        body(buf, first + j, e)

        @block.sync
        def _(sp):
            for c in range(PIECES):
                if c >= 2:
                    sp.wait_ge(w0_ready, c - 1)
                sp.dma_start(stage(c % 2, c), piece_src(0, c)).then_inc(raw_loaded[c % 2], 16)
            for n in range(NT):
                if n >= RING:
                    sp.wait_ge(scattered[n % RING], 32 * (n // RING))
                sp.dma_start(rows[:, n % RING], dram["xn2"][n // QT, :, n % QT]).then_inc(rows_loaded[n % RING], 16)
            for i in range(RING):
                sp.wait_ge(scattered[i], 32 * len(range(i, NT, RING)))
            slots = dram["slots"].rearrange("(g s p) d -> g p s d", s=2, p=P)
            ys = dram["slots"].rearrange("(g s p) d -> g s p d", s=2, p=P)

            def load(g):
                sp.dma_start(xg[:], slots[bass.ds(g, 1)].rearrange("o p s d -> (o p) s d")).then_inc(x_loaded, 16)

            for i in range(2):
                sp.sem_inc(y_stored[i], 16)
            load(0)
            sp.wait_ge(turned, 2)
            load(1)

            def body(buf, g, e):
                sp.wait_ge(y_done, g * 2 + 2)
                sp.dma_start(ys[bass.ds(g, 1), 0].rearrange("o p d -> (o p) d"), y[:, 0]).then_inc(y_stored[0], 16)
                sp.wait_ge(turned, g * 6 + 6)
                load(g + 2)
                sp.wait_ge(y_done, g * 2 + 3)
                sp.dma_start(ys[bass.ds(g, 1), 1].rearrange("o p d -> (o p) d"), y[:, 1]).then_inc(y_stored[1], 16)

            each_step(sp, body)
            steps = sp.value_load(table[0:1, 2 * E - 1:2 * E], min_val=E - 1, max_val=MAXSTEPS - 1) \
                + sp.value_load(table[0:1, E - 1:E], min_val=1, max_val=KMAX)
            sp.wait_ge(x_loaded, steps * 16 + 32)
            sp.sem_inc(ended, 1)
            for i in range(2):
                sp.wait_ge(y_stored[i], steps * 16 + 16)
                sp.sem_inc(ended, 1)

        @block.gpsimd
        def _(pool):
            nc.gpsimd.memset(ones[:], 1.0).then_inc(const_set, 1)
            pool.wait_ge(const_set, 1)
            nc.gpsimd.affine_select(out=tri[:], in_=ones[:], compare_op=ALU.is_gt, fill=0.0, base=0,
                                    pattern=[[1, TQ]], channel_multiplier=-1).then_inc(tri_set, 1)
            pool.wait_ge(table_ready, 1)
            for n in range(NT):
                pool.wait_ge(rows_loaded[n % RING], 16 * (n // RING + 1))
                for j in range(2):
                    nc.gpsimd.indirect_dma_start(out=dram["slots"], out_offset=bass.IndirectOffsetOnAxis(ap=pos[:, j, n:n + 1], axis=0),
                                                 in_=rows[:, n % RING], in_offset=None).then_inc(scattered[n % RING], 16)

            def weights(e, buf):
                for c in range(PIECES):
                    if c < 2:
                        pool.dma_start(stage(c, c), piece_src(e, c)).then_inc(stage_loaded[c], 16)
                for c in range(PIECES):
                    pool.wait_ge(stage_loaded[c % 2], (e - 1) * (8 * PIECES) + 16 * (c // 2 + 1))
                    pool.sem_inc(passed, 1)
                    nc.gpsimd.tensor_scalar(piece_dst(buf, 0, c), raw[:, c % 2], 1.0, 1.0, ALU.mult, ALU.mult).then_inc(w_high, 1)
                    pool.wait_ge(w_high, (e - 1) * PIECES + (c + 1))
                    nc.gpsimd.tensor_tensor(piece_dst(buf, 1, c), raw[:, c % 2], piece_dst(buf, 0, c).bitcast(F32), ALU.subtract).then_inc(w_ready, 1)
                    if c + 2 < PIECES:
                        pool.wait_ge(w_ready, (e - 1) * PIECES + (c + 2))
                        pool.sem_inc(passed, 1)
                        pool.dma_start(stage(c % 2, c + 2), piece_src(e, c + 2)).then_inc(stage_loaded[c % 2], 16)

            pool.wait_ge(w0_ready, PIECES)
            pool.sem_inc(w_ready, 1)
            weights(1, 1)
            with pool.Fori(0, E // 2 - 1) as pair:
                for buf in range(2):
                    e = pair * 2 + (buf + 2)
                    steps = pool.value_load(table[0:1, bass.ds(e + (E - 1), 1)], min_val=1, max_val=MAXSTEPS - 1)
                    pool.wait_ge(y_ready, steps * 2)
                    pool.sem_inc(passed, 1)
                    pool.wait_ge(w_ready, (e - 1) * PIECES + 1)
                    pool.sem_inc(passed, 1)
                    weights(e, buf)

        @block.scalar
        def _(act):
            act.wait_ge(shifted_ready, 1)
            nc.scalar.activation(expo[:], shifted[:], ACT.Exp)
            nc.scalar.activation(second_e[:], second[:], ACT.Exp).then_inc(expo_ready, 1)
            for c in range(PIECES):
                act.wait_ge(raw_loaded[c % 2], 16 * (c // 2 + 1))
                nc.scalar.copy(piece_dst(0, 0, c), raw[:, c % 2]).then_inc(w0_high, 1)

            def high(no, dst, src):
                act.wait_ge(turned, no + 1)
                nc.scalar.copy(dst, src.rearrange("p (c t) -> p c t", t=SUB)).then_inc(turned_high, 1)

            def silu(g, s):
                act.wait_ge(hidden, g * 2 + (s + 1))
                nc.scalar.activation(act_sb[:, s], ps_h[s][:].rearrange("p j n -> p (j n)")[:, 0:F], ACT.Silu).then_inc(silu_done, 1)

            def out(g, s):
                act.wait_ge(y_ready, g * 2 + (s + 1))
                act.wait_ge(y_stored[s], g * 16 + 16)
                nc.scalar.copy(y[:, s], ps_y[:]).then_inc(y_done, 1)

            act.sem_inc(y_done, 1)
            for s in range(2):
                high(s, xT[:, s, 0], ps_t[:])

            def body(buf, g, e):
                no = g * 6 + 2
                silu(g, 0)
                high(no, hT[:, 0, 0, 0:3], ps_t[:, 0:3 * SUB])
                high(no + 1, hT[:, 0, 0, 3:6], ps_t[:, 0:3 * SUB])
                silu(g, 1)
                high(no + 2, xT[:, 0, 0], ps_t[:])
                high(no + 3, xT[:, 1, 0], ps_t[:])
                high(no + 4, hT[:, 1, 0, 0:3], ps_h[0][:, 0, 0:3 * SUB])
                high(no + 5, hT[:, 1, 0, 3:6], ps_h[0][:, 1, 0:3 * SUB])
                out(g, 0)
                out(g, 1)

            each_step(act, body)

        @block.vector
        def _(dve):
            done = [0]

            def step(ins):
                done[0] += 1
                ins.then_inc(routed, 1)
                dve.wait_ge(routed, done[0])

            def over_e(ap):
                return ap.rearrange("p (n o) -> p n o", o=1).to_broadcast((TQ, NT, E))

            for e in range(E):
                last = nc.vector.memset(iota[:, e:e + 1], float(e))
            for k in range(KMAX):
                last = nc.vector.memset(thr[:, k:k + 1], float(STEP * k))
            step(last)
            for n in range(NT):
                last = nc.vector.max(top[:, n], logits[:, n])
            step(last)
            for n in range(NT):
                last = nc.vector.max_index(idx[:, n], top[:, n], logits[:, n])
            step(last)
            step(nc.vector.tensor_tensor(second[:], top[:, :, 1], top[:, :, 0], ALU.subtract))
            nc.vector.tensor_tensor(shifted[:], logits[:], over_e(top[:, :, 0]), ALU.subtract).then_inc(shifted_ready, 1)
            step(nc.vector.tensor_copy(idxf[:], idx[:, :, 0:2]))
            for j in range(2):
                last = nc.vector.tensor_tensor(hot[:, j], iota[:].rearrange("p (o e) -> p o e", o=1).to_broadcast((TQ, NT, E)),
                                               over_e(idxf[:, :, j]), ALU.is_equal)
            step(last)
            nc.vector.tensor_tensor(both[:], hot[:, 0], hot[:, 1], ALU.add).then_inc(both_ready, 1)
            dve.wait_ge(expo_ready, 1)
            step(nc.vector.tensor_reduce(weight[:, 1], expo[:], AX.X, ALU.add))
            step(nc.vector.reciprocal(weight[:, 0], weight[:, 1]))
            step(nc.vector.tensor_tensor(weight[:, 1], weight[:, 0], second_e[:], ALU.mult))
            dve.wait_ge(ranked, 1)
            step(nc.vector.tensor_copy(count[:], ps_y[0:TQ, 0:NT * E].rearrange("p (n e) -> p n e", e=E)))
            step(nc.vector.tensor_reduce(total[:], count[:].rearrange("p n e -> p e n"), AX.X, ALU.add))
            step(nc.vector.tensor_tensor(over[:], total[:].rearrange("p (e o) -> p e o", o=1).to_broadcast((TQ, E, KMAX)),
                                         thr[:].rearrange("p (o k) -> p o k", o=1).to_broadcast((TQ, E, KMAX)), ALU.is_gt))
            step(nc.vector.tensor_reduce(nsteps[:], over[:], AX.X, ALU.add))
            step(nc.vector.tensor_scalar(nsteps[:], nsteps[:], 1.0, None, ALU.max))
            step(nc.vector.memset(before[:, 0:1], 0.0))
            for e in range(1, E):
                step(nc.vector.tensor_tensor(before[:, e:e + 1], before[:, e - 1:e], nsteps[:, e - 1:e], ALU.add))
            nc.vector.tensor_copy(table[0:1, 0:E], nsteps[0:1, :])
            nc.vector.tensor_copy(table[0:1, E:2 * E], before[0:1, :])
            step(nc.vector.tensor_scalar(start[:, 0], before[:], float(STEP), None, ALU.mult))
            for n in range(1, NT):
                step(nc.vector.tensor_tensor(start[:, n], start[:, n - 1], count[:, n - 1], ALU.add))
            step(nc.vector.tensor_tensor(slot[:], ps_t[0:TQ, 0:NT * E].rearrange("p (n e) -> p n e", e=E), start[:], ALU.add))
            for j in range(2):
                last = nc.vector.tensor_tensor(picked[:, j], hot[:, j], slot[:], ALU.mult)
            step(last)
            step(nc.vector.tensor_reduce(posf[:].rearrange("p j n -> p (j n)"), picked[:].rearrange("p j n e -> p (j n) e"), AX.X, ALU.add))
            nc.vector.tensor_copy(pos[:], posf[:]).then_inc(table_ready, 1)
            for c in range(PIECES):
                dve.wait_ge(w0_high, c + 1)
                nc.vector.tensor_tensor(piece_dst(0, 1, c), raw[:, c % 2], piece_dst(0, 0, c).bitcast(F32), ALU.subtract).then_inc(w0_ready, 1)

            def low(no, dst, high, src):
                dve.wait_ge(turned_high, no + 1)
                nc.vector.tensor_tensor(dst, src.rearrange("p (c t) -> p c t", t=SUB), high.bitcast(F32), ALU.subtract).then_inc(turned_done, 1)

            def glu(g, s):
                dve.wait_ge(silu_done, g * 2 + (s + 1))
                nc.vector.tensor_tensor(act_sb[:, s], ps_h[s][:].rearrange("p j n -> p (j n)")[:, F:2 * F], act_sb[:, s], ALU.mult).then_inc(glu_done, 1)

            for s in range(2):
                low(s, xT[:, s, 1], xT[:, s, 0], ps_t[:])

            def body(buf, g, e):
                no = g * 6 + 2
                glu(g, 0)
                low(no, hT[:, 0, 1, 0:3], hT[:, 0, 0, 0:3], ps_t[:, 0:3 * SUB])
                low(no + 1, hT[:, 0, 1, 3:6], hT[:, 0, 0, 3:6], ps_t[:, 0:3 * SUB])
                glu(g, 1)
                low(no + 2, xT[:, 0, 1], xT[:, 0, 0], ps_t[:])
                low(no + 3, xT[:, 1, 1], xT[:, 1, 0], ps_t[:])
                low(no + 4, hT[:, 1, 1, 0:3], hT[:, 1, 0, 0:3], ps_h[0][:, 0, 0:3 * SUB])
                low(no + 5, hT[:, 1, 1, 3:6], hT[:, 1, 0, 3:6], ps_h[0][:, 1, 0:3 * SUB])

            each_step(dve, body)

        @block.tensor
        def _(pe):
            passes = ((0, 0), (1, 0), (0, 1))
            pe.wait_ge(tri_set, 1)
            pe.wait_ge(both_ready, 1)
            flat = both[:].rearrange("p n e -> p (n e)")
            nc.tensor.matmul(ps_t[0:TQ, 0:NT * E], tri[:], flat, start=True, stop=True)
            nc.tensor.matmul(ps_y[0:TQ, 0:NT * E], ones[:], flat, start=True, stop=True).then_inc(ranked, 1)

            def turn(dst, src):
                n = src.shape[-1] // SUB
                for c in range(n):
                    mm = nc.tensor.transpose(dst[:, c * SUB:(c + 1) * SUB], src[:, c * SUB:(c + 1) * SUB], ident[:])
                mm.then_inc(turned, 1)

            def hidden_bank(buf, s, j):
                for n, (c, (a, m)) in enumerate((c, p) for c in range(XC) for p in passes):
                    mm = nc.tensor.matmul(ps_h[s][:, j], xT[:, s, a, c], W1[:, buf, m, c, j * 512:(j + 1) * 512], start=(n == 0), stop=(n == 3 * XC - 1))
                return mm

            def result(buf, s, half):
                for n, (c, (a, m)) in enumerate((c, p) for c in range(FC) for p in passes):
                    if n // (3 * FC // 2) == half:
                        mm = nc.tensor.matmul(ps_y[:], hT[:, s, a, c], W2[:, buf, m, c], start=(n == 0), stop=(n == 3 * FC - 1))
                if half == 1:
                    mm.then_inc(y_ready, 1)

            pe.wait_ge(table_ready, 1)
            pe.wait_ge(x_loaded, 16)
            turn(ps_t[:], xg[:, 0])
            pe.wait_ge(turned_done, 1)
            turn(ps_t[:], xg[:, 1])
            pe.wait_ge(turned_done, 2)

            def body(buf, g, e):
                no = g * 6 + 2
                pe.wait_ge(w_ready, e * PIECES + 1)
                for j in range(3):
                    mm = hidden_bank(buf, 0, j)
                mm.then_inc(hidden, 1)
                hidden_bank(buf, 1, 0)
                pe.wait_ge(glu_done, g * 2 + 1)
                turn(ps_t[:], act_sb[:, 0, 0:F // 2])
                hidden_bank(buf, 1, 1)
                pe.wait_ge(turned_done, no + 1)
                turn(ps_t[:], act_sb[:, 0, F // 2:F])
                hidden_bank(buf, 1, 2).then_inc(hidden, 1)
                pe.wait_ge(x_loaded, g * 16 + 32)
                pe.wait_ge(turned_done, no + 2)
                turn(ps_t[:], xg[:, 0])
                pe.wait_ge(y_done, g * 2 + 1)
                result(buf, 0, 0)
                pe.wait_ge(turned_done, no + 3)
                turn(ps_t[:], xg[:, 1])
                pe.wait_ge(glu_done, g * 2 + 2)
                turn(ps_h[0][:, 0], act_sb[:, 1, 0:F // 2])
                turn(ps_h[0][:, 1], act_sb[:, 1, F // 2:F])
                result(buf, 0, 1)
                pe.wait_ge(turned_done, no + 6)
                pe.wait_ge(y_done, g * 2 + 2)
                result(buf, 1, 0)
                result(buf, 1, 1)

            each_step(pe, body)


def combine(nc, dram, const):
    pos, weight = const["pos"], const["weight"]
    RING = 4
    with ExitStack() as ctx:
        def sb(name, shape, dt=F32):
            return ctx.enter_context(nc.sbuf_tensor(name, shape, dt))

        def sem(name):
            return ctx.enter_context(nc.semaphore(name))

        x2 = sb("x2_in", [TQ, NT, D])
        got = sb("got", [TQ, RING, 2, D])
        part = sb("part", [TQ, RING, D])
        x2_loaded = sem("x2_loaded")
        gathered = [sem(f"gathered{i}") for i in range(RING)]
        first_added = sem("first_added")
        added = sem("added")
        stored = sem("stored")
        block = ctx.enter_context(nc.Block())

        @block.sync
        def _(sp):
            sp.dma_start(x2[:].rearrange("p (b t) d -> p b t d", t=QT), dram["x2"].rearrange("b p t d -> p b t d")).then_inc(x2_loaded, 16)
            for n in range(NT):
                sp.wait_ge(added, n + 1)
                sp.dma_start(dram["out_pq"][n // QT, :, n % QT], x2[:, n]).then_inc(stored, 16)
            sp.wait_ge(stored, 16 * NT)

        @block.gpsimd
        def _(pool):
            for n in range(NT):
                if n >= RING:
                    pool.wait_ge(added, n - RING + 1)
                for j in range(2):
                    nc.gpsimd.indirect_dma_start(out=got[:, n % RING, j], out_offset=None, in_=dram["slots"],
                                                 in_offset=bass.IndirectOffsetOnAxis(ap=pos[:, j, n:n + 1], axis=0)).then_inc(gathered[n % RING], 16)

        @block.vector
        def _(dve):
            dve.wait_ge(x2_loaded, 16)
            for n in range(NT):
                dve.wait_ge(gathered[n % RING], 32 * (n // RING + 1))
                nc.vector.scalar_tensor_tensor(out=part[:, n % RING], in0=got[:, n % RING, 0], scalar=weight[:, 0, n:n + 1], in1=x2[:, n],
                                               op0=ALU.mult, op1=ALU.add).then_inc(first_added, 1)
                dve.wait_ge(first_added, n + 1)
                nc.vector.scalar_tensor_tensor(out=x2[:, n], in0=got[:, n % RING, 1], scalar=weight[:, 1, n:n + 1], in1=part[:, n % RING],
                                               op0=ALU.mult, op1=ALU.add).then_inc(added, 1)


def block_kernel(nc, x, ctx_768, Wq, Wk, Wv, Wo, bo, q_down, q_up, q_alpha, k_down, k_up, k_alpha, v_down, v_up,
                 v_alpha, o_down, o_up, o_alpha, Wk_ipa, Wv_ipa, w_gate, c_fc, c_proj, out):
    dram = dict(x=x, ctx=ctx_768, Wq=Wq, Wk=Wk, Wv=Wv, Wo=Wo, bo=bo, q_down=q_down, q_up=q_up, q_alpha=q_alpha,
                k_down=k_down, k_up=k_up, k_alpha=k_alpha, v_down=v_down, v_up=v_up, v_alpha=v_alpha,
                o_down=o_down, o_up=o_up, o_alpha=o_alpha, Wk_ipa=Wk_ipa, Wv_ipa=Wv_ipa,
                w_gate=w_gate, c_fc=c_fc, c_proj=c_proj,
                x_pq=x.rearrange("b (t p) d -> b p t d", p=TQ), out_pq=out.rearrange("b (t p) d -> b p t d", p=TQ))
    for name, shape in (("vipa", [B * IPA, HEADS * 2 * DH]), ("oT", [ID, B, N]), ("x2", [B, TQ, QT, D]), ("xn2", [B, TQ, QT, D]),
                        ("slots", [ROOM * STEP, D])):
        dram[name] = nc.dram_tensor(f"{name}_scratch", shape, F32).ap()
    with ExitStack() as ctx:
        const = {}

        def sb(stack, name, shape, dt=F32):
            const[name] = stack.enter_context(nc.sbuf_tensor(name, shape, dt))

        sb(ctx, "ident", [P, P])
        sb(ctx, "logits", [TQ, NT, E])
        sb(ctx, "pos", [TQ, 2, NT], U32)
        sb(ctx, "weight", [TQ, 2, NT])
        with ExitStack() as inner:
            sb(inner, "kipa", [P, PAIRS, 2, B * IPA], F32R)
            sb(inner, "rstd", [TQ, NT])
            sb(inner, "mean", [TQ, NT])
            for k, n in (("q", XC), ("k", CC), ("v", CC)):
                for part in "hl":
                    sb(inner, f"w{k}_{part}", [P, n, ID], F32R)
            prepare(nc, dram, const)
            attend(nc, dram, const)
        project(nc, dram, const)
        experts(nc, dram, const)
        combine(nc, dram, const)


_INS = ["x", "ctx_768"] + [f"L0_xattn_{n}" for n in (
    "Wq", "Wk", "Wv", "Wo", "bo", "q_down", "q_up", "q_alpha", "k_down", "k_up", "k_alpha", "v_down", "v_up", "v_alpha",
    "o_down", "o_up", "o_alpha", "Wk_ipa", "Wv_ipa")] + [f"L0_ffn_{n}" for n in ("w_gate", "c_fc", "c_proj")]


def kernel(**inputs):
    import concourse.bacc as bacc
    from concourse.bass_utils import run_bass_kernel_spmd

    nc = bacc.Bacc("TRN2", target_bir_lowering=False, num_devices=1)
    arrays, args = {}, []
    for name in _INS:
        a = np.ascontiguousarray(inputs[name])
        arrays[f"in_{name}"] = a
        args.append(nc.dram_tensor(f"in_{name}", a.shape, mybir.dt.from_np(a.dtype), kind="ExternalInput").ap())
    args.append(nc.dram_tensor("out_0", (B, N, D), F32, kind="ExternalOutput").ap())
    block_kernel(nc, *args)
    r = run_bass_kernel_spmd(nc, [arrays], core_ids=[0])
    return r.results[0]["out_0"]
```

```python
from contextlib import ExitStack

import numpy as np

import concourse.bass as bass
from concourse import mybir

F32 = mybir.dt.float32
F32R = mybir.dt.float32r
I32 = mybir.dt.int32
U32 = mybir.dt.uint32
ALU = mybir.AluOpType
ACT = mybir.ActivationFunctionType
AX = mybir.AxisListType

B, N, D = 8, 224, 512
CTX, CD = 750, 384
IPA = 4
HEADS, DH = 16, 64
ID = HEADS * DH
RANK = 32
SCALE = DH ** -0.5
EPS = 1e-5
P = 128
QT, TQ = 2, 112
NT = B * QT
PAIRS = HEADS // 2
XC, CC = D // P, CD // P
KH, KHP = CTX // 2, CTX // 2 + 1
ORG = KH - 2
KC, KCN = 125, 6
VG, VH = 4, 4
E, F = 8, 768
FC = F // P
GROUPS = 8 + 3 * PAIRS + KCN * VG
STEP = P
TOKENS = B * N
MINSTEPS = 2
MAXSTEPS = 2 * TOKENS // STEP + MINSTEPS * E
KMAX = -(-TOKENS // STEP)
ROOM = MAXSTEPS + KMAX + 1


def prepare(nc, dram, const):
    wq_h, wq_l, wk_h, wk_l, wv_h, wv_l, ident, kipa, rstd, mean = (
        const[k] for k in ("wq_h", "wq_l", "wk_h", "wk_l", "wv_h", "wv_l", "ident", "kipa", "rstd", "mean"))
    with ExitStack() as ctx:
        def sb(name, shape, dt=F32):
            return ctx.enter_context(nc.sbuf_tensor(name, shape, dt))

        def sem(name):
            return ctx.enter_context(nc.semaphore(name))

        DC = XC + 2 * CC
        raw = {"q": sb("wq_raw", [P, XC, ID]), "k": sb("wk_raw", [P, CC, ID]), "v": sb("wv_raw", [P, CC, ID])}
        split = {"q": (wq_h, wq_l), "k": (wk_h, wk_l), "v": (wv_h, wv_l)}
        down = sb("down", [P, DC, RANK])
        down_h = sb("down_h", [P, DC, RANK], F32R)
        down3 = sb("down3", [P, DC, 3, RANK])
        downT = sb("downT", [3 * RANK, DC, P], F32R)
        up = sb("up", [RANK, 3, ID])
        up3 = sb("up3", [3 * RANK, 3, ID], F32R)
        alpha = sb("alpha", [P, 3])
        alpha_r = sb("alpha_r", [P, 3])
        wki = sb("wk_ipa", [P, CC, ID])
        wvi = sb("wv_ipa", [P, CC, ID])
        ictx = sb("ipa_ctx", [B * IPA, CD])
        ictxT = sb("ipa_ctxT", [P, CC, B * IPA])
        vipa_h = sb("vipa_h", [B * IPA, HEADS, DH], F32R)
        vipa = sb("vipa", [B * IPA, HEADS, 2 * DH])
        q_space, k_space = raw["q"][0:TQ].rearrange("p c (h d) -> p (c h) d", d=D), raw["k"][0:TQ].rearrange("p c (h d) -> p (c h) d", d=D)
        xb = [sb("x_stat", [TQ, 4, D])[:], q_space[:, 0:4], q_space[:, 4:8], k_space[:, 0:4]]
        bn = sb("bn", [TQ, NT, 6])
        mv = sb("mv", [TQ, NT, 2])
        eps = sb("eps", [TQ, 1])
        std = sb("std", [TQ, NT])
        ones = sb("ones_sq", [P, P])
        ps_down = ctx.enter_context(nc.psum_tensor("ps_down", [3 * RANK, 12, P], F32))
        ps_w = ctx.enter_context(nc.psum_tensor("ps_w", [P, 2, 512], F32))
        ps_i = ctx.enter_context(nc.psum_tensor("ps_i", [P, 512], F32))
        ps_v = ctx.enter_context(nc.psum_tensor("ps_v", [B * IPA, 2, 512], F32))

        small_loaded = sem("small_loaded")
        up_loaded = [sem(f"up{k}_loaded") for k in "kqv"]
        down_high = sem("down_high")
        down_split = sem("down_split")
        up_high = sem("up_high")
        up_split = sem("up_split")
        w_loaded = {k: sem(f"w{k}_loaded") for k in "qkv"}
        ipa_loaded = sem("ipa_loaded")
        x_loaded = [sem(f"xstat{i}_loaded") for i in range(4)]
        stats_done = sem("stats_done")
        ident_done = sem("ident_done")
        down_turned = sem("down_turned")
        down_copied = sem("down_copied")
        lora_done = sem("lora_done")
        eff_done = sem("eff_done")
        high_done = sem("high_done")
        q_split = sem("q_split")
        low_done = sem("low_done")
        ictx_turned = sem("ictx_turned")
        ictx_copied = sem("ictx_copied")
        kipa_done = sem("kipa_done")
        vipa_done = sem("vipa_done")
        kipa_h = sem("kipa_h_done")
        vipa_hd = sem("vipa_h_done")
        vipa_stored = sem("vipa_stored")
        aggr_done = sem("aggr_done")
        std_done = sem("std_done")
        prep_done = sem("prep_done")
        bn_done = sem("bn_done")
        pieces = [("k", c, n, XC + c, 1.0, 1) for c in range(CC) for n in range(2)]
        pieces += [("q", c, n, c, SCALE, 0) for c in range(XC) for n in range(2)]
        pieces += [("v", c, n, XC + CC + c, 1.0, 2) for c in range(CC) for n in range(2)]
        block = ctx.enter_context(nc.Block())

        @block.sync
        def _(sp):
            def load_weights(k):
                sp.dma_start(raw[k][:], dram[f"W{k}"].rearrange("(c p) n -> p c n", p=P)).then_inc(w_loaded[k], 16)

            def load_x(i):
                sp.dma_start(xb[i].rearrange("p (b t) d -> p b t d", t=QT),
                             dram["x_pq"].rearrange("b p t d -> p b t d")[:, 2 * i:2 * i + 2]).then_inc(x_loaded[i], 16)

            load_weights("k")
            for b in range(B):
                sp.dma_start(ictx[b * IPA:(b + 1) * IPA, :], dram["ctx"][b, CTX - IPA:CTX, :]).then_inc(ipa_loaded, 16)
            sp.dma_start(wki[:], dram["Wk_ipa"].rearrange("(c p) n -> p c n", p=P)).then_inc(ipa_loaded, 16)
            sp.dma_start(wvi[:], dram["Wv_ipa"].rearrange("(c p) n -> p c n", p=P)).then_inc(ipa_loaded, 16)
            load_x(0)
            load_weights("q")
            load_weights("v")
            sp.wait_ge(q_split, 2 * XC)
            sp.wait_ge(low_done, 2 * CC)
            for i in range(1, 4):
                load_x(i)
            sp.wait_ge(prep_done, 3)
            sp.dma_start(dram["vipa"], vipa[:].rearrange("p h d -> p (h d)")).then_inc(vipa_stored, 16)
            sp.wait_ge(vipa_stored, 16)

        @block.gpsimd
        def _(pool):
            nc.gpsimd.memset(ones[:], 1.0).then_inc(ident_done, 1)
            pool.wait_ge(ident_done, 1)
            nc.gpsimd.affine_select(out=ident[:], in_=ones[:], compare_op=ALU.is_equal, fill=0.0, base=0,
                                    pattern=[[-1, P]], channel_multiplier=1).then_inc(ident_done, 1)
            for i, (k, c, n, _, s, _) in enumerate(pieces):
                if k != "q":
                    pool.wait_ge(high_done, i + 1)
                    at = (slice(None), c, slice(n * 512, n * 512 + 512))
                    nc.gpsimd.tensor_tensor(split[k][1][at], raw[k][at], split[k][0][at].bitcast(F32), ALU.subtract).then_inc(low_done, 1)

        @block.scalar
        def _(act):
            for k, c0, n, j in (("k", XC, CC, 1), ("q", 0, XC, 0), ("v", XC + CC, CC, 2)):
                act.dma_start(down[:, c0:c0 + n, :], dram[f"{k}_down"].rearrange("(c p) r -> p c r", p=P)).then_inc(small_loaded, 16)
                act.dma_start(alpha[:, j:j + 1], dram[f"{k}_alpha"].rearrange("(a o) -> a o", o=1).to_broadcast((P, 1))).then_inc(small_loaded, 16)
                act.dma_start(up[:, j, :], dram[f"{k}_up"]).then_inc(up_loaded["kqv".index(k)], 16)
            act.wait_ge(small_loaded, 6 * 16)
            nc.scalar.copy(down_h[:], down[:]).then_inc(down_high, 1)
            def image_highs():
                act.wait_ge(kipa_done, 1)
                nc.scalar.copy(kipa[:, :, 0, :], ps_i[:, 0:PAIRS * B * IPA].rearrange("p (s j) -> p s j", s=PAIRS)).then_inc(kipa_h, 1)
                act.wait_ge(vipa_done, 1)
                nc.scalar.copy(vipa_h[:], ps_v[:].rearrange("p n (h d) -> p (n h) d", d=DH)).then_inc(vipa_hd, 1)

            def up_highs(i, j):
                act.wait_ge(up_loaded[i], 16)
                for r in range(2):
                    last = nc.scalar.copy(up3[r * RANK:(r + 1) * RANK, j], up[:, j])
                last.then_inc(up_high, 1)

            up_highs(0, 1)
            act.wait_ge(down_turned, 1)
            nc.scalar.copy(downT[:], ps_down[:, 0:DC, :]).then_inc(down_copied, 1)
            up_highs(1, 0)
            up_highs(2, 2)
            for i, (k, c, n, _, s, _) in enumerate(pieces):
                act.wait_ge(eff_done, i + 1)
                nc.scalar.activation(split[k][0][:, c, n * 512:n * 512 + 512], raw[k][:, c, n * 512:n * 512 + 512],
                                     ACT.Copy, scale=s).then_inc(high_done, 1)
                if i == 2 * CC - 1:
                    image_highs()
            act.wait_ge(aggr_done, NT + 1)
            nc.scalar.activation(std[:], mv[:, :, 1], ACT.Sqrt, bias=eps[:, 0:1]).then_inc(std_done, 1)

        @block.vector
        def _(dve):
            nc.vector.memset(eps[:], EPS).then_inc(aggr_done, 1)
            dve.wait_ge(small_loaded, 6 * 16)
            nc.vector.tensor_scalar(alpha_r[:], alpha[:], 1.0 / RANK, None, ALU.mult).then_inc(stats_done, 1)
            dve.wait_ge(down_high, 1)
            nc.vector.tensor_copy(down3[:, :, 0], down_h[:].bitcast(F32))
            nc.vector.tensor_tensor(down3[:, :, 1], down[:], down_h[:].bitcast(F32), ALU.subtract)
            nc.vector.tensor_copy(down3[:, :, 2], down_h[:].bitcast(F32)).then_inc(down_split, 1)

            def up_low(i, j):
                dve.wait_ge(up_high, i + 1)
                nc.vector.tensor_tensor(up3[2 * RANK:3 * RANK, j], up[:, j], up3[0:RANK, j].bitcast(F32), ALU.subtract).then_inc(up_split, 1)

            up_low(0, 1)
            dve.wait_ge(stats_done, 1)

            def low(i):
                k, c, n, _, s, _ = pieces[i]
                if k == "q":
                    at = (slice(None), c, slice(n * 512, n * 512 + 512))
                    dve.wait_ge(high_done, i + 1)
                    nc.vector.scalar_tensor_tensor(out=split[k][1][at], in0=raw[k][at], scalar=s, in1=split[k][0][at].bitcast(F32),
                                                   op0=ALU.mult, op1=ALU.subtract).then_inc(q_split, 1)

            def stats(i):
                dve.wait_ge(x_loaded[i], 16)
                for n in range(4 * i, 4 * i + 4):
                    nc.vector.bn_stats(bn[:, n], xb[i][:, n % 4]).then_inc(bn_done, 1)

            def image_parts():
                up_low(1, 0)
                up_low(2, 2)
                dve.wait_ge(ictx_turned, 1)
                nc.vector.tensor_copy(ictxT[:], ps_i[:, 0:CC * B * IPA].rearrange("p (c j) -> p c j", c=CC)).then_inc(ictx_copied, 1)
                dve.wait_ge(kipa_h, 1)
                nc.vector.tensor_tensor(kipa[:, :, 1, :], ps_i[:, 0:PAIRS * B * IPA].rearrange("p (s j) -> p s j", s=PAIRS),
                                        kipa[:, :, 0, :].bitcast(F32), ALU.subtract).then_inc(prep_done, 1)
                stats(0)
                dve.wait_ge(vipa_hd, 1)
                nc.vector.tensor_copy(vipa[:, :, 0:DH], vipa_h[:].bitcast(F32)).then_inc(prep_done, 1)
                nc.vector.tensor_tensor(vipa[:, :, DH:2 * DH], ps_v[:].rearrange("p n (h d) -> p (n h) d", d=DH),
                                        vipa_h[:].bitcast(F32), ALU.subtract).then_inc(prep_done, 1)

            for i, (k, c, n, _, s, j) in enumerate(pieces):
                w = raw[k][:, c, n * 512:n * 512 + 512]
                if i == 2 * CC:
                    image_parts()
                if c == 0 and n == 0:
                    dve.wait_ge(w_loaded[k], 16)
                dve.wait_ge(lora_done, i + 1)
                nc.vector.scalar_tensor_tensor(out=w, in0=ps_w[:, i % 2, :], scalar=alpha_r[:, j:j + 1], in1=w,
                                               op0=ALU.mult, op1=ALU.add).then_inc(eff_done, 1)
                if i > 0:
                    low(i - 1)
            for i in range(1, 4):
                stats(i)
            dve.wait_ge(bn_done, NT)
            for n in range(NT):
                nc.vector.bn_aggr(mv[:, n, :], bn[:, n, :]).then_inc(aggr_done, 1)
            dve.wait_ge(aggr_done, NT + 1)
            nc.vector.tensor_copy(mean[:], mv[:, :, 0]).then_inc(prep_done, 1)
            dve.wait_ge(std_done, 1)
            nc.vector.reciprocal(rstd[:], std[:]).then_inc(prep_done, 1)

        @block.tensor
        def _(pe):
            pe.wait_ge(ident_done, 2)
            pe.wait_ge(down_split, 1)
            for c in range(DC):
                mm = nc.tensor.transpose(ps_down[:, c, :], down3[:, c].rearrange("p t r -> p (t r)"), ident[:])
            mm.then_inc(down_turned, 1)
            pe.wait_ge(down_copied, 1)

            def image_products():
                pe.wait_ge(ipa_loaded, (B + 2) * 16)
                for c in range(CC):
                    mm = nc.tensor.transpose(ps_i[:, c * B * IPA:(c + 1) * B * IPA], ictx[:, c * P:(c + 1) * P], ident[0:B * IPA, 0:B * IPA])
                mm.then_inc(ictx_turned, 1)
                pe.wait_ge(ictx_copied, 1)
                for s in range(PAIRS):
                    for c in range(CC):
                        mm = nc.tensor.matmul(ps_i[:, s * B * IPA:(s + 1) * B * IPA], wki[:, c, s * P:(s + 1) * P], ictxT[:, c, :],
                                              start=(c == 0), stop=(c == CC - 1))
                mm.then_inc(kipa_done, 1)
                for n in range(2):
                    for c in range(CC):
                        mm = nc.tensor.matmul(ps_v[:, n, :], ictxT[:, c, :], wvi[:, c, n * 512:n * 512 + 512],
                                              start=(c == 0), stop=(c == CC - 1))
                mm.then_inc(vipa_done, 1)

            for i, (k, c, n, dc, _, j) in enumerate(pieces):
                if i == 2 * CC:
                    image_products()
                if c == 0 and n == 0:
                    pe.wait_ge(up_split, "kqv".index(k) + 1)
                if i >= 2:
                    pe.wait_ge(eff_done, i - 1)
                nc.tensor.matmul(ps_w[:, i % 2, :], downT[:, dc, :], up3[:, j, n * 512:n * 512 + 512],
                                 start=True, stop=True).then_inc(lora_done, 1)


def batch_schedule():
    prep = [("ctx", c) for c in range(KCN)] + [("x", q) for q in range(QT)]
    pair = lambda s: [("k", s, 0), ("k", s, 1), ("q", s)]
    values = lambda g: [("v", g, c) for c in range(KCN)]
    own = prep + pair(0) + values(0) + pair(1)[:1]
    prologue = list(enumerate(own))
    rest = pair(1)[1:]
    for s in range(2, PAIRS):
        rest += values(s // 2)[(s % 2) * 3:(s % 2) * 3 + 3] + pair(s)
    rest = list(enumerate(rest, len(own)))
    assert len(own) + len(rest) == GROUPS
    per_head = [rest[3 * k:3 * k + 3] for k in range(HEADS)]
    after = {13: prologue[:8], 14: prologue[8:13], 15: prologue[13:]}
    return prologue, per_head, after


def attend(nc, dram, const):
    wq_h, wq_l, wk_h, wk_l, wv_h, wv_l, ident, kipa, rstd, mean = (
        const[k] for k in ("wq_h", "wq_l", "wk_h", "wk_l", "wv_h", "wv_l", "ident", "kipa", "rstd", "mean"))
    with ExitStack() as ctx:
        def sb(name, shape, dt=F32):
            return ctx.enter_context(nc.sbuf_tensor(name, shape, dt))

        def psum(name, shape):
            return ctx.enter_context(nc.psum_tensor(name, shape, F32))

        def sem(name):
            return ctx.enter_context(nc.semaphore(name))

        x_raw = sb("x_raw", [TQ, QT, D])
        xT = [sb(f"xT_{p}", [P, XC, N], F32R) for p in "hl"]
        ctx_raw = sb("ctx_raw", [KC, KCN, CD])
        ctxT = [sb(f"ctxT_{p}", [P, CC, 2, KHP], F32R) for p in "hl"]
        K = sb("K", [P, 2, 2, 2, KHP], F32R)
        Q = sb("Q", [P, 2, 2, 2, N], F32R)
        V = sb("V", [KC, 2, KCN, VH, 2 * DH], F32R)
        vipa = sb("vipa_rows", [2, 2, VH * 2 * DH])
        prob = sb("prob", [TQ, 2, QT, 2, KHP])
        pT = [sb(f"pT_{p}", [KC, 2, KCN, N], F32R) for p in "hl"]
        nmax = sb("nmax", [TQ, 2, QT, 2])
        sums = sb("sums", [TQ, 2, QT, 2])
        rsum = sb("rsum", [TQ, 2, QT, 2])
        one = sb("one", [2, 1])
        zero = sb("zero", [P, D // 2])
        low_o = sb("low_o", [DH, 2, N])
        oT = sb("oT", [P, 2, N])
        ps_s = psum("ps_s", [TQ, QT, 2, 512])
        ps_t = psum("ps_t", [P, 512])
        ps_o = psum("ps_o", [P, 512])
        banks = psum("ps_g", [P, 2, 512])

        x_loaded = sem("x_loaded")
        ctx_loaded = [sem(f"ctx_half{h}_loaded") for h in range(2)]
        x_normed = sem("x_normed")
        vipa_loaded = sem("vipa_loaded")
        vipa_used = sem("vipa_used")
        zeroed = sem("zeroed")
        pads_cleared = sem("pads_cleared")
        q_cleared = sem("q_cleared")
        cleared = sem("cleared")
        group_ready = sem("group_ready")
        group_high = sem("group_high")
        group_done = sem("group_done")
        kipa_ready = sem("kipa_ready")
        scores_ready = sem("scores_ready")
        max_ready = sem("max_ready")
        exp_done = sem("exp_done")
        rsum_ready = sem("rsum_ready")
        prob_ready = sem("prob_ready")
        turned = sem("turned")
        turned_high = sem("turned_high")
        turned_done = sem("turned_done")
        out_ready = sem("out_ready")
        out_low = sem("out_low")
        out_done = sem("out_done")
        out_stored = [sem(f"out_stored{i}") for i in range(2)]

        prologue, per_head, after = batch_schedule()
        block = ctx.enter_context(nc.Block())

        def group_no(b, n, ahead):
            return b * GROUPS + (n + GROUPS * ahead)

        def scores_unit(b, k, q):
            return b * HEADS * QT + (k * QT + q)

        def iteration(b, k, last):
            todo, ahead = (per_head[k], 0) if per_head[k] else (after[k], 1)
            return ([] if last and ahead else todo), ahead, (k + 1 < HEADS or not last), ((b, k + 1) if k + 1 < HEADS else (b + 1, 0))

        def places(todo):
            sizes = {0: (0, 0, 0, 0, 0, 0), 2: (0, 0, 1, 0, 1, 0), 3: (0, 0, 1, 0, 1, 1), 5: (0, 0, 2, 0, 1, 2), 8: (1, 1, 1, 1, 2, 2)}[len(todo)]
            return [todo[sum(sizes[:i]):sum(sizes[:i + 1])] for i in range(6)]

        def each_batch(engine, first, body):
            first()
            with engine.Fori(0, B - 1) as b:
                body(b, False)
            body(B - 1, True)

        @block.sync
        def _(sp):
            def load_ctx(b):
                src = dram["ctx"][b] if isinstance(b, int) else dram["ctx"][bass.ds(b, 1)].rearrange("o k d -> (o k) d")
                for h in range(2):
                    t0 = h * ORG
                    c0 = 3 * h
                    sp.dma_start(ctx_raw[0:2, c0, :], src[CTX - IPA + 2 * h:CTX - IPA + 2 * h + 2, :]).then_inc(ctx_loaded[h], 16)
                    sp.dma_start(ctx_raw[2:KC, c0, :], src[t0:t0 + KC - 2, :]).then_inc(ctx_loaded[h], 16)
                    sp.dma_start(ctx_raw[:, c0 + 1:c0 + 3, :],
                                 src[t0 + KC - 2:t0 + ORG, :].rearrange("(c p) d -> p c d", p=KC)).then_inc(ctx_loaded[h], 16)

            def load_x(b):
                src = dram["x_pq"][b] if isinstance(b, int) else dram["x_pq"][bass.ds(b, 1)].rearrange("o p t d -> (o p) t d")
                sp.dma_start(x_raw[:], src).then_inc(x_loaded, 16)

            def load_vipa(b, g):
                src = dram["vipa"].rearrange("(b h j) n -> b j h n", h=2, j=2)
                src = src[b] if isinstance(b, int) else src[bass.ds(b, 1)].rearrange("o j h n -> (o j) h n")
                sp.dma_start(vipa[:], src[:, :, g * VH * 2 * DH:(g + 1) * VH * 2 * DH]).then_inc(vipa_loaded, 16)

            def store(b, s):
                sp.wait_ge(out_done, b * HEADS + (2 * s + 3))
                dst = dram["oT"][s * P:(s + 1) * P]
                dst = dst[:, b, :] if isinstance(b, int) else dst[:, bass.ds(b, 1), :].rearrange("p o n -> p (o n)")
                sp.dma_start(dst, oT[:, s % 2, :]).then_inc(out_stored[s % 2], 16)

            def first():
                for i in range(2):
                    sp.sem_inc(out_stored[i], 16)
                load_ctx(0)
                load_x(0)
                load_vipa(0, 0)
                sp.wait_ge(cleared, 2)
                slots = dram["slots"].rearrange("(p s) (h d) -> p (s h) d", p=P, h=2)
                sp.dma_start(slots, zero[:].rearrange("p (o d) -> p o d", o=1).to_broadcast((P, ROOM * STEP // P * 2, D // 2))).then_inc(zeroed, 16)

            def body(b, last):
                for s in range(PAIRS):
                    if s in (0, 2, 4):
                        g = s // 2 + 1
                        sp.wait_ge(vipa_used, b * VG + g)
                        load_vipa(b, g)
                    if s == 1 and not last:
                        sp.wait_ge(group_ready, group_no(b, KCN + QT, 0))
                        load_ctx(b + 1)
                        load_x(b + 1)
                    if s == 6 and not last:
                        sp.wait_ge(vipa_used, b * VG + VG)
                        load_vipa(b + 1, 0)
                    store(b, s)

            each_batch(sp, first, body)
            for i in range(2):
                sp.wait_ge(out_stored[i], 16 * B * PAIRS // 2 + 16)
            sp.wait_ge(zeroed, 16)

        @block.gpsimd
        def _(pool):
            for p in range(2):
                nc.gpsimd.memset(ctxT[p][:, :, :, KH:KHP].bitcast(F32), 0.0).then_inc(pads_cleared, 1)
            nc.gpsimd.memset(one[:], 1.0).then_inc(cleared, 1)
            nc.gpsimd.memset(zero[:], 0.0).then_inc(cleared, 1)

            def kipa_columns(b, n, s, ahead):
                pool.wait_ge(group_ready, group_no(b, n + 1, ahead))
                j0 = b * IPA + ahead * IPA
                src = kipa[:, s, :, bass.ds(j0, IPA)] if not isinstance(j0, int) else kipa[:, s, :, j0:j0 + IPA]
                nc.gpsimd.tensor_copy(K[:, s % 2, :, :, 0:2],
                                      src.bitcast(F32).rearrange("p l (h j) -> p l h j", h=2)).then_inc(kipa_ready, 1)

            def vipa_rows(b, n, g, ahead):
                pool.wait_ge(group_done, group_no(b, n + 1, ahead))
                pool.wait_ge(vipa_loaded, 16 * (b * VG + (g + ahead * VG + 1)))
                nc.gpsimd.tensor_tensor(V[0:2, g % 2, 0:4:3].rearrange("p c h d -> p c (h d)"), vipa[:],
                                        one[:].rearrange("p (o u) -> p o u", o=1).to_broadcast((2, 2, VH * 2 * DH)), ALU.mult).then_inc(vipa_used, 1)

            def normalise(b, k, q):
                pool.wait_ge(rsum_ready, scores_unit(b, k, q) + 1)
                p = prob[:, k % 2, q]
                nc.gpsimd.tensor_tensor(p[:, :, 0:2], p[:, :, 0:2], rsum[:, k % 2, q, 1:2].rearrange("p (o u) -> p o u", o=1).to_broadcast((TQ, 2, 2)), ALU.mult)
                nc.gpsimd.tensor_scalar(p[:, :, 2:KH], p[:, :, 2:KH], rsum[:, k % 2, q, 0:1], 1.0, ALU.mult, ALU.mult).then_inc(prob_ready, 1)

            def keys(b, todo, ahead):
                for n, what in todo:
                    if what[0] == "k" and what[2] == 0:
                        kipa_columns(b, n, what[1], ahead)

            def value_rows(b, todo, ahead):
                for n, what in todo:
                    if what[0] == "v" and what[2] == KCN - 1:
                        vipa_rows(b, n, what[1], ahead)

            def first():
                pool.wait_ge(cleared, 2)
                keys(0, prologue, 0)
                value_rows(0, prologue, 0)
                for q in range(QT):
                    normalise(0, 0, q)

            def body(b, last):
                for k in range(HEADS):
                    todo, ahead, more, nxt = iteration(b, k, last)
                    if more:
                        for q in range(QT):
                            normalise(*nxt, q)
                    value_rows(b, todo, ahead)
                    keys(b, todo, ahead)

            each_batch(pool, first, body)

        @block.scalar
        def _(act):
            def high(b, todo, ahead):
                for n, what in todo:
                    ps_g = banks[:, n % 2]
                    act.wait_ge(group_ready, group_no(b, n + 1, ahead))
                    if what[0] == "ctx":
                        c = what[1]
                        last = nc.scalar.copy(ctxT[0][:, :, c // 3, c % 3 * KC:(c % 3 + 1) * KC], ps_g[:, 0:CC * KC].rearrange("p (c k) -> p c k", c=CC))
                    elif what[0] == "x":
                        q = what[1]
                        last = nc.scalar.copy(xT[0][:, :, q * TQ:(q + 1) * TQ], ps_g[:, 0:XC * TQ].rearrange("p (c k) -> p c k", c=XC))
                    elif what[0] == "k":
                        s, h = what[1:]
                        last = nc.scalar.copy(K[:, s % 2, 0, h, 2:KHP], ps_g[:, 2:KHP])
                    elif what[0] == "q":
                        s = what[1]
                        nc.scalar.copy(Q[0:DH, s % 2, 0, 0, :], ps_g[0:DH, 0:N])
                        last = nc.scalar.copy(Q[DH:P, s % 2, 0, 1, :], ps_g[DH:P, 0:N])
                    else:
                        g, c = what[1:]
                        last = nc.scalar.copy(V[:, g % 2, c, :, 0:DH], ps_g[0:KC, 0:VH * DH].rearrange("p (h d) -> p h d", d=DH))
                    last.then_inc(group_high, 1)

            def exponentials(b, k, q):
                act.wait_ge(max_ready, scores_unit(b, k, q) + 1)
                for i, (a, e) in enumerate(((2, KH), (0, 2))):
                    last = nc.scalar.activation(prob[:, k % 2, q, :, a:e], ps_s[:, q, :, a:e], ACT.Exp,
                                                bias=nmax[:, k % 2, q, i:i + 1], accum_out=sums[:, k % 2, q, i:i + 1])
                last.then_inc(exp_done, 1)

            def out_part(b, k):
                act.wait_ge(out_ready, b * HEADS + (k + 1))
                nc.scalar.copy(low_o[:, k % 2, :], ps_o[DH:P, 0:N]).then_inc(out_low, 1)

            def turned_part(b, k, j):
                act.wait_ge(turned, b * HEADS * 3 + (k * 3 + j + 1))
                nc.scalar.copy(pT[0][:, k % 2, 2 * j:2 * j + 2, :].rearrange("p c n -> p (c n)"), ps_t[0:KC, 0:2 * N]).then_inc(turned_high, 1)

            def first():
                act.wait_ge(pads_cleared, 2)
                act.wait_ge(q_cleared, 1)
                high(0, prologue, 0)
                exponentials(0, 0, 0)
                exponentials(0, 0, 1)

            def body(b, last):
                for k in range(HEADS):
                    todo, ahead, more, nxt = iteration(b, k, last)
                    at = places(todo)
                    turned_part(b, k, 0)
                    high(b, at[0] + at[1], ahead)
                    if more:
                        exponentials(*nxt, 0)
                    turned_part(b, k, 1)
                    if more:
                        exponentials(*nxt, 1)
                    high(b, at[2], ahead)
                    if k > 0:
                        out_part(b, k - 1)
                    high(b, at[3], ahead)
                    turned_part(b, k, 2)
                    high(b, at[4] + at[5], ahead)
                out_part(b, HEADS - 1)

            each_batch(act, first, body)

        @block.vector
        def _(dve):
            def norm_x(b):
                dve.wait_ge(x_loaded, 16 * b + 16)
                for q in range(QT):
                    i = b * QT + q
                    m = mean[:, i:i + 1] if isinstance(i, int) else mean[:, bass.ds(i, 1)]
                    r = rstd[:, i:i + 1] if isinstance(i, int) else rstd[:, bass.ds(i, 1)]
                    last = nc.vector.tensor_scalar(x_raw[:, q, :], x_raw[:, q, :], m, r, ALU.subtract, ALU.mult)
                last.then_inc(x_normed, 1)

            def low(b, todo, ahead):
                for n, what in todo:
                    ps_g = banks[:, n % 2]
                    dve.wait_ge(group_high, group_no(b, n + 1, ahead))
                    if what[0] == "ctx":
                        c = what[1]
                        at = (slice(None), slice(None), c // 3, slice(c % 3 * KC, (c % 3 + 1) * KC))
                        last = nc.vector.tensor_tensor(ctxT[1][at], ps_g[:, 0:CC * KC].rearrange("p (c k) -> p c k", c=CC), ctxT[0][at].bitcast(F32), ALU.subtract)
                    elif what[0] == "x":
                        q = what[1]
                        last = nc.vector.tensor_tensor(xT[1][:, :, q * TQ:(q + 1) * TQ], ps_g[:, 0:XC * TQ].rearrange("p (c k) -> p c k", c=XC),
                                                       xT[0][:, :, q * TQ:(q + 1) * TQ].bitcast(F32), ALU.subtract)
                    elif what[0] == "k":
                        s, h = what[1:]
                        last = nc.vector.tensor_tensor(K[:, s % 2, 1, h, 2:KHP], ps_g[:, 2:KHP], K[:, s % 2, 0, h, 2:KHP].bitcast(F32), ALU.subtract)
                    elif what[0] == "q":
                        s = what[1]
                        for i, r in enumerate((slice(0, DH), slice(DH, P))):
                            last = nc.vector.tensor_tensor(Q[r, s % 2, 1, i, :], ps_g[r, 0:N], Q[r, s % 2, 0, i, :].bitcast(F32), ALU.subtract)
                    else:
                        g, c = what[1:]
                        last = nc.vector.tensor_tensor(V[:, g % 2, c, :, DH:2 * DH], ps_g[0:KC, 0:VH * DH].rearrange("p (h d) -> p h d", d=DH),
                                                       V[:, g % 2, c, :, 0:DH].bitcast(F32), ALU.subtract)
                    last.then_inc(group_done, 1)

            def maxima(b, k, q):
                dve.wait_ge(scores_ready, scores_unit(b, k, q) + 1)
                for i, (a, e) in enumerate(((2, KH), (0, 2))):
                    last = nc.vector.tensor_reduce(nmax[:, k % 2, q, i:i + 1], ps_s[:, q, :, a:e], AX.XY, ALU.max, negate=True)
                last.then_inc(max_ready, 1)

            def reciprocals(b, k, q):
                dve.wait_ge(exp_done, scores_unit(b, k, q) + 1)
                nc.vector.reciprocal(rsum[:, k % 2, q], sums[:, k % 2, q]).then_inc(rsum_ready, 1)

            def out_part(b, k):
                s = k // 2
                if k % 2 == 0:
                    dve.wait_ge(out_stored[s % 2], b * (16 * PAIRS // 2) + 16 * (s // 2 + 1))
                dve.wait_ge(out_low, b * HEADS + (k + 1))
                nc.vector.tensor_tensor(oT[k % 2 * DH:(k % 2 + 1) * DH, s % 2, :], ps_o[0:DH, 0:N], low_o[:, k % 2, :], ALU.add).then_inc(out_done, 1)

            def turned_part(b, k, j):
                dve.wait_ge(turned_high, b * HEADS * 3 + (k * 3 + j + 1))
                nc.vector.tensor_tensor(pT[1][:, k % 2, 2 * j:2 * j + 2, :].rearrange("p c n -> p (c n)"), ps_t[0:KC, 0:2 * N],
                                        pT[0][:, k % 2, 2 * j:2 * j + 2, :].rearrange("p c n -> p (c n)").bitcast(F32), ALU.subtract).then_inc(turned_done, 1)

            def first():
                dve.sem_inc(out_done, 1)
                nc.vector.memset(Q[:].bitcast(F32), 0.0).then_inc(q_cleared, 1)
                norm_x(0)
                low(0, prologue, 0)
                for q in range(QT):
                    maxima(0, 0, q)
                for q in range(QT):
                    reciprocals(0, 0, q)

            def body(b, last):
                for k in range(HEADS):
                    todo, ahead, more, nxt = iteration(b, k, last)
                    at = places(todo)
                    turned_part(b, k, 0)
                    low(b, at[0], ahead)
                    if more:
                        maxima(*nxt, 0)
                    low(b, at[1], ahead)
                    if more:
                        maxima(*nxt, 1)
                        reciprocals(*nxt, 0)
                    turned_part(b, k, 1)
                    if more:
                        reciprocals(*nxt, 1)
                    low(b, at[2], ahead)
                    if k > 0:
                        out_part(b, k - 1)
                    low(b, at[3], ahead)
                    turned_part(b, k, 2)
                    low(b, at[4] + at[5], ahead)
                    if k == 11 and not last:
                        norm_x(b + 1)
                out_part(b, HEADS - 1)

            each_batch(dve, first, body)

        @block.tensor
        def _(pe):
            passes = ((0, 0), (1, 0), (0, 1))

            def project(b, todo, ahead):
                for n, what in todo:
                    ps_g = banks[:, n % 2]
                    if not (isinstance(b, int) and b == 0 and n < 2):
                        pe.wait_ge(group_done, group_no(b, n - 1, ahead))
                    if what[0] == "ctx":
                        c = what[1]
                        if c % 3 == 0:
                            pe.wait_ge(ctx_loaded[c // 3], 48 * b + 48 * (1 + ahead))
                        for j in range(CC):
                            mm = nc.tensor.transpose(ps_g[:, j * KC:(j + 1) * KC], ctx_raw[:, c, j * P:(j + 1) * P], ident[0:KC, 0:KC])
                    elif what[0] == "x":
                        q = what[1]
                        if q == 0:
                            pe.wait_ge(x_normed, b + (1 + ahead))
                        for j in range(XC):
                            mm = nc.tensor.transpose(ps_g[:, j * TQ:(j + 1) * TQ], x_raw[:, q, j * P:(j + 1) * P], ident[0:TQ, 0:TQ])
                    elif what[0] == "k":
                        s, h = what[1:]
                        w = (wk_h, wk_l)
                        for i, (c, (a, m)) in enumerate((c, p) for c in range(CC) for p in passes):
                            mm = nc.tensor.matmul(ps_g[:, 0:KHP], w[a][:, c, s * P:(s + 1) * P], ctxT[m][:, c, h, :], start=(i == 0), stop=(i == 3 * CC - 1))
                    elif what[0] == "q":
                        s = what[1]
                        w = (wq_h, wq_l)
                        for i, (c, (a, m)) in enumerate((c, p) for c in range(XC) for p in passes):
                            mm = nc.tensor.matmul(ps_g[:, 0:N], w[a][:, c, s * P:(s + 1) * P], xT[m][:, c, :], start=(i == 0), stop=(i == 3 * XC - 1))
                    else:
                        g, kc = what[1:]
                        w = (wv_h, wv_l)
                        for i, (c, (a, m)) in enumerate((c, p) for c in range(CC) for p in passes):
                            mm = nc.tensor.matmul(ps_g[0:KC, 0:VH * DH], ctxT[a][:, c, kc // 3, kc % 3 * KC:(kc % 3 + 1) * KC],
                                                  w[m][:, c, g * VH * DH:(g + 1) * VH * DH], start=(i == 0), stop=(i == 3 * CC - 1))
                    mm.then_inc(group_ready, 1)

            def score(b, k, q, first=False):
                s = k // 2
                if k % 2 == 0 and q == 0:
                    n = 11 if s == 0 else next(n for n, w in per_head[2 * s - 2] if w[0] == "q") + 1
                    pe.wait_ge(group_done, group_no(b, n, 0))
                    pe.wait_ge(kipa_ready, b * PAIRS + (s + 1))
                if not first:
                    pe.wait_ge(exp_done, scores_unit(b, k, q) - 1)
                for h in range(2):
                    for i, (a, m) in enumerate(passes):
                        mm = nc.tensor.matmul(ps_s[:, q, h, 0:KHP], Q[:, s % 2, a, k % 2, q * TQ:(q + 1) * TQ], K[:, s % 2, m, h, :],
                                              start=(i == 0), stop=(i == 2))
                mm.then_inc(scores_ready, 1)

            def turn(b, k, j):
                if j == 0:
                    pe.wait_ge(prob_ready, scores_unit(b, k, 1) + 1)
                if k > 0 or j > 0:
                    pe.wait_ge(turned_done, b * HEADS * 3 + (k * 3 + j))
                for c in range(2 * j, 2 * j + 2):
                    for q in range(QT):
                        o = (c - 2 * j) * N + q * TQ
                        mm = nc.tensor.transpose(ps_t[0:KC, o:o + TQ],
                                                 prob[:, k % 2, q, c // 3, c % 3 * KC:(c % 3 + 1) * KC], ident[0:TQ, 0:TQ])
                mm.then_inc(turned, 1)

            def values(b, k):
                pe.wait_ge(turned_done, b * HEADS * 3 + 3 * (k + 1))
                if k % VH == 0:
                    pe.wait_ge(vipa_used, b * VG + (k // VH + 1))
                pe.wait_ge(out_done, b * HEADS + (k + 1))
                for i, (c, m) in enumerate((c, m) for c in range(KCN) for m in range(2)):
                    mm = nc.tensor.matmul(ps_o[:, 0:N], V[:, k // VH % 2, c, k % VH, :], pT[m][:, k % 2, c, :], start=(i == 0), stop=(i == 2 * KCN - 1))
                mm.then_inc(out_ready, 1)

            def first():
                project(0, prologue, 0)
                score(0, 0, 0, True)
                score(0, 0, 1, True)

            def body(b, last):
                for k in range(HEADS):
                    todo, ahead, more, nxt = iteration(b, k, last)
                    at = places(todo)
                    turn(b, k, 0)
                    project(b, at[0], ahead)
                    if more:
                        score(*nxt, 0)
                    project(b, at[1], ahead)
                    if more:
                        score(*nxt, 1)
                    turn(b, k, 1)
                    project(b, at[2], ahead)
                    if k > 0:
                        values(b, k - 1)
                    project(b, at[3], ahead)
                    turn(b, k, 2)
                    project(b, at[4] + at[5], ahead)
                values(b, HEADS - 1)

            each_batch(pe, first, body)


PIECE = 2 * F
FC_PIECES, PIECES = XC, XC + FC * D // PIECE


def expert_weights(dram, stage, e):
    fc = dram["c_fc"].rearrange("e (c p) f -> e p c f", p=P)[bass.ds(e, 1)].rearrange("o p c f -> (o p) c f")
    proj = dram["c_proj"].rearrange("e (c p) d -> e p c d", p=P)[bass.ds(e, 1)].rearrange("o p c d -> (o p) c d")
    return ((stage[:, 0:FC_PIECES, :], fc),
            (stage[:, FC_PIECES:PIECES, :].rearrange("p h (c d) -> p (h c) d", d=D), proj))


def weight_piece(w1, w2, part, c):
    if c < FC_PIECES:
        return w1[:, part, c]
    h = (c - FC_PIECES) * (FC // 2)
    return w2[:, part, h:h + FC // 2].rearrange("p c d -> p (c d)")


def project(nc, dram, const):
    ident, logits, stage, xn_all = (const[k] for k in ("ident", "logits", "stage", "xn_all"))
    OC = ID // P
    with ExitStack() as ctx:
        def sb(name, shape, dt=F32):
            return ctx.enter_context(nc.sbuf_tensor(name, shape, dt))

        def psum(name, shape):
            return ctx.enter_context(nc.psum_tensor(name, shape, F32))

        def sem(name):
            return ctx.enter_context(nc.semaphore(name))

        wo = sb("wo_raw", [P, OC, D])
        wo_h = sb("wo_h", [P, OC, D], F32R)
        wo_l = sb("wo_l", [P, OC, D], F32R)
        down = sb("o_down_sb", [P, OC, RANK])
        down_h = sb("o_down_h", [P, OC, RANK], F32R)
        down3 = sb("o_down3", [P, OC, 3, RANK])
        downT = sb("o_downT", [3 * RANK, OC, P], F32R)
        up = sb("o_up_sb", [3 * RANK, D])
        up3 = sb("o_up3", [3 * RANK, D], F32R)
        alpha = sb("o_alpha_sb", [P, 2])
        bo = sb("bo_sb", [TQ, D])
        wg = sb("w_gate_sb", [P, XC, E])
        eps = sb("eps2", [TQ, 1])
        o_raw = sb("o_raw", [P, 2, OC, N])
        o_h = sb("o_h", [P, 2, QT, OC, TQ], F32R)
        o_l = sb("o_l", [P, 2, QT, OC, TQ], F32R)
        x_in = sb("x_in", [TQ, 2, QT, D])
        x2 = sb("x2_sb", [TQ, 2, QT, D])
        xn = sb("xn2_sb", [TQ, 2, QT, D])
        xnT = sb("xn2T", [P, QT, XC, TQ])
        bn = sb("bn2", [TQ, QT, 6])
        mv = sb("mv2", [TQ, QT, 2])
        std = sb("std2", [TQ, QT])
        rstd = sb("rstd2", [TQ, QT])
        ps_o = psum("ps_proj", [TQ, QT, 512])
        ps_t = psum("ps_xn2T", [P, QT, 512])
        ps_l = psum("ps_logits", [TQ, QT, 512])
        ps_w = psum("ps_wo", [P, 2, 512])

        small_loaded = sem("o_small_loaded")
        late_loaded = sem("o_late_loaded")
        wo_loaded = [sem(f"wo_loaded{i}") for i in range(2)]
        o_loaded = [sem(f"o_loaded{i}") for i in range(2)]
        x_loaded = [sem(f"x_in_loaded{i}") for i in range(2)]
        eps_set = sem("eps_set")
        small_high = sem("o_small_high")
        small_split = sem("o_small_split")
        down_turned = sem("o_down_turned")
        down_copied = sem("o_down_copied")
        lora_done = sem("o_lora_done")
        eff_done = sem("o_eff_done")
        high_done = sem("wo_high")
        low_done = sem("wo_low")
        o_high = sem("o_high")
        o_split = sem("o_split")
        projected = sem("projected")
        x2_partial = sem("x2_partial")
        x2_done = sem("x2_done")
        stats = sem("stats2")
        passed = sem("passed2")
        var_done = sem("var_done")
        std_done = sem("std2_done")
        rstd_done = sem("rstd2_done")
        xn_done = sem("xn2_done")
        xn_kept = [sem(f"xn2_kept{i}") for i in range(2)]
        w0_loaded = sem("w0_loaded")
        xn_turned = sem("xn2_turned")
        xn_copied = sem("xn2_copied")
        gated = sem("gated")
        logits_done = sem("logits_done")
        x2_stored = [sem(f"x2_stored{i}") for i in range(2)]
        block = ctx.enter_context(nc.Block())

        def pairs(engine, n, body):
            with engine.Fori(0, n) as two:
                body(two * 2 + 1, two, 1)
                body(two * 2 + 2, two + 1, 0)

        def rows(name, b):
            return dram[name][bass.ds(b, 1)].rearrange("o p t d -> (o p) t d")

        @block.sync
        def _(sp):
            sp.dma_start(down[:], dram["o_down"].rearrange("(c p) r -> p c r", p=P)).then_inc(small_loaded, 16)
            for r in range(3):
                sp.dma_start(up[r * RANK:(r + 1) * RANK, :], dram["o_up"]).then_inc(small_loaded, 16)
            sp.dma_start(alpha[:, 0:1], dram["o_alpha"].rearrange("(a o) -> a o", o=1).to_broadcast((P, 1))).then_inc(small_loaded, 16)
            def load_o(b, i):
                sp.dma_start(o_raw[:, i], dram["oT"].rearrange("(c p) b n -> p c b n", p=P)[:, :, bass.ds(b, 1), :].rearrange("p c o n -> p c (o n)")).then_inc(o_loaded[i], 16)

            def load_x(b, i):
                sp.dma_start(x_in[:, i], rows("x_pq", b)).then_inc(x_loaded[i], 16)

            load_o(0, 0)
            for i in range(2):
                h = slice(i * OC // 2, (i + 1) * OC // 2)
                sp.dma_start(wo[:, h], dram["Wo"].rearrange("(c p) n -> p c n", p=P)[:, h]).then_inc(wo_loaded[i], 16)
            load_x(0, 0)
            sp.dma_start(bo[:], dram["bo"].rearrange("(o d) -> o d", o=1).to_broadcast((TQ, D))).then_inc(late_loaded, 16)
            load_o(1, 1)
            load_x(1, 1)
            sp.dma_start(wg[:], dram["w_gate"].rearrange("(c p) e -> p c e", p=P)).then_inc(late_loaded, 16)
            sp.wait_ge(o_split, QT)
            load_o(2, 0)

            def batch(b, i, more_o=True, more_x=True):
                if more_o:
                    sp.wait_ge(o_split, b * QT + 2 * QT)
                    load_o(b + 3, 1 - i)
                sp.wait_ge(x2_done, b * QT + QT)
                sp.dma_start(rows("x2", b), x2[:, i]).then_inc(x2_stored[i], 16)
                if more_x:
                    load_x(b + 2, i)
                sp.wait_ge(xn_done, b * QT + QT)
                sp.dma_start(xn_all[:, bass.ds(b * QT, QT), :], xn[:, i]).then_inc(xn_kept[i], 16)

            batch(0, 0)
            for dst, src in expert_weights(dram, stage, 0):
                sp.dma_start(dst, src).then_inc(w0_loaded, 16)
            pairs(sp, 2, lambda b, h, i: batch(b, i))
            batch(B - 3, 1, more_o=False)
            batch(B - 2, 0, more_o=False, more_x=False)
            batch(B - 1, 1, more_o=False, more_x=False)
            for i in range(2):
                sp.wait_ge(x2_stored[i], 16 * B // 2)
                sp.wait_ge(xn_kept[i], 16 * B // 2)
            sp.wait_ge(w0_loaded, 2 * 16)

        @block.gpsimd
        def _(pool):
            pool.wait_ge(late_loaded, 2 * 16)
            with pool.Fori(0, B // 2) as two:
                for i in range(2):
                    pool.wait_ge(x_loaded[i], two * 16 + 16)
                    for q in range(QT):
                        nc.gpsimd.tensor_tensor(x_in[:, i, q], x_in[:, i, q], bo[:], ALU.add).then_inc(x2_partial, 1)

        @block.scalar
        def _(act):
            act.wait_ge(small_loaded, 5 * 16)
            nc.scalar.copy(down_h[:], down[:]).then_inc(small_high, 1)
            nc.scalar.copy(up3[:], up[:]).then_inc(small_high, 1)
            act.wait_ge(down_turned, 1)
            for i in range(2):
                last = nc.scalar.copy(downT[:, 4 * i:4 * i + 4], ps_w[0:3 * RANK, i].rearrange("r (c p) -> r c p", p=P))
            last.then_inc(down_copied, 1)
            def split(b, h, i):
                act.wait_ge(o_loaded[i], h * 16 + 16)
                for q in range(QT):
                    if not (isinstance(b, int) and b < 2):
                        act.wait_ge(projected, b * QT + (q - 2 * QT + 1))
                    nc.scalar.copy(o_h[:, i, q], o_raw[:, i, :, q * TQ:(q + 1) * TQ]).then_inc(o_high, 1)

            def turned_copy(b):
                for q in range(QT):
                    act.wait_ge(xn_turned, b * QT + (q + 1))
                    nc.scalar.copy(xnT[:, q], ps_t[:, q, 0:XC * TQ].rearrange("p (c t) -> p c t", c=XC)).then_inc(xn_copied, 1)

            def deviations(b):
                for q in range(QT):
                    act.wait_ge(var_done, b * QT + (q + 1))
                    nc.scalar.activation(std[:, q:q + 1], mv[:, q, 1:2], ACT.Sqrt, bias=eps[:, 0:1]).then_inc(std_done, 1)

            split(0, 0, 0)
            for c in range(OC):
                act.wait_ge(eff_done, c + 1)
                nc.scalar.copy(wo_h[:, c], wo[:, c]).then_inc(high_done, 1)
            split(1, 0, 1)
            deviations(0)

            def batch(b, h, i):
                split(b + 1, h + i, 1 - i)
                turned_copy(b - 1)
                deviations(b)

            pairs(act, B // 2 - 1, batch)
            turned_copy(B - 2)
            deviations(B - 1)
            turned_copy(B - 1)

        @block.vector
        def _(dve):
            nc.vector.memset(eps[:], EPS).then_inc(eps_set, 1)
            dve.wait_ge(small_loaded, 5 * 16)
            nc.vector.tensor_scalar(alpha[:, 1:2], alpha[:, 0:1], 1.0 / RANK, None, ALU.mult).then_inc(eps_set, 1)
            dve.wait_ge(small_high, 1)
            nc.vector.tensor_copy(down3[:, :, 0], down_h[:].bitcast(F32))
            nc.vector.tensor_tensor(down3[:, :, 1], down[:], down_h[:].bitcast(F32), ALU.subtract)
            nc.vector.tensor_copy(down3[:, :, 2], down_h[:].bitcast(F32)).then_inc(small_split, 1)
            dve.wait_ge(small_high, 2)
            r = slice(2 * RANK, 3 * RANK)
            nc.vector.tensor_tensor(up3[r], up[r], up3[r].bitcast(F32), ALU.subtract).then_inc(small_split, 1)
            dve.wait_ge(eps_set, 2)

            def split(b, i):
                for q in range(QT):
                    dve.wait_ge(o_high, b * QT + (q + 1))
                    nc.vector.tensor_tensor(o_l[:, i, q], o_raw[:, i, :, q * TQ:(q + 1) * TQ], o_h[:, i, q].bitcast(F32), ALU.subtract).then_inc(o_split, 1)

            def norm(b, h, i):
                for q in range(QT):
                    T = b * QT + q
                    dve.wait_ge(projected, T + 1)
                    dve.wait_ge(x2_partial, T + 1)
                    if q == 0 and not (isinstance(b, int) and b < 2):
                        dve.wait_ge(x2_stored[i], h * 16)
                        dve.wait_ge(xn_kept[i], h * 16)
                    nc.vector.tensor_tensor(x2[:, i, q], ps_o[:, q, :], x_in[:, i, q], ALU.add).then_inc(x2_done, 1)
                    dve.wait_ge(x2_done, T + 1)
                    nc.vector.bn_stats(bn[:, q], x2[:, i, q]).then_inc(stats, 1)
                    dve.wait_ge(stats, T + 1)
                    dve.sem_inc(passed, 1)
                    nc.vector.bn_aggr(mv[:, q], bn[:, q]).then_inc(var_done, 1)
                    dve.wait_ge(std_done, T + 1)
                    nc.vector.reciprocal(rstd[:, q:q + 1], std[:, q:q + 1]).then_inc(rstd_done, 1)
                    dve.wait_ge(rstd_done, T + 1)
                    nc.vector.tensor_scalar(xn[:, i, q], x2[:, i, q], mv[:, q, 0:1], rstd[:, q:q + 1], ALU.subtract, ALU.mult).then_inc(xn_done, 1)

            def keep_logits(b):
                for q in range(QT):
                    T = b * QT + q
                    dve.wait_ge(gated, T + 1)
                    nc.vector.tensor_copy(logits[:, bass.ds(T, 1), :].rearrange("p o e -> p (o e)"), ps_l[:, q, 0:E]).then_inc(logits_done, 1)

            split(0, 0)

            def low(c):
                dve.wait_ge(high_done, c + 1)
                nc.vector.tensor_tensor(wo_l[:, c], wo[:, c], wo_h[:, c].bitcast(F32), ALU.subtract).then_inc(low_done, 1)

            for c in range(OC):
                if c % (OC // 2) == 0:
                    dve.wait_ge(wo_loaded[c // (OC // 2)], 16)
                dve.wait_ge(lora_done, c + 1)
                nc.vector.scalar_tensor_tensor(out=wo[:, c], in0=ps_w[:, c % 2, :], scalar=alpha[:, 1:2], in1=wo[:, c],
                                               op0=ALU.mult, op1=ALU.add).then_inc(eff_done, 1)
                if c > 0:
                    low(c - 1)
            low(OC - 1)
            split(1, 1)
            norm(0, 0, 0)

            def batch(b, h, i):
                split(b + 1, 1 - i)
                norm(b, h, i)
                keep_logits(b - 1)

            split(2, 0)
            norm(1, 0, 1)
            keep_logits(0)
            with dve.Fori(1, B // 2 - 1) as two:
                batch(two * 2, two, 0)
                batch(two * 2 + 1, two, 1)
            batch(B - 2, B // 2 - 1, 0)
            norm(B - 1, B // 2 - 1, 1)
            keep_logits(B - 2)
            keep_logits(B - 1)

        @block.tensor
        def _(pe):
            pe.wait_ge(small_split, 1)
            for c in range(OC):
                mm = nc.tensor.transpose(ps_w[0:3 * RANK, c // 4, c % 4 * P:(c % 4 + 1) * P], down3[:, c].rearrange("p t r -> p (t r)"), ident[:])
            mm.then_inc(down_turned, 1)
            pe.wait_ge(small_split, 2)
            pe.wait_ge(down_copied, 1)

            def lora(c):
                nc.tensor.matmul(ps_w[:, c % 2, :], downT[:, c], up3[:], start=True, stop=True).then_inc(lora_done, 1)

            for c in range(2):
                lora(c)

            def multiply(b, i, q):
                T = b * QT + q
                pe.wait_ge(o_split, T + 1)
                pe.wait_ge(x2_done, T - 1)
                for n, (c, (a, m)) in enumerate((c, p) for c in range(OC) for p in ((0, 0), (1, 0), (0, 1))):
                    mm = nc.tensor.matmul(ps_o[:, q, :], (o_h, o_l)[a][:, i, q, c], (wo_h, wo_l)[m][:, c], start=(n == 0), stop=(n == 3 * OC - 1))
                mm.then_inc(projected, 1)

            def turn(b, i):
                for q in range(QT):
                    pe.wait_ge(xn_done, b * QT + (q + 1))
                    for c in range(XC):
                        mm = nc.tensor.transpose(ps_t[:, q, c * TQ:(c + 1) * TQ], xn[:, i, q, c * P:(c + 1) * P], ident[0:TQ, 0:TQ])
                    mm.then_inc(xn_turned, 1)

            def gate(b):
                for q in range(QT):
                    T = b * QT + q
                    pe.wait_ge(xn_copied, T + 1)
                    if not (isinstance(b, int) and b == 0):
                        pe.wait_ge(logits_done, T - 1)
                    for c in range(XC):
                        mm = nc.tensor.matmul(ps_l[:, q, 0:E], xnT[:, q, c], wg[:, c], start=(c == 0), stop=(c == XC - 1))
                    mm.then_inc(gated, 1)

            def batch(b, i):
                multiply(b, i, 0)
                turn(b - 1, 1 - i)
                multiply(b, i, 1)
                gate(b - 1)

            pe.wait_ge(o_split, QT)
            for c in range(OC):
                if c + 2 < OC:
                    pe.wait_ge(eff_done, c + 1)
                    lora(c + 2)
                pe.wait_ge(low_done, c + 1)
                for q in range(QT):
                    for n, (a, m) in enumerate(((0, 0), (1, 0), (0, 1))):
                        mm = nc.tensor.matmul(ps_o[:, q, :], (o_h, o_l)[a][:, 0, q, c], (wo_h, wo_l)[m][:, c],
                                              start=(c == 0 and n == 0), stop=(c == OC - 1 and n == 2))
                    if c == OC - 1:
                        mm.then_inc(projected, 1)
            pe.wait_ge(late_loaded, 2 * 16)
            batch(1, 1)
            with pe.Fori(1, B // 2) as two:
                batch(two * 2, 0)
                batch(two * 2 + 1, 1)
            turn(B - 1, 1)
            gate(B - 1)


def route(nc, dram, const):
    logits, pos, weight, table, stage, xn_all, w1, w2 = (
        const[k] for k in ("logits", "pos", "weight", "table", "stage", "xn_all", "w1_0", "w2_0"))
    with ExitStack() as ctx:
        def sb(name, shape, dt=F32):
            return ctx.enter_context(nc.sbuf_tensor(name, shape, dt))

        def sem(name):
            return ctx.enter_context(nc.semaphore(name))

        ones = sb("ones_r", [TQ, TQ])
        tri = sb("tri", [TQ, TQ])
        iota = sb("iota_e", [TQ, E])
        thr = sb("thresholds", [TQ, KMAX])
        top = sb("top", [TQ, NT, 8])
        idx = sb("idx", [TQ, NT, 8], U32)
        idxf = sb("idxf", [TQ, NT, 2])
        hot = sb("hot", [TQ, 2, NT, E])
        both = sb("both", [TQ, NT, E])
        shifted = sb("shifted", [TQ, NT, E])
        expo = sb("expo", [TQ, NT, E])
        second = sb("second", [TQ, NT])
        second_e = sb("second_e", [TQ, NT])
        total = sb("total", [TQ, E])
        over = sb("over", [TQ, E, KMAX])
        nsteps = sb("nsteps", [TQ, E])
        before = sb("before", [TQ, 2, E])
        start = sb("start", [TQ, 2, NT, E])
        slot = sb("slot", [TQ, NT, E])
        picked = sb("picked", [TQ, 2, NT, E])
        posf = sb("posf", [TQ, 2, NT])
        ps_r = ctx.enter_context(nc.psum_tensor("ps_rank", [TQ, 2, 512], F32))

        const_set = sem("const_set")
        tri_set = sem("tri_set")
        routed = sem("routed")
        shifted_ready = sem("shifted_ready")
        expo_ready = sem("expo_ready")
        both_ready = sem("both_ready")
        ranked = sem("ranked")
        pos_ready = sem("pos_ready")
        scattered = [sem(f"scattered{i}") for i in range(4)]
        w0_high = sem("w0_high")
        w0_split = sem("w0_split")
        block = ctx.enter_context(nc.Block())

        @block.sync
        def _(sp):
            for i in range(4):
                sp.wait_ge(scattered[i], 32 * (NT // 4))

        @block.gpsimd
        def _(pool):
            nc.gpsimd.memset(ones[:], 1.0).then_inc(const_set, 1)
            pool.wait_ge(const_set, 1)
            nc.gpsimd.affine_select(out=tri[:], in_=ones[:], compare_op=ALU.is_gt, fill=0.0, base=0,
                                    pattern=[[1, TQ]], channel_multiplier=-1).then_inc(tri_set, 1)
            pool.wait_ge(pos_ready, 1)
            for n in range(NT):
                if n >= 4:
                    pool.wait_ge(scattered[n % 4], 32 * (n // 4))
                for j in range(2):
                    nc.gpsimd.indirect_dma_start(out=dram["slots"], out_offset=bass.IndirectOffsetOnAxis(ap=pos[:, j, n:n + 1], axis=0),
                                                 in_=xn_all[:, n], in_offset=None).then_inc(scattered[n % 4], 16)

        @block.scalar
        def _(act):
            act.wait_ge(shifted_ready, 1)
            nc.scalar.activation(expo[:], shifted[:], ACT.Exp)
            nc.scalar.activation(second_e[:], second[:], ACT.Exp).then_inc(expo_ready, 1)
            for c in range(PIECES):
                nc.scalar.copy(weight_piece(w1, w2, 0, c), stage[:, c]).then_inc(w0_high, 1)

        @block.vector
        def _(dve):
            done = [0]

            def step(ins):
                done[0] += 1
                ins.then_inc(routed, 1)
                dve.wait_ge(routed, done[0])

            def over_e(ap):
                return ap.rearrange("p (n o) -> p n o", o=1).to_broadcast((TQ, NT, E))

            def running_sums(two, n):
                at, d = 0, 1
                while d < n:
                    nc.vector.tensor_copy(two[:, 1 - at, 0:d], two[:, at, 0:d])
                    step(nc.vector.tensor_tensor(two[:, 1 - at, d:n], two[:, at, d:n], two[:, at, 0:n - d], ALU.add))
                    at, d = 1 - at, 2 * d
                return two[:, at]

            for e in range(E):
                last = nc.vector.memset(iota[:, e:e + 1], float(e))
            for k in range(KMAX):
                last = nc.vector.memset(thr[:, k:k + 1], float(STEP * k))
            step(last)
            for n in range(NT):
                last = nc.vector.max(top[:, n], logits[:, n])
            step(last)
            for n in range(NT):
                last = nc.vector.max_index(idx[:, n], top[:, n], logits[:, n])
            step(last)
            step(nc.vector.tensor_tensor(second[:], top[:, :, 1], top[:, :, 0], ALU.subtract))
            nc.vector.tensor_tensor(shifted[:], logits[:], over_e(top[:, :, 0]), ALU.subtract).then_inc(shifted_ready, 1)
            step(nc.vector.tensor_copy(idxf[:], idx[:, :, 0:2]))
            for j in range(2):
                last = nc.vector.tensor_tensor(hot[:, j], iota[:].rearrange("p (o e) -> p o e", o=1).to_broadcast((TQ, NT, E)),
                                               over_e(idxf[:, :, j]), ALU.is_equal)
            step(last)
            nc.vector.tensor_tensor(both[:], hot[:, 0], hot[:, 1], ALU.add).then_inc(both_ready, 1)
            dve.wait_ge(expo_ready, 1)
            step(nc.vector.tensor_reduce(weight[:, 1], expo[:], AX.X, ALU.add))
            step(nc.vector.reciprocal(weight[:, 0], weight[:, 1]))
            step(nc.vector.tensor_tensor(weight[:, 1], weight[:, 0], second_e[:], ALU.mult))
            dve.wait_ge(ranked, 1)
            counts = ps_r[:, 1, 0:NT * E].rearrange("p (n e) -> p n e", e=E)
            nc.vector.tensor_copy(start[:, 0, 1:NT], counts[:, 0:NT - 1])
            step(nc.vector.tensor_reduce(total[:], counts.rearrange("p n e -> p e n"), AX.X, ALU.add))
            step(nc.vector.tensor_tensor(over[:], total[:].rearrange("p (e o) -> p e o", o=1).to_broadcast((TQ, E, KMAX)),
                                         thr[:].rearrange("p (o k) -> p o k", o=1).to_broadcast((TQ, E, KMAX)), ALU.is_gt))
            step(nc.vector.tensor_reduce(nsteps[:], over[:], AX.X, ALU.add))
            step(nc.vector.tensor_scalar(nsteps[:], nsteps[:], float(MINSTEPS), None, ALU.max))
            nc.vector.tensor_copy(before[:, 0, :], nsteps[:])
            nc.vector.tensor_copy(table[0:1, 0:E], nsteps[0:1, :])
            step(nc.vector.memset(start[:, 0, 0], 0.0))
            upto = running_sums(before, E)
            nc.vector.memset(table[0:1, E:E + 1], 0)
            nc.vector.tensor_copy(table[0:1, E + 1:2 * E + 1], upto[0:1, :])
            step(nc.vector.tensor_scalar(start[:, 0, 0, 1:E], upto[:, 0:E - 1], float(STEP), None, ALU.mult))
            begins = running_sums(start, NT)
            step(nc.vector.tensor_tensor(slot[:], ps_r[:, 0, 0:NT * E].rearrange("p (n e) -> p n e", e=E), begins, ALU.add))
            for j in range(2):
                last = nc.vector.tensor_tensor(picked[:, j], hot[:, j], slot[:], ALU.mult)
            step(last)
            step(nc.vector.tensor_reduce(posf[:].rearrange("p j n -> p (j n)"), picked[:].rearrange("p j n e -> p (j n) e"), AX.X, ALU.add))
            nc.vector.tensor_copy(pos[:], posf[:]).then_inc(pos_ready, 1)
            for c in range(PIECES):
                dve.wait_ge(w0_high, c + 1)
                nc.vector.tensor_tensor(weight_piece(w1, w2, 1, c), stage[:, c], weight_piece(w1, w2, 0, c).bitcast(F32), ALU.subtract).then_inc(w0_split, 1)

        @block.tensor
        def _(pe):
            pe.wait_ge(tri_set, 1)
            pe.wait_ge(both_ready, 1)
            flat = both[:].rearrange("p n e -> p (n e)")
            nc.tensor.matmul(ps_r[:, 0, 0:NT * E], tri[:], flat, start=True, stop=True)
            nc.tensor.matmul(ps_r[:, 1, 0:NT * E], ones[:], flat, start=True, stop=True).then_inc(ranked, 1)


def experts(nc, dram, const):
    ident, table, stage = (const[k] for k in ("ident", "table", "stage"))
    with ExitStack() as ctx:
        def sb(name, shape, dt=F32):
            return ctx.enter_context(nc.sbuf_tensor(name, shape, dt))

        def psum(name, shape):
            return ctx.enter_context(nc.psum_tensor(name, shape, F32))

        def sem(name):
            return ctx.enter_context(nc.semaphore(name))

        W1 = [const["w1_0"], sb("w1_1", [P, 2, XC, 2 * F], F32R)]
        W2 = [const["w2_0"], sb("w2_1", [P, 2, FC, D], F32R)]
        xg = sb("x_slots", [P, D])
        xT = sb("x_slotsT", [P, 2, XC, STEP], F32R)
        act_sb = sb("act", [P, F])
        hT = sb("hT", [P, 2, FC, STEP], F32R)
        y = sb("y", [P, D])
        ps_h = psum("ps_h", [P, 3, 512])
        ps_x = psum("ps_x", [P, 512])
        ps_a = psum("ps_a", [P, 2, 512])
        ps_y = psum("ps_y", [P, 512])

        w1_loaded = sem("w1_loaded")
        w_loaded = [sem(f"{k}_loaded") for k in ("c_fc", "c_proj")]
        w_high = sem("w_high")
        w_ready = sem("w_ready")
        passed = sem("passed")
        ended = sem("ended")
        x_loaded = sem("slots_loaded")
        x_turned = sem("slots_turned")
        x_high = sem("slots_high")
        x_split = sem("slots_split")
        hidden = sem("hidden")
        silu_done = sem("silu_done")
        glu_done = sem("glu_done")
        h_turned = sem("h_turned")
        h_high = sem("h_high")
        h_split = sem("h_split")
        y_ready = sem("y_ready")
        y_done = sem("y_done")
        y_stored = sem("y_stored")
        block = ctx.enter_context(nc.Block())

        def steps(engine, e, buf, body):
            n = engine.value_load(table[0:1, bass.ds(e, 1)], min_val=MINSTEPS, max_val=KMAX)
            begin = engine.value_load(table[0:1, bass.ds(e + E, 1)], min_val=MINSTEPS, max_val=MAXSTEPS - MINSTEPS)
            body(buf, 1 - buf, begin, e)
            with engine.Fori(1, n) as j:
                body(buf, buf, begin + j, None)

        def each_step(engine, body):
            body(0, None, 0, 0)
            n = engine.value_load(table[0:1, 0:1], min_val=MINSTEPS, max_val=KMAX)
            with engine.Fori(1, n) as j:
                body(0, 0, j, None)
            with engine.Fori(0, E // 2 - 1) as pair:
                for i in range(2):
                    steps(engine, pair * 2 + (1 + i), 1 - i, body)
            steps(engine, E - 1, 1, body)

        def all_steps(engine):
            return engine.value_load(table[0:1, 2 * E:2 * E + 1], min_val=MINSTEPS * E, max_val=MAXSTEPS)

        @block.sync
        def _(sp):
            slots = dram["slots"].rearrange("(g p) d -> g p d", p=P)

            def load(g):
                sp.dma_start(xg[:], slots[bass.ds(g, 1)].rearrange("o p d -> (o p) d")).then_inc(x_loaded, 16)

            def store(g):
                sp.dma_start(slots[bass.ds(g, 1)].rearrange("o p d -> (o p) d"), y[:]).then_inc(y_stored, 16)

            sp.sem_inc(y_stored, 16)
            load(0)
            for dst, src in expert_weights(dram, stage, 1):
                sp.dma_start(dst, src).then_inc(w1_loaded, 16)
            sp.wait_ge(x_turned, 1)
            load(1)

            def body(buf, before, g, e):
                sp.wait_ge(x_turned, g + 2)
                load(g + 2)
                if before is not None:
                    sp.wait_ge(y_done, g + 1)
                    store(g - 1)

            each_step(sp, body)
            G = all_steps(sp)
            sp.wait_ge(y_done, G + 1)
            store(G - 1)
            sp.wait_ge(x_loaded, G * 16 + 32)
            sp.sem_inc(ended, 1)
            sp.wait_ge(y_stored, G * 16 + 16)
            sp.sem_inc(ended, 1)

        @block.gpsimd
        def _(pool):
            def experts_weights(e, buf, more=True):
                for i, (c0, c1) in enumerate(((0, FC_PIECES), (FC_PIECES, PIECES))):
                    if not (isinstance(e, int) and e == 1):
                        pool.wait_ge(w_loaded[i], e * 16 - 16)
                        pool.sem_inc(passed, 1)
                    for c in range(c0, c1):
                        high, low = (weight_piece(W1[buf], W2[buf], part, c) for part in range(2))
                        nc.gpsimd.tensor_scalar(high, stage[:, c], 1.0, 1.0, ALU.mult, ALU.mult).then_inc(w_high, 1)
                        pool.wait_ge(w_high, (e - 1) * PIECES + (c + 1))
                        nc.gpsimd.tensor_tensor(low, stage[:, c], high.bitcast(F32), ALU.subtract).then_inc(w_ready, 1)
                    if more:
                        pool.wait_ge(w_ready, (e - 1) * PIECES + c1)
                        pool.sem_inc(passed, 1)
                        pool.dma_start(*expert_weights(dram, stage, e + 1)[i]).then_inc(w_loaded[i], 16)

            def buffer_free(e):
                over_by = pool.value_load(table[0:1, bass.ds(e + (E - 1), 1)], min_val=MINSTEPS, max_val=MAXSTEPS - MINSTEPS)
                pool.wait_ge(y_ready, over_by)
                pool.sem_inc(passed, 1)

            pool.wait_ge(w1_loaded, 2 * 16)
            experts_weights(1, 1)
            with pool.Fori(1, E // 2 - 1) as pair:
                for buf in range(2):
                    e = pair * 2 + buf
                    buffer_free(e)
                    experts_weights(e, buf)
            for e in (E - 2, E - 1):
                buffer_free(e)
                experts_weights(e, e % 2, more=(e < E - 1))

        @block.scalar
        def _(act):
            def x_part(g):
                act.wait_ge(x_turned, g + 1)
                nc.scalar.copy(xT[:, 0], ps_x[:].rearrange("p (c t) -> p c t", t=STEP)).then_inc(x_high, 1)

            def out(g):
                act.wait_ge(y_ready, g + 1)
                act.wait_ge(y_stored, g * 16 + 16)
                nc.scalar.copy(y[:], ps_y[:]).then_inc(y_done, 1)

            act.sem_inc(y_done, 1)
            x_part(0)

            def body(buf, before, g, e):
                act.wait_ge(hidden, g + 1)
                nc.scalar.activation(act_sb[:], ps_h[:].rearrange("p j n -> p (j n)")[:, 0:F], ACT.Silu).then_inc(silu_done, 1)
                x_part(g + 1)
                for j in range(2):
                    act.wait_ge(h_turned, g * 2 + (j + 1))
                    nc.scalar.copy(hT[:, 0, 3 * j:3 * j + 3], ps_a[:, j, 0:3 * STEP].rearrange("p (c t) -> p c t", t=STEP)).then_inc(h_high, 1)
                if before is not None:
                    out(g - 1)

            each_step(act, body)
            G = all_steps(act)
            out(G - 1)

        @block.vector
        def _(dve):
            def x_part(g):
                dve.wait_ge(x_high, g + 1)
                nc.vector.tensor_tensor(xT[:, 1], ps_x[:].rearrange("p (c t) -> p c t", t=STEP), xT[:, 0].bitcast(F32), ALU.subtract).then_inc(x_split, 1)

            x_part(0)

            def body(buf, before, g, e):
                dve.wait_ge(silu_done, g + 1)
                nc.vector.tensor_tensor(act_sb[:], ps_h[:].rearrange("p j n -> p (j n)")[:, F:2 * F], act_sb[:], ALU.mult).then_inc(glu_done, 1)
                x_part(g + 1)
                for j in range(2):
                    dve.wait_ge(h_high, g * 2 + (j + 1))
                    nc.vector.tensor_tensor(hT[:, 1, 3 * j:3 * j + 3], ps_a[:, j, 0:3 * STEP].rearrange("p (c t) -> p c t", t=STEP),
                                            hT[:, 0, 3 * j:3 * j + 3].bitcast(F32), ALU.subtract).then_inc(h_split, 1)

            each_step(dve, body)

        @block.tensor
        def _(pe):
            passes = ((0, 0), (1, 0), (0, 1))
            def turn(dst, src):
                for c in range(src.shape[-1] // STEP):
                    mm = nc.tensor.transpose(dst[:, c * STEP:(c + 1) * STEP], src[:, c * STEP:(c + 1) * STEP], ident[:])
                return mm

            def turn_x(g):
                pe.wait_ge(x_loaded, g * 16 + 16)
                turn(ps_x, xg[:]).then_inc(x_turned, 1)

            def result(g, buf):
                pe.wait_ge(h_split, g * 2 + 2)
                pe.wait_ge(y_done, g + 1)
                for n, (c, (a, m)) in enumerate((c, p) for c in range(FC) for p in passes):
                    mm = nc.tensor.matmul(ps_y[:], hT[:, a, c], W2[buf][:, m, c], start=(n == 0), stop=(n == 3 * FC - 1))
                mm.then_inc(y_ready, 1)

            turn_x(0)

            def body(buf, before, g, e):
                if before is not None and e is not None:
                    pe.wait_ge(w_ready, e * PIECES)
                pe.wait_ge(x_split, g + 1)
                for j in range(3):
                    for n, (c, (a, m)) in enumerate((c, p) for c in range(XC) for p in passes):
                        mm = nc.tensor.matmul(ps_h[:, j], xT[:, a, c], W1[buf][:, m, c, j * 512:(j + 1) * 512], start=(n == 0), stop=(n == 3 * XC - 1))
                mm.then_inc(hidden, 1)
                turn_x(g + 1)
                if before is not None:
                    result(g - 1, before)
                pe.wait_ge(glu_done, g + 1)
                for j in range(2):
                    turn(ps_a[:, j], act_sb[:, j * F // 2:(j + 1) * F // 2]).then_inc(h_turned, 1)

            each_step(pe, body)
            result(all_steps(pe) - 1, 1)


def combine(nc, dram, const):
    pos, weight = const["pos"], const["weight"]
    RING = 8
    with ExitStack() as ctx:
        def sb(name, shape, dt=F32):
            return ctx.enter_context(nc.sbuf_tensor(name, shape, dt))

        def sem(name):
            return ctx.enter_context(nc.semaphore(name))

        x2 = sb("x2_in", [TQ, NT, D])
        got = sb("got", [TQ, RING, 2, D])
        part = sb("part", [TQ, RING, D])
        x2_loaded = [sem(f"x2_loaded{i}") for i in range(4)]
        gathered = [sem(f"gathered{i}") for i in range(RING)]
        first_added = sem("first_added")
        added = sem("added")
        stored = sem("stored")
        block = ctx.enter_context(nc.Block())

        @block.sync
        def _(sp):
            for i in range(4):
                at = slice(i * B // 4, (i + 1) * B // 4)
                sp.dma_start(x2[:].rearrange("p (b t) d -> p b t d", t=QT)[:, at], dram["x2"].rearrange("b p t d -> p b t d")[:, at]).then_inc(x2_loaded[i], 16)
            for n in range(NT):
                sp.wait_ge(added, n + 1)
                sp.dma_start(dram["out_pq"][n // QT, :, n % QT], x2[:, n]).then_inc(stored, 16)
            sp.wait_ge(stored, 16 * NT)

        @block.gpsimd
        def _(pool):
            for n in range(NT):
                if n >= RING:
                    pool.wait_ge(added, n - RING + 1)
                for j in range(2):
                    nc.gpsimd.indirect_dma_start(out=got[:, n % RING, j], out_offset=None, in_=dram["slots"],
                                                 in_offset=bass.IndirectOffsetOnAxis(ap=pos[:, j, n:n + 1], axis=0)).then_inc(gathered[n % RING], 16)

        @block.vector
        def _(dve):
            for n in range(NT):
                if n % 4 == 0:
                    dve.wait_ge(x2_loaded[n // 4], 16)
                dve.wait_ge(gathered[n % RING], 32 * (n // RING + 1))
                nc.vector.scalar_tensor_tensor(out=part[:, n % RING], in0=got[:, n % RING, 0], scalar=weight[:, 0, n:n + 1], in1=x2[:, n],
                                               op0=ALU.mult, op1=ALU.add).then_inc(first_added, 1)
                dve.wait_ge(first_added, n + 1)
                nc.vector.scalar_tensor_tensor(out=x2[:, n], in0=got[:, n % RING, 1], scalar=weight[:, 1, n:n + 1], in1=part[:, n % RING],
                                               op0=ALU.mult, op1=ALU.add).then_inc(added, 1)


def block_kernel(nc, x, ctx_768, Wq, Wk, Wv, Wo, bo, q_down, q_up, q_alpha, k_down, k_up, k_alpha, v_down, v_up,
                 v_alpha, o_down, o_up, o_alpha, Wk_ipa, Wv_ipa, w_gate, c_fc, c_proj, out):
    dram = dict(x=x, ctx=ctx_768, Wq=Wq, Wk=Wk, Wv=Wv, Wo=Wo, bo=bo, q_down=q_down, q_up=q_up, q_alpha=q_alpha,
                k_down=k_down, k_up=k_up, k_alpha=k_alpha, v_down=v_down, v_up=v_up, v_alpha=v_alpha,
                o_down=o_down, o_up=o_up, o_alpha=o_alpha, Wk_ipa=Wk_ipa, Wv_ipa=Wv_ipa,
                w_gate=w_gate, c_fc=c_fc, c_proj=c_proj,
                x_pq=x.rearrange("b (t p) d -> b p t d", p=TQ), out_pq=out.rearrange("b (t p) d -> b p t d", p=TQ))
    for name, shape in (("vipa", [B * IPA, HEADS * 2 * DH]), ("oT", [ID, B, N]), ("x2", [B, TQ, QT, D]),
                        ("slots", [ROOM * STEP, D])):
        dram[name] = nc.dram_tensor(f"{name}_scratch", shape, F32).ap()
    with ExitStack() as ctx:
        const = {}

        def sb(stack, name, shape, dt=F32):
            const[name] = stack.enter_context(nc.sbuf_tensor(name, shape, dt))

        sb(ctx, "ident", [P, P])
        sb(ctx, "logits", [TQ, NT, E])
        sb(ctx, "pos", [TQ, 2, NT], U32)
        sb(ctx, "weight", [TQ, 2, NT])
        with ExitStack() as inner:
            sb(inner, "kipa", [P, PAIRS, 2, B * IPA], F32R)
            sb(inner, "rstd", [TQ, NT])
            sb(inner, "mean", [TQ, NT])
            for k, n in (("q", XC), ("k", CC), ("v", CC)):
                for part in "hl":
                    sb(inner, f"w{k}_{part}", [P, n, ID], F32R)
            prepare(nc, dram, const)
            attend(nc, dram, const)
        sb(ctx, "table", [1, 2 * E + 1], I32)
        with ExitStack() as inner:
            sb(inner, "stage", [P, PIECES, PIECE])
            with ExitStack() as rows:
                const["xn_all"] = rows.enter_context(nc.sbuf_tensor("xn_all", [TQ, NT, D], F32, side="right"))
                project(nc, dram, const)
                sb(inner, "w1_0", [P, 2, XC, 2 * F], F32R)
                sb(inner, "w2_0", [P, 2, FC, D], F32R)
                route(nc, dram, const)
            experts(nc, dram, const)
        combine(nc, dram, const)


_INS = ["x", "ctx_768"] + [f"L0_xattn_{n}" for n in (
    "Wq", "Wk", "Wv", "Wo", "bo", "q_down", "q_up", "q_alpha", "k_down", "k_up", "k_alpha", "v_down", "v_up", "v_alpha",
    "o_down", "o_up", "o_alpha", "Wk_ipa", "Wv_ipa")] + [f"L0_ffn_{n}" for n in ("w_gate", "c_fc", "c_proj")]


def kernel(**inputs):
    import concourse.bacc as bacc
    from concourse.bass_utils import run_bass_kernel_spmd

    nc = bacc.Bacc("TRN2", target_bir_lowering=False, num_devices=1)
    arrays, args = {}, []
    for name in _INS:
        a = np.ascontiguousarray(inputs[name])
        arrays[f"in_{name}"] = a
        args.append(nc.dram_tensor(f"in_{name}", a.shape, mybir.dt.from_np(a.dtype), kind="ExternalInput").ap())
    args.append(nc.dram_tensor("out_0", (B, N, D), F32, kind="ExternalOutput").ap())
    block_kernel(nc, *args)
    r = run_bass_kernel_spmd(nc, [arrays], core_ids=[0])
    return r.results[0]["out_0"]
```
